# Optimizing a Trainium2 kernel written in Bass

```python
import numpy as np
import jax
import jax.numpy as jnp

def _softmax(x, axis=-1):
    return jax.nn.softmax(x, axis=axis)

def _gelu(x):
    return jax.nn.gelu(x, approximate=True)

def _silu(x):
    return jax.nn.silu(x)

def _sigmoid(x):
    return jax.nn.sigmoid(x)

def _layernorm(x, axis=-1, eps=1e-05):
    m = jnp.mean(x, axis=axis, keepdims=True)
    v = jnp.var(x, axis=axis, keepdims=True)
    return (x - m) / jnp.sqrt(v + eps)

def _scatter_add(tgt, idx, src, axis=0):
    return tgt.at[idx].add(src)

def _segment_sum(src, seg, n):
    return jax.ops.segment_sum(src, seg, n)
kernel_name = 'mk_adj_preln_d4_adj_r2_d4a346'

def setup_inputs(seed: int=0):
    np.random.seed(seed)
    _w = jnp.asarray

    def _rec_inputs():
        import jax
        import jax.numpy as jnp
        _gk = jax.random.key(seed)
        x = -0.000929 + 1 * jax.random.normal(jax.random.fold_in(_gk, 1), (4096, 128), jnp.float32)
        _a = jax.random.bernoulli(jax.random.fold_in(_gk, 2), 0.00390625, (4096, 4096))
        _a = jnp.logical_or(_a, jnp.eye(4096, dtype=bool))
        _af = _a.astype(jnp.float32)
        adj = _af
        return (x, adj)
    x, adj = _rec_inputs()

    def _L0_gnn_setup():
        import jax, jax.numpy as jnp
        import numpy as np
        N = 4096
        F_IN = 128
        F_OUT = 128
        BLOCK = 64

        def _graph_pool(out, adj):
            neg = jnp.asarray(jnp.finfo(out.dtype).min, out.dtype)

            def body(_, adj_blk):
                masked = jnp.where(adj_blk[:, :, None] != 0, out[None, :, :], neg)
                return (None, jnp.max(masked, axis=1))
            _, blocks = jax.lax.scan(body, None, adj.reshape(N // BLOCK, BLOCK, N))
            return blocks.reshape(N, out.shape[-1])
        key = jax.random.key(seed)
        k_in, k_adj, k_w, k_b = jax.random.split(key, 4)
        x = jax.random.normal(k_in, (N, F_IN), dtype=jnp.float32)
        adj = (jax.random.uniform(k_adj, (N, N)) < 0.01).astype(jnp.float32)
        adj = adj.at[jnp.arange(N), jnp.arange(N)].set(1.0)
        stdv = 1.0 / np.sqrt(F_OUT)
        weight = jax.random.uniform(k_w, (F_IN, F_OUT), minval=-stdv, maxval=stdv, dtype=jnp.float32)
        bias = jax.random.uniform(k_b, (F_OUT,), minval=-stdv, maxval=stdv, dtype=jnp.float32)
        return {'input': x, 'adj': adj, 'weight': weight, 'bias': bias}
    _L0_gnn_all = _L0_gnn_setup()
    _L0_gnn_in = {k: v for k, v in _L0_gnn_all.items() if k in ('weight', 'bias')}
    del _L0_gnn_all

    def _L1_gnn_setup():
        import jax, jax.numpy as jnp
        import numpy as np
        N = 8192
        F_IN = 128
        F_OUT = 128
        key = jax.random.key(seed)
        k1, k2, k3 = jax.random.split(key, 3)
        x = jax.random.normal(k1, (N, F_IN), dtype=jnp.float32)
        adj = jax.random.uniform(k2, (N, N), dtype=jnp.float32)
        stdv = 1.0 / np.sqrt(F_OUT)
        w = jax.random.uniform(k3, (2 * F_IN, F_OUT), dtype=jnp.float32, minval=-stdv, maxval=stdv)
        return {'input': x, 'adj': adj, 'weight': w}
    _L1_gnn_all = _L1_gnn_setup()
    _L1_gnn_in = {k: v for k, v in _L1_gnn_all.items() if k in ('weight',)}
    del _L1_gnn_all

    def _L2_gnn_setup():
        import jax, jax.numpy as jnp
        import numpy as np
        EPS = 1e-05
        MIN_NORM = 1e-15

        def _norm(x):
            return jnp.maximum(jnp.linalg.norm(x, axis=-1, keepdims=True), MIN_NORM)

        def _artanh(x):
            return jnp.arctanh(jnp.clip(x, -1.0 + EPS, 1.0 - EPS))

        def expmap0(u):
            un = _norm(u)
            return jnp.tanh(un) * u / un

        def logmap0(y):
            yn = _norm(y)
            return _artanh(yn) * y / yn

        def mobius_matvec(W, x):
            mx = x @ W
            xn = _norm(x)
            mxn = _norm(mx)
            res = jnp.tanh(mxn / xn * _artanh(xn)) * mx / mxn
            zero = jnp.all(mx == 0.0, axis=-1, keepdims=True)
            return jnp.where(zero, 0.0, res)

        def mobius_scalar_mul(r, x):
            xn = _norm(x)
            return jnp.tanh(r * _artanh(xn)) * x / xn

        def _clamp_abs(x, eps=1e-10):
            return jnp.where(x >= 0.0, jnp.maximum(x, eps), jnp.minimum(x, -eps))
        key = jax.random.key(seed)
        k1, k2, k3 = jax.random.split(key, 3)
        N, D_IN, D_OUT = (4096, 128, 128)
        AVG_DEG = 64.0
        v = 0.1 * jax.random.normal(k1, (N, D_IN), dtype=jnp.float32)
        X = expmap0(v)
        mask = (jax.random.uniform(k2, (N, N)) < AVG_DEG / N).astype(jnp.float32)
        mask = mask + jnp.eye(N, dtype=jnp.float32)
        A_hat = mask / mask.sum(-1, keepdims=True)
        W = jax.random.uniform(k3, (D_IN, D_OUT), dtype=jnp.float32)
        return {'X': X, 'A_hat': A_hat, 'W': W}
    _L2_gnn_all = _L2_gnn_setup()
    _L2_gnn_in = {k: v for k, v in _L2_gnn_all.items() if k in ('W',)}
    del _L2_gnn_all

    def _L3_gnn_setup():
        import jax, jax.numpy as jnp
        import numpy as np

        def _lap_mul(A, x):
            d = 1.0 / jnp.sqrt(jnp.sum(A, axis=-1))
            return d[:, None] * (A @ (d[:, None] * x))
        key = jax.random.key(seed)
        k1, k2, k3, k4, k5, k6 = jax.random.split(key, 6)
        N, D_IN, D_OUT = (2048, 128, 128)
        x = jax.random.normal(k1, (N, D_IN), dtype=jnp.float32)
        A = jax.random.uniform(k2, (N, N), dtype=jnp.float32)
        s1 = 1.0 / np.sqrt(D_IN)
        W1 = jax.random.uniform(k3, (D_IN, D_OUT), minval=-s1, maxval=s1, dtype=jnp.float32)
        b1 = jax.random.uniform(k4, (D_OUT,), minval=-s1, maxval=s1, dtype=jnp.float32)
        W2 = jax.random.uniform(k5, (D_IN, D_OUT), minval=-s1, maxval=s1, dtype=jnp.float32)
        b2 = jax.random.uniform(k6, (D_OUT,), minval=-s1, maxval=s1, dtype=jnp.float32)
        return {'x': x, 'A': A, 'W1': W1, 'b1': b1, 'W2': W2, 'b2': b2, 'sigma': 1, 'k': 4}
    _L3_gnn_all = _L3_gnn_setup()
    _L3_gnn_in = {k: v for k, v in _L3_gnn_all.items() if k in ('W1', 'b1', 'W2', 'b2')}
    del _L3_gnn_all
    return {'x': x, 'adj': adj, 'L0_gnn_weight': _L0_gnn_in['weight'], 'L0_gnn_bias': _L0_gnn_in['bias'], 'L1_gnn_weight': _L1_gnn_in['weight'], 'L2_gnn_W': _L2_gnn_in['W'], 'L3_gnn_W1': _L3_gnn_in['W1'], 'L3_gnn_b1': _L3_gnn_in['b1'], 'L3_gnn_W2': _L3_gnn_in['W2'], 'L3_gnn_b2': _L3_gnn_in['b2']}

def reference(x, adj, L0_gnn_weight, L0_gnn_bias, L1_gnn_weight, L2_gnn_W, L3_gnn_W1, L3_gnn_b1, L3_gnn_W2, L3_gnn_b2):
    import jax
    import jax.numpy as jnp

    def _L0_gnn_ref(input, adj, weight, bias):
        import jax, jax.numpy as jnp
        import numpy as np
        N = 4096
        F_IN = 128
        F_OUT = 128
        BLOCK = 64

        def _graph_pool(out, adj):
            neg = jnp.asarray(jnp.finfo(out.dtype).min, out.dtype)

            def body(_, adj_blk):
                masked = jnp.where(adj_blk[:, :, None] != 0, out[None, :, :], neg)
                return (None, jnp.max(masked, axis=1))
            _, blocks = jax.lax.scan(body, None, adj.reshape(N // BLOCK, BLOCK, N))
            return blocks.reshape(N, out.shape[-1])
        h = input @ weight
        out = jnp.maximum(adj @ h + bias, 0.0)
        return _graph_pool(out, adj)

    def _L1_gnn_ref(input, adj, weight):
        import jax, jax.numpy as jnp
        import numpy as np
        N = 8192
        F_IN = 128
        F_OUT = 128
        support = adj @ input
        h = jnp.concatenate([input, support], axis=1)
        return h @ weight

    def _L2_gnn_ref(X, A_hat, W):
        import jax, jax.numpy as jnp
        import numpy as np
        EPS = 1e-05
        MIN_NORM = 1e-15

        def _norm(x):
            return jnp.maximum(jnp.linalg.norm(x, axis=-1, keepdims=True), MIN_NORM)

        def _artanh(x):
            return jnp.arctanh(jnp.clip(x, -1.0 + EPS, 1.0 - EPS))

        def expmap0(u):
            un = _norm(u)
            return jnp.tanh(un) * u / un

        def logmap0(y):
            yn = _norm(y)
            return _artanh(yn) * y / yn

        def mobius_matvec(W, x):
            mx = x @ W
            xn = _norm(x)
            mxn = _norm(mx)
            res = jnp.tanh(mxn / xn * _artanh(xn)) * mx / mxn
            zero = jnp.all(mx == 0.0, axis=-1, keepdims=True)
            return jnp.where(zero, 0.0, res)

        def mobius_scalar_mul(r, x):
            xn = _norm(x)
            return jnp.tanh(r * _artanh(xn)) * x / xn

        def _clamp_abs(x, eps=1e-10):
            return jnp.where(x >= 0.0, jnp.maximum(x, eps), jnp.minimum(x, -eps))
        XW = mobius_matvec(W, X)
        sq = jnp.sum(XW * XW, axis=-1, keepdims=True)
        gamma = 2.0 / jnp.maximum(1.0 - sq, EPS)
        nominator = A_hat @ (gamma * XW)
        denominator = _clamp_abs(A_hat @ (gamma - 1.0))
        two_mean = nominator / denominator
        m = mobius_scalar_mul(0.5, two_mean)
        r = A_hat.sum(-1, keepdims=True)
        AXW = mobius_scalar_mul(r, m)
        return expmap0(jax.nn.relu(logmap0(AXW)))

    def _L3_gnn_ref(x, A, W1, b1, W2, b2, sigma, k):
        import jax, jax.numpy as jnp
        import numpy as np

        def _lap_mul(A, x):
            d = 1.0 / jnp.sqrt(jnp.sum(A, axis=-1))
            return d[:, None] * (A @ (d[:, None] * x))
        z = _lap_mul(A, x) @ W1 + b1
        z = jax.nn.leaky_relu(z, negative_slope=0.1)
        sq = jnp.sum(z * z, axis=-1)
        d2 = sq[:, None] + sq[None, :] - 2.0 * (z @ z.T)
        d2 = jnp.maximum(d2, 0.0)
        S = jnp.sqrt(d2 + 1e-10)
        S = jnp.exp(-S / (2.0 * sigma))
        order = jnp.argsort(-S, axis=-1)
        ranks = jnp.argsort(order, axis=-1)
        S = jnp.where(ranks < k, S, 0.0)
        A2 = S + A
        out = _lap_mul(A2, x) @ W2 + b2
        return out
    h = jnp.maximum(_layernorm(x, axis=-1), 0.0)
    x = x + _L0_gnn_ref(h, adj, L0_gnn_weight, L0_gnn_bias)
    h = jnp.maximum(_layernorm(x, axis=-1), 0.0)
    x = x + _L1_gnn_ref(h, adj, L1_gnn_weight)
    h = jnp.maximum(_layernorm(x, axis=-1), 0.0)
    x = x + _L2_gnn_ref(h, adj, L2_gnn_W)
    h = jnp.maximum(_layernorm(x, axis=-1), 0.0)
    x = x + _L3_gnn_ref(h, adj, L3_gnn_W1, L3_gnn_b1, L3_gnn_W2, L3_gnn_b2, 1, 4)
    return x

_drawn_inputs = setup_inputs


def setup_inputs(seed=0):
    import zlib

    import numpy as np

    out = dict(_drawn_inputs(seed))
    spreads = {}
    factors = {'L0_gnn_bias': 5.577,
     'L2_gnn_W': 8.0,
     'L3_gnn_W1': 8.0,
     'L3_gnn_b1': 8.0,
     'L3_gnn_b2': 8.0}
    for name, (base, spread) in spreads.items():
        noise = np.random.default_rng([zlib.crc32(name.encode()), seed]).standard_normal(out[name].shape)
        drawn = base * np.exp(spread * noise) if base else spread * noise
        out[name] = jnp.asarray(drawn.astype(out[name].dtype))
    for name, factor in factors.items():
        out[name] = (out[name] * factor).astype(out[name].dtype)
    return out
```

```python
import numpy as np
import concourse.bass as bass
from concourse import mybir
from contextlib import ExitStack

F32, BF16, F8, I32, U32 = (mybir.dt.float32, mybir.dt.bfloat16, mybir.dt.float8e4, mybir.dt.int32,
                           mybir.dt.uint32)
ALU = mybir.AluOpType
ACT = mybir.ActivationFunctionType
AX = mybir.AxisListType.X
ts, ds = bass.ts, bass.ds

P = 128
G = 4
LN_EPS = 1e-5
BALL_EPS = 1e-5
MIN_NORM = 1e-15
MIN_DENOMINATOR = 1e-10
DISTANCE_EPS = 1e-10
SLOPE = 0.1
TOP = 4
LIST = 16
FLT_MAX = float(np.finfo(np.float32).max)
BALL_CLIP = float(np.float32(1.0) - np.float32(BALL_EPS))
ARTANH_CLIP = float(0.5 * np.log((1.0 + BALL_CLIP) / (1.0 - BALL_CLIP)))


def program(nc, x, adj, w0, b0, w1, w2, w31, b31, w32, b32, out):
    N, F = x.shape
    NT = N // P
    NG = NT // G
    FE = F + 1
    FW = 3 * FE
    BPB = 512 // P

    ctx = ExitStack()
    with ctx:
        def sb(name, shape, dt):
            return ctx.enter_context(nc.sbuf_tensor(name, shape, dt))

        def sem(name):
            return ctx.enter_context(nc.semaphore(name))

        adjT_dram = nc.dram_tensor("adjT_panels", (NT, P, NT * P // 2), BF16).ap()
        feat_dram = nc.dram_tensor("pool_features", (N + 1, F), F32).ap()
        g2_dram = nc.dram_tensor("last_features", (N, F), F32).ap()

        X = sb("X", [P, NT, F], F32)
        spare = sb("partsA", [P, NT * FW], BF16)
        partsA = spare[:, :].rearrange("p (t w) -> p t w", t=NT)
        partsB = sb("partsB", [P, NT, FW], BF16)
        side = sb("side", [P, NT, F], F32)
        rows = sb("rows", [P, 2, N], F32)
        panel = sb("panel", [P, G, NT, P], F8)
        first = sb("first", [P, 2, NT, P], F8)
        wide = sb("wide", [P, NT, F], F32)
        zT = wide[:, :, :].rearrange("p t f -> p (t f)")
        gath = sb("gath", [P, 2, LIST + 8, F], F32)
        gsc = sb("gsc", [P, G, FE], F32)
        rem = sb("rem", [P, G, FE], F32)
        agg = sb("agg", [P, G, FE], F32)
        xg = sb("xg", [P, G, F], F32)
        hn = sb("hn", [P, G, F], F32)
        hT = sb("hT", [P, G * P], F32)
        tmp = sb("tmp", [P, G, F], F32)
        relu_junk = sb("relu_junk", [P, G, F], BF16)
        st = sb("st", [P, G, nc.vector.BN_STATS_DIM], F32)
        mv = sb("mv", [P, G, nc.vector.BN_AGGR_DIM], F32)
        std = sb("std", [P, G], F32)
        rstd = sb("rstd", [P, G], F32)
        W = {k: sb(k, [P, F], F32) for k in ("W0", "W1a", "W1b", "W2", "W31", "W32")}
        B = {k: sb(k, [P, F], F32) for k in ("b0", "b31", "b32")}
        ident = sb("ident", [P, P], F32)
        identb = sb("identb", [P, P], BF16)
        tri = sb("tri", [P, P], BF16)
        diag_code = sb("diag_code", [P, P], BF16)
        code_row = sb("code_row", [P, P], F32)
        block_code = sb("block_code", [P, NT, 7], BF16)
        eps_ln = sb("eps_ln", [P, 1], F32)
        eps_dist = sb("eps_dist", [P, 1], F32)
        ones_col = sb("ones_col", [P, 1], F32)
        ones3 = sb("ones3", [3, P], BF16)
        zero_row = sb("zero_row", [1, F], F32)
        cand = sb("cand", [P, NT, 8], F32)
        rest = sb("rest", [P, NT * 7], F32)
        rest2 = sb("rest2", [P, NT * 7], F32)
        listed = sb("listed", [P, G, LIST], F32)
        found = sb("found", [P, G, NT + LIST], F32)
        found_n = sb("found_n", [P, G], F32)
        IDX = sb("IDX", [P, NT, LIST], I32)
        idx_now = sb("idx_now", [P, 2, LIST], I32)
        DEG = sb("DEG", [P, NT], F32)
        FOUND = sb("FOUND", [P, NT], F32)
        missing = sb("missing", [P, NT], F32)
        missing_n = sb("missing_n", [P, 1], F32)
        flag = sb("flag", [1, 1], I32)
        NOROW = sb("NOROW", [P, NT], F32)
        DSTD = sb("DSTD", [P, NT], F32)
        DINV = sb("DINV", [P, NT], F32)
        general_mask, general_cap = hT[:, 0:64], hT[:, 64:128]
        general_new, general_acc = hn[:, 0, :], hn[:, 1, :]
        ss = sb("ss", [P, 2, G], F32)
        nn = sb("nn", [P, 2, G], F32)
        v = [sb(f"v{i}", [P, G], F32) for i in range(16)]
        SQ = sb("SQ", [P, NT], F32)
        sqg = sb("sqg", [P, G], F32)
        sqh = sb("sqh", [P, G], F32)
        sqr = sb("sqr", [P, G], F32)
        sqp = sb("sqp", [P, G, 3], BF16)
        SQT = first[0:3, :, :, :].bitcast(BF16).rearrange("p a b i -> p (a b i)")
        top_v = sb("top_v", [P, G, 8], F32)
        top_i = sb("top_i", [P, G, 8], U32)
        D2 = rest[:, 0:NT * TOP].rearrange("p (t k) -> p t k", k=TOP)
        D2c = rest2[:, 0:NT * TOP].rearrange("p (t k) -> p t k", k=TOP)
        DR = cand[:, :, 0:TOP]
        at = 4 * P + 4 * G * F
        TK, TI, S = (spare[:, at + k * 2 * NT * TOP:at + (k + 1) * 2 * NT * TOP].bitcast(dt)
                     .rearrange("p (t k) -> p t k", k=TOP) for k, dt in ((0, F32), (1, I32), (2, F32)))
        zs = spare[:, 0:4 * P].bitcast(F32).rearrange("p (r c) -> p r c", r=2)
        fin = spare[:, 4 * P:4 * P + 4 * G * F].bitcast(F32).rearrange("p (r q f) -> p r q f", r=2, q=G)
        SSUM = sb("SSUM", [P, NT], F32)
        SDEG = sb("SDEG", [P, NT], F32)
        SSTD = sb("SSTD", [P, NT], F32)
        D2INV = sb("D2INV", [P, NT], F32)
        sg = sb("sg", [P, G, TOP], F32)

        bank = [ctx.enter_context(nc.psum_tensor(f"bank{i}", [P, 512], F32)) for i in range(8)]
        psT, psW, psV = bank[6], bank[7], bank[5]
        sq_junk = bank[4][:, :].rearrange("p (q f) -> p q f", q=G)

        s_loaded = sem("inputs_loaded")
        s_const = sem("constants_ready")
        s_x = sem("x_group_ready")
        s_stats = sem("stats_ready")
        s_mv = sem("mean_var_ready")
        s_std = sem("std_ready")
        s_rstd = sem("rstd_ready")
        s_norm = sem("norm_ready")
        s_hTp = sem("hT_in_psum")
        s_hT = sem("hT_ready")
        s_hw = sem("hw_in_psum")
        s_side = sem("side_ready")
        s_gsc = sem("operand_ready")
        s_p0 = sem("part0_ready")
        s_rem = sem("remainder_ready")
        s_p1 = sem("part1_ready")
        s_parts = sem("parts_ready")
        s_rows = [sem(f"adj_rows_loaded{i}") for i in range(2)]
        s_tr = sem("blocks_transposed")
        s_panel = sem("panel_chunk_ready")
        s_stored = [sem(f"panel_stored{i}") for i in range(G)]
        s_code = sem("codes_in_psum")
        s_code_used = sem("codes_used")
        s_list = sem("list_chain")
        s_prod = sem("product_in_psum")
        s_agg = sem("product_taken")
        s_post = sem("post_chain")
        s_feat = sem("features_stored")
        s_deg = sem("degree_chain")
        s_missing = sem("missing_in_psum")
        s_flag = sem("flag_ready")
        s_gen_m = sem("general_mask_loaded")
        s_gen_f = sem("general_features_loaded")
        s_gen_used = sem("general_chunk_used")
        s_gen = sem("general_chain")
        s_load = [sem(f"panel_loaded{i}") for i in range(G)]
        s_tri = sem("first_codes_in_psum")
        s_first = sem("first_chunk_ready")
        s_fp = sem("first_features_in_psum")
        s_fp_used = sem("first_features_taken")
        s_idx = sem("indices_staged")
        s_gath = [sem(f"rows_gathered{i}") for i in range(2)]
        s_gath_used = sem("gathered_used")
        s_y = sem("pooled_ready")
        s_hyp = sem("ball_chain")
        s_ssm = sem("mx_squares_ready")
        s_ssh = sem("h_squares_ready")
        s_nn = sem("norms_ready")
        s_ratio = sem("ln_argument_ready")
        s_ln = sem("ln_ready")
        s_targ = sem("tanh_argument_ready")
        s_tanh = sem("tanh_ready")
        s_z = sem("z_ready")
        s_zTp = sem("zT_in_psum")
        s_zT = sem("zT_ready")
        s_sqp = sem("square_parts_ready")
        s_sqTp = sem("squares_in_psum")
        s_sqT = sem("squares_row_ready")
        s_zs = sem("z_tile_staged")
        s_key = sem("keys_in_psum")
        s_keyrow = sem("key_chunk_ready")
        s_keyused = sem("key_row_used")
        s_top = sem("top_chain")
        s_topi = sem("top_lists_ready")
        s_w = sem("weights_chain")
        s_sqrt = sem("distances_ready")
        s_exp = sem("similarities_ready")
        s_sstd = sem("second_std_ready")
        s_g2 = sem("last_features_stored")
        s_fin = sem("output_ready")
        s_out = [sem(f"output_stored{i}") for i in range(2)]
        s_last = sem("last_chain")
        waited = {k: sem(f"{k}_has_waited") for k in ("pe", "act", "dve", "pool")}

        block = ctx.enter_context(nc.Block())

        class Count:
            def __init__(self, base):
                self.base, self.k = base, 0

            def up(self):
                self.k += 1
                return self.base + self.k

        parts_of = {0: partsA, 1: partsB, 2: partsA, 3: partsB, 4: partsA, 5: partsB}
        SPLIT_OF_PREP = {0: 0, 1: 2, 2: 3, 3: 4}

        def part(u, g, k):
            return parts_of[u][:, ds(g * G, G), k * FE:(k + 1) * FE]

        def grp(t, g):
            return t[:, ds(g * G, G)]

        def turns(eng, body, first=0):
            body(first, True)
            with eng.Fori(first + 1, NG) as g:
                body(g, False)

        @block.sync
        def _(sp):
            n = 0
            loads = [(W["W0"], w0), (W["W1a"], w1[0:F, :]), (W["W1b"], w1[F:2 * F, :]), (W["W2"], w2),
                     (W["W31"], w31), (W["W32"], w32)]
            sp.dma_start(X[:, :, :], x.rearrange("(t p) f -> p t f", p=P)).then_inc(s_loaded, 16)
            for t, a in loads:
                sp.dma_start(t[:, :], a).then_inc(s_loaded, 16)
            for k, a in (("b0", b0), ("b31", b31), ("b32", b32)):
                sp.dma_start(B[k][:, :], a.partition_broadcast(P)).then_inc(s_loaded, 16)
            sp.wait_ge(s_const, 1)
            sp.dma_start(feat_dram[N:N + 1, :], zero_row[:, :]).then_inc(s_loaded, 16)

            def load_rows(g, q, peeled):
                t = g * G + q
                if not (peeled and q < 2):
                    sp.wait_ge(s_tr, 4 * (t - 1))
                sp.dma_start(rows[:, q % 2, :], adj[ts(t, P), :]).then_inc(s_rows[q % 2], 16)

            def store_panel(g, q):
                t = g * G + q
                sp.wait_ge(s_panel, 4 * (t + 1) + 2)
                sp.dma_start(adjT_dram[ds(t, 1), :, :].rearrange("a p n -> p (a n)"),
                             panel[:, q, :, :].rearrange("p b i -> p (b i)").bitcast(BF16)).then_inc(s_stored[q], 16)

            def turn(g, peeled):
                for q in range(G):
                    load_rows(g, q, peeled)
                    if not (peeled and q == 0):
                        if q:
                            store_panel(g, q - 1)
                        else:
                            store_panel(g - 1, G - 1)
            turns(sp, turn)
            store_panel(NG - 1, G - 1)
            for q in range(G):
                sp.wait_ge(s_stored[q], 16 * NG)

            sp.wait_ge(s_feat, 16 * NG)
            sp.wait_ge(s_flag, 1)
            short = sp.value_load(flag[0:1, 0:1], min_val=0, max_val=1 << 24)
            with sp.If(short > 0):
                with sp.Fori(0, NT) as t:
                    with sp.Fori(0, N // 64) as c:
                        m = t * (N // 64) + c
                        sp.wait_ge(s_gen_used, m + 1)
                        sp.dma_start(general_mask[:, :], adj[ts(t, P), ts(c, 64)]).then_inc(s_gen_m, 16)
                        sp.dma_start(rows[:, :, :].rearrange("p a n -> p (a n)"),
                                     feat_dram[ts(c, 64), :].rearrange("j f -> (j f)").partition_broadcast(P)
                                     ).then_inc(s_gen_f, 16)

            def load_panel(g, q):
                sp.dma_start(panel[:, q, :, :].rearrange("p b i -> p (b i)").bitcast(BF16),
                             adjT_dram[ds(g * G + q, 1), :, :].rearrange("a p n -> p (a n)")
                             ).then_inc(s_load[q], 16)

            def turn(g, peeled):
                for q in range(G):
                    if not peeled:
                        sp.wait_ge(s_tri, 8 * (g * G + q - G + 1))
                    load_panel(g, q)
            turns(sp, turn)
            for ps in range(1, 5):
                def turn(g, peeled):
                    for q in range(G):
                        if peeled and ps == 1:
                            sp.wait_ge(s_tri, 8 * (NT - G + q + 1))
                        else:
                            sp.wait_ge(s_prod, (g + ps * NG) * G + q - G + 1)
                        load_panel(g, q)
                turns(sp, turn)
            sp.wait_ge(s_g2, 16 * NG)

        @block.tensor
        def _(pe):
            pe.wait_ge(s_const, 7)
            pe.wait_ge(s_loaded, 16 * 11)

            def aux(s, g):
                n, m = g + s * NG, g + SPLIT_OF_PREP[s] * NG
                pe.wait_ge(s_norm, n + 1)
                for q in range(G):
                    i = pe.transpose(psT[:, q * P:(q + 1) * P], hn[:, q, :], ident[:, :])
                i.then_inc(s_hTp, 1)
                pe.wait_ge(s_hT, n + 1)
                pe.wait_ge(s_gsc, m + 1)
                ws = {0: ["W0"], 1: ["W1b", "W1a"], 2: ["W2"], 3: ["W31", "W32"]}[s]
                for w, o in zip(ws, (psW, psV)):
                    if o is psV:
                        pe.wait_ge(s_side, (g + (0 if s == 1 else NG)) + 1)
                    for q in range(G):
                        i = pe.matmul(o[:, q * P:(q + 1) * P], hT[:, q * P:(q + 1) * P], W[w][:, :],
                                      start=True, stop=True)
                i.then_inc(s_hw, 1)

            turns(pe, lambda g, peeled: aux(0, g))

            def transposes(g, q):
                t = g * G + q
                pe.wait_ge(s_rows[q % 2], 16 * (g * 2 + q // 2 + 1))
                rb = rows[:, q % 2, :].bitcast(BF16).rearrange("p (n two) -> p n two", two=2)
                for c in range(4):
                    pe.wait_ge(s_panel, 4 * t + c + 1)
                    o = bank[2 + c % 2][:, :].bitcast(BF16)
                    for b in range(8):
                        j = c * 8 + b
                        i = pe.transpose(o[:, b * P:(b + 1) * P], rb[:, j * P:(j + 1) * P, 1], identb[:, :])
                    i.then_inc(s_tr, 1)

            def product(u, T, q, wait_parts=None):
                pe.wait_ge(s_agg, T + 1)
                pe.sem_inc(waited["pe"], 1)
                o = bank[q % 2]
                for j in range(NT):
                    if wait_parts is not None and j % G == 0:
                        pe.wait_ge(s_parts, wait_parts + j // G + 1)
                        pe.sem_inc(waited["pe"], 1)
                    i = pe.matmul(o[:, 0:FW], panel[:, q, j, :], parts_of[u][:, j, :],
                                  start=(j == 0), stop=(j == NT - 1))
                return i

            def codes(g, q):
                t = g * G + q
                for c in range(NT // BPB):
                    pe.wait_ge(s_code_used, 8 * t + c + 1)
                    pe.sem_inc(waited["pe"], 1)
                    for b in range(BPB):
                        i = pe.matmul(bank[4 + c % 2][:, b * P:(b + 1) * P], panel[:, q, c * BPB + b, :],
                                      diag_code[:, :], start=True, stop=True)
                    i.then_inc(s_code, 1)

            def taken(g, q, wait_parts=None):
                t = g * G + q
                pe.wait_ge(s_panel, 4 * (t + 1) + 2)
                product(0, t, q, wait_parts).then_inc(s_prod, 1)
                codes(g, q)

            def turn(g, peeled):
                for q in range(G):
                    transposes(g, q)
                    if q:
                        taken(g, q - 1, 0 if (peeled and q == 1) else None)
                    elif not peeled:
                        taken(g - 1, G - 1)
            turns(pe, turn)
            taken(NG - 1, G - 1)

            pe.wait_ge(s_deg, 3)
            pe.matmul(psT[0:1, 0:1], missing_n[:, 0:1], ones_col[:, 0:1], start=True, stop=True
                      ).then_inc(s_missing, 1)

            pparts = parts_of[1]

            def firsts(g, q, peeled):
                t = g * G + q
                pe.wait_ge(s_load[q], 16 * (g + 1))

                def tri_chunk(c):
                    pe.wait_ge(s_first, 8 * t + c + 1)
                    pe.sem_inc(waited["pe"], 1)
                    i = pe.matmul(bank[2 + c % 2][:, :], tri[:, :],
                                  panel[:, q, c * BPB:(c + 1) * BPB, :].rearrange("p b i -> p (b i)"),
                                  start=True, stop=True)
                    i.then_inc(s_tri, 1)

                tri_chunk(0)
                tri_chunk(1)
                for c in range(NT // BPB):
                    pe.wait_ge(s_first, 8 * t + c + 3)
                    pe.wait_ge(s_fp_used, 8 * t + c + 1)
                    pe.sem_inc(waited["pe"], 1)
                    for b in range(BPB):
                        j = c * BPB + b
                        for k in range(3):
                            i = pe.matmul(bank[c % 2][:, b * P:(b + 1) * P], first[:, q % 2, j, :],
                                          pparts[:, j, k * FE:k * FE + F], start=(k == 0), stop=(k == 2))
                    i.then_inc(s_fp, 1)
                    if c + 2 < NT // BPB:
                        tri_chunk(c + 2)

            def pool_turn(g, peeled):
                for q in range(G):
                    firsts(g, q, peeled)
                if not peeled:
                    aux(1, g - 1)
            pe.wait_ge(s_parts, 2 * NG)
            turns(pe, pool_turn)
            aux(1, NG - 1)

            def layer(u, ps, s):
                def turn(g, peeled):
                    for q in range(G):
                        pe.wait_ge(s_load[q], 16 * (g + ps * NG + 1))
                        T = (g + ps * NG) * G + q
                        product(u, T, q, u * NG if (peeled and q == 0) else None).then_inc(s_prod, 1)
                    if not peeled and s is not None:
                        aux(s, g - 1)
                turns(pe, turn)
                if s is not None:
                    aux(s, NG - 1)

            pe.wait_ge(s_fp_used, 8 * NT + 2)
            layer(2, 1, 2)
            layer(3, 2, 3)

            def z_aux(g, peeled):
                if not peeled:
                    pe.wait_ge(s_zT, g)
                    pe.wait_ge(s_sqT, g)
                pe.wait_ge(s_z, g + 1)
                for q in range(G):
                    i = pe.transpose(psT[:, q * P:(q + 1) * P], agg[:, q, 0:F], ident[:, :])
                i.then_inc(s_zTp, 1)
                pe.wait_ge(s_sqp, g + 1)
                for q in range(G):
                    i = pe.transpose(psW[0:3, :].bitcast(BF16)[:, q * P:(q + 1) * P], sqp[:, q, :], identb[:, :])
                i.then_inc(s_sqTp, 1)

            def turn3(g, peeled):
                for q in range(G):
                    pe.wait_ge(s_load[q], 16 * (g + 3 * NG + 1))
                    product(4, (g + 3 * NG) * G + q, q, 4 * NG if (peeled and q == 0) else None).then_inc(s_prod, 1)
                z_aux(g, peeled)
            turns(pe, turn3)

            pe.wait_ge(s_zT, NG)
            pe.wait_ge(s_sqT, NG)
            pe.wait_ge(s_agg, 4 * NT + 2)

            def keys(g, peeled):
                for q in range(G):
                    t = g * G + q
                    pe.wait_ge(s_zs, t + 1)
                    for c in range(8):
                        pe.wait_ge(s_keyrow, 8 * t + c + 1)
                        o = bank[c % 4]
                        pe.matmul(o[:, :], zs[:, q % 2, :], zT[:, c * 512:(c + 1) * 512], start=True, stop=False)
                        pe.matmul(o[:, :], ones3[:, :], SQT[:, c * 512:(c + 1) * 512], start=False, stop=True
                                  ).then_inc(s_key, 1)
            with pe.Fori(0, NG) as g:
                keys(g, False)
            pe.wait_ge(s_keyrow, 8 * NT + 4)
            layer(5, 4, None)

        @block.scalar
        def _(act):
            act.wait_ge(s_const, 7)
            for s, k in ((s_panel, 2), (s_first, 2), (s_side, 1), (s_keyrow, 4)):
                act.sem_inc(s, k)

            def std_of(s, g):
                n = g + s * NG
                act.wait_ge(s_mv, n + 1)
                act.activation(std[:, :], mv[:, :, 1], ACT.Sqrt, bias=eps_ln[:, 0:1]).then_inc(s_std, 1)

            def hT_of(s, g):
                act.wait_ge(s_hTp, g + s * NG + 1)
                act.activation(hT[:, :], psT[:, :], ACT.Relu).then_inc(s_hT, 1)

            def side_of(s, g):
                act.wait_ge(s_hw, g + s * NG + 1)
                act.copy(grp(side, g), psV[:, :].rearrange("p (q f) -> p q f", q=G)).then_inc(s_side, 1)

            def split(u, g):
                m = g + u * NG
                act.wait_ge(s_gsc, m + 2)
                act.copy(part(u, g, 0), gsc[:, :, :]).then_inc(s_p0, 1)
                act.wait_ge(s_rem, m + 2)
                act.copy(part(u, g, 1), rem[:, :, :]).then_inc(s_p1, 1)

            def turn(g, peeled):
                std_of(0, g)
                hT_of(0, g)
                if not peeled:
                    split(0, g - 1)
            turns(act, turn)
            split(0, NG - 1)

            def evac_panel(g, q, first_group):
                t = g * G + q
                if not first_group:
                    act.wait_ge(s_stored[q], 16 * g)
                    act.wait_ge(s_code, 8 * (t - G + 1))
                for c in range(4):
                    act.wait_ge(s_tr, 4 * t + c + 1)
                    act.sem_inc(waited["act"], 1)
                    act.activation(panel[:, q, c * 8:(c + 1) * 8, :].rearrange("p b i -> p (b i)"),
                                   bank[2 + c % 2][:, :].bitcast(BF16), ACT.Copy, saturate=False
                                   ).then_inc(s_panel, 1)

            def feat_store(g):
                act.wait_ge(s_post, 2 * (g + 1))
                act.dma_start(feat_dram[ds(g * G * P, G * P), :].rearrange("(t p) f -> p t f", p=P),
                              gsc[:, :, 0:F]).then_inc(s_feat, 16)

            def turn(g, peeled):
                for q in range(G):
                    evac_panel(g, q, peeled)
                    if q == 2 and not peeled:
                        feat_store(g - 1)
                        split(1, g - 1)
            turns(act, turn)
            feat_store(NG - 1)
            split(1, NG - 1)

            act.wait_ge(s_deg, 3)
            act.activation(DSTD[:, :], DEG[:, :], ACT.Sqrt).then_inc(s_sstd, 1)

            def firsts(g, q):
                t = g * G + q
                for c in range(8):
                    act.wait_ge(s_tri, 8 * t + c + 1)
                    act.sem_inc(waited["act"], 1)
                    act.activation(first[:, q % 2, c * BPB:(c + 1) * BPB, :].rearrange("p b i -> p (b i)"),
                                   bank[2 + c % 2][:, :], ACT.Relu, saturate=False).then_inc(s_first, 1)

            def after(u, s, g, more=None):
                hT_of(s, g)
                if s in (1, 3):
                    side_of(s, g)
                if more:
                    more(g)
                split(u, g)

            def turn(g, peeled):
                for q in range(G):
                    firsts(g, q)
                if not peeled:
                    after(2, 1, g - 1)
                std_of(1, g)
            turns(act, turn)
            after(2, 1, NG - 1)

            def ball_in(g):
                act.wait_ge(s_hw, g + 2 * NG + 1)
                for q in range(G):
                    i = act.activation(sq_junk[:, q, :], psW[:, q * P:(q + 1) * P], ACT.Square,
                                       accum_out=ss[:, 1, q:q + 1])
                i.then_inc(s_ssm, 1)
                act.wait_ge(s_ssm, g + 1)
                act.wait_ge(s_ssh, g + 1)
                act.activation(nn[:, :, :], ss[:, :, :], ACT.Sqrt).then_inc(s_nn, 1)
                act.wait_ge(s_ratio, g + 1)
                act.activation(v[3][:, :], v[2][:, :], ACT.Ln).then_inc(s_ln, 1)
                act.wait_ge(s_targ, g + 1)
                act.activation(v[5][:, :], v[4][:, :], ACT.Tanh).then_inc(s_tanh, 1)

            def turn(g, peeled):
                if not peeled:
                    after(3, 2, g - 1, ball_in)
                std_of(2, g)
            turns(act, turn)
            after(3, 2, NG - 1, ball_in)

            def ball_out(g):
                act.wait_ge(s_ssm, NG + g + 1)
                act.activation(nn[:, :, :], ss[:, :, :], ACT.Sqrt).then_inc(s_nn, 1)
                act.wait_ge(s_ratio, NG + g + 1)
                act.activation(v[3][:, :], v[2][:, :], ACT.Ln).then_inc(s_ln, 1)
                act.wait_ge(s_targ, NG + g + 1)
                act.activation(v[5][:, :], v[4][:, :], ACT.Tanh).then_inc(s_tanh, 1)

            def turn(g, peeled):
                if not peeled:
                    after(4, 3, g - 1)
                ball_out(g)
                std_of(3, g)
            turns(act, turn)
            after(4, 3, NG - 1)

            with act.Fori(0, NG) as g:
                act.wait_ge(s_zTp, g + 1)
                act.copy(zT[:, ds(g * G * P, G * P)], psT[:, :]).then_inc(s_zT, 1)
                act.wait_ge(s_sqTp, g + 1)
                act.copy(SQT[:, ds(g * G * P, G * P)], psW[0:3, :].bitcast(BF16)[:, 0:G * P]).then_inc(s_sqT, 1)

            act.wait_ge(s_zT, NG)
            with act.Fori(0, NG) as g:
                for q in range(G):
                    t = g * G + q
                    act.wait_ge(s_keyused, t + 1)
                    act.copy(zs[:, q % 2, :], zT[:, ts(t, P)]).then_inc(s_zs, 1)
                    for c in range(8):
                        act.wait_ge(s_key, 8 * t + c + 1)
                        act.copy(rows[:, q % 2, c * 512:(c + 1) * 512], bank[c % 4][:, :]).then_inc(s_keyrow, 1)

            act.wait_ge(s_w, 2)
            act.activation(DR[:, :, :], D2c[:, :, :], ACT.Sqrt, bias=eps_dist[:, 0:1]).then_inc(s_sqrt, 1)
            act.wait_ge(s_sqrt, 1)
            act.activation(S[:, :, :], DR[:, :, :], ACT.Exp, scale=-0.5).then_inc(s_exp, 1)
            act.wait_ge(s_w, 4)
            act.activation(SSTD[:, :], SDEG[:, :], ACT.Sqrt).then_inc(s_sstd, 1)

            with act.Fori(0, NG) as g:
                act.wait_ge(s_gsc, g + 5 * NG + 2)
                act.dma_start(g2_dram[ds(g * G * P, G * P), :].rearrange("(t p) f -> p t f", p=P),
                              gsc[:, :, 0:F]).then_inc(s_g2, 16)
                split(5, g)
                act.wait_ge(s_g2, 16 * (g + 1))

            with act.Fori(0, NG // 2) as h:
                for r in range(2):
                    g = h * 2 + r
                    act.wait_ge(s_fin, g + 1)
                    act.dma_start(out[ds(g * G * P, G * P), :].rearrange("(t p) f -> p t f", p=P),
                                 fin[:, r, :, :]).then_inc(s_out[r], 16)
            for r in range(2):
                act.wait_ge(s_out[r], 16 * (NG // 2))

        @block.gpsimd
        def _(pool):
            pool.memset(zero_row[:, :], 0.0).then_inc(s_const, 1)
            pool.memset(ident[:, :], 0.0).then_inc(s_const, 1)
            pool.wait_ge(s_const, 2)
            pool.affine_select(out=ident[:, :], in_=ident[:, :], compare_op=ALU.not_equal, fill=1.0, base=0,
                               pattern=[[-1, P]], channel_multiplier=1).then_inc(s_const, 1)
            pool.iota(code_row[:, :], pattern=[[-1, P]], base=P, channel_multiplier=0,
                      allow_small_or_imprecise_dtypes=True)
            pool.iota(block_code[:, :, :], pattern=[[-P, NT], [0, 7]], base=N - P, channel_multiplier=0,
                      allow_small_or_imprecise_dtypes=True)
            pool.memset(eps_ln[:, :], LN_EPS)
            pool.memset(eps_dist[:, :], DISTANCE_EPS)
            pool.memset(ones_col[:, :], 1.0)
            pool.memset(ones3[:, :], 1.0)
            pool.memset(gsc[:, :, F:FE], 1.0)
            pool.memset(wide[:, :, :], 0.0).then_inc(s_const, 1)
            pool.wait_ge(s_const, 4)
            pool.tensor_copy(identb[:, :], ident[:, :]).then_inc(s_const, 1)
            pool.tensor_tensor(diag_code[:, :], ident[:, :], code_row[:, :], ALU.mult).then_inc(s_const, 1)
            pool.affine_select(out=tri[:, :], in_=ident[:, :], compare_op=ALU.is_ge, fill=-1.0, base=0,
                               pattern=[[-1, P]], channel_multiplier=1).then_inc(s_const, 1)
            pool.sem_inc(s_rem, 1)

            def split(u, g):
                m = g + u * NG
                pool.wait_ge(s_p0, m + 1)
                pool.tensor_tensor(rem[:, :, :], gsc[:, :, :], part(u, g, 0), ALU.subtract).then_inc(s_rem, 1)
                pool.wait_ge(s_p1, m + 1)
                pool.tensor_tensor(part(u, g, 2), rem[:, :, :], part(u, g, 1), ALU.subtract).then_inc(s_parts, 1)
                pool.wait_ge(s_parts, m + 1)

            with pool.Fori(0, NG) as g:
                split(0, g)
            with pool.Fori(0, NG) as g:
                split(1, g)

            pool.wait_ge(s_feat, 16 * NG)
            pool.wait_ge(s_loaded, 16 * 11)
            pool.wait_ge(s_list, 8 * NT + 2 * NG)

            def gathers(g, q):
                t = g * G + q
                pool.wait_ge(s_gath_used, t + 1)
                pool.tensor_copy(idx_now[:, q % 2, :], IDX[:, ds(t, 1), :].rearrange("p a k -> p (a k)")
                                 ).then_inc(s_idx, 1)
                pool.wait_ge(s_idx, t + 1)
                pool.sem_inc(waited["pool"], 1)
                for k in range(LIST):
                    pool.indirect_dma_start(gath[:, q % 2, k, :], None, feat_dram,
                                            bass.IndirectOffsetOnAxis(idx_now[:, q % 2, k:k + 1], axis=0)
                                            ).then_inc(s_gath[q % 2], 16)

            def turn(g, peeled):
                for q in range(G):
                    gathers(g, q)
                if not peeled:
                    split(2, g - 1)
            turns(pool, turn)
            split(2, NG - 1)
            for u in (3, 4):
                with pool.Fori(0, NG) as g:
                    split(u, g)
            with pool.Fori(0, NG) as g:
                split(5, g)

            pool.wait_ge(s_g2, 16 * NG)

            def last_gathers(g, q):
                t = NT + g * G + q
                pool.wait_ge(s_gath_used, t + 1)
                pool.tensor_copy(idx_now[:, q % 2, 0:TOP], TI[:, ds(g * G + q, 1), :].rearrange("p a k -> p (a k)")
                                 ).then_inc(s_idx, 1)
                pool.wait_ge(s_idx, t + 1)
                pool.sem_inc(waited["pool"], 1)
                for k in range(TOP):
                    pool.indirect_dma_start(gath[:, q % 2, k, :], None, g2_dram,
                                            bass.IndirectOffsetOnAxis(idx_now[:, q % 2, k:k + 1], axis=0)
                                            ).then_inc(s_gath[q % 2], 16)
            with pool.Fori(0, NG) as g:
                for q in range(G):
                    last_gathers(g, q)

        @block.vector
        def _(dve):
            V = [t[:, :] for t in v]
            dve.wait_ge(s_const, 7)
            dve.wait_ge(s_loaded, 16 * 11)
            for s, k in ((s_gsc, 1), (s_agg, 2), (s_code_used, 2), (s_fp_used, 2), (s_gath_used, 2),
                         (s_keyused, 2), (s_gen_used, 1)):
                dve.sem_inc(s, k)

            def per_row(t2, width=F):
                return t2.unsqueeze(2).to_broadcast([P, G, width])

            def bias3(k):
                return B[k][:, :].unsqueeze(1).to_broadcast([P, G, F])

            def normalise(s, g):
                n = g + s * NG
                dve.wait_ge(s_x, n + 1)
                for q in range(G):
                    i = dve.bn_stats(st[:, q, :], xg[:, q, :])
                i.then_inc(s_stats, 1)
                dve.wait_ge(s_stats, n + 1)
                dve.sem_inc(waited["dve"], 1)
                for q in range(G):
                    i = dve.bn_aggr(mv[:, q, :], st[:, q, :])
                i.then_inc(s_mv, 1)
                dve.wait_ge(s_std, n + 1)
                dve.reciprocal(rstd[:, :], std[:, :]).then_inc(s_rstd, 1)
                dve.wait_ge(s_rstd, n + 1)
                for q in range(G):
                    i = dve.tensor_scalar(hn[:, q, :], xg[:, q, :], mv[:, q, 0:1], rstd[:, q:q + 1],
                                          ALU.subtract, ALU.mult)
                i.then_inc(s_norm, 1)

            def gsc_free(u, g):
                dve.wait_ge(s_rem, g + u * NG + 1)

            def operand(s, g):
                u = SPLIT_OF_PREP[s]
                dve.wait_ge(s_hw, g + s * NG + 1)
                gsc_free(u, g)
                ps = psW[:, :].rearrange("p (q f) -> p q f", q=G)
                if s == 3:
                    dve.tensor_tensor(gsc[:, :, 0:F], ps, per_row(grp(DINV, g)), ALU.mult).then_inc(s_gsc, 1)
                else:
                    dve.tensor_copy(gsc[:, :, 0:F], ps).then_inc(s_gsc, 1)

            def turn(g, peeled):
                if not peeled:
                    dve.wait_ge(s_norm, g)
                    dve.wait_ge(s_hTp, g)
                dve.tensor_copy(xg[:, :, :], grp(X, g)).then_inc(s_x, 1)
                normalise(0, g)
                if not peeled:
                    operand(0, g - 1)
            turns(dve, turn)
            operand(0, NG - 1)

            def take_product(T, q):
                dve.wait_ge(s_prod, T + 1)
                dve.tensor_reduce(agg[:, q, :], bank[q % 2][:, 0:FW].rearrange("p (k f) -> p f k", k=3),
                                  axis=AX, op=ALU.add).then_inc(s_agg, 1)

            LSTEPS = 8

            def lists(g, q):
                t = g * G + q
                c = Count(t * LSTEPS + g * 2)
                for ch in range(NT // BPB):
                    dve.wait_ge(s_code, 8 * t + ch + 1)
                    dve.sem_inc(waited["dve"], 1)
                    for b in range(BPB):
                        i = dve.max(cand[:, ch * BPB + b, :], bank[4 + ch % 2][:, b * P:(b + 1) * P])
                    i.then_inc(s_code_used, 1)
                dve.wait_ge(s_code_used, 8 * (t + 1) + 2)
                r3 = rest[:, :].rearrange("p (b k) -> p b k", k=7)
                dve.scalar_tensor_tensor(r3, cand[:, :, 1:8], 0.0, block_code[:, :, :], ALU.is_gt, ALU.mult).then_inc(s_list, 1)
                dve.wait_ge(s_list, c.up())
                dve.tensor_tensor(r3, r3, cand[:, :, 1:8], ALU.add).then_inc(s_list, 1)
                dve.wait_ge(s_list, c.up())
                dve.sem_inc(waited["dve"], 1)
                dve.max(listed[:, q, 0:8], rest[:, :]).then_inc(s_list, 1)
                dve.wait_ge(s_list, c.up())
                dve.scalar_tensor_tensor(rest2[:, :], rest[:, :], listed[:, q, 7:8], rest[:, :],
                                         ALU.is_lt, ALU.mult).then_inc(s_list, 1)
                dve.wait_ge(s_list, c.up())
                dve.sem_inc(waited["dve"], 1)
                dve.max(listed[:, q, 8:16], rest2[:, :]).then_inc(s_list, 1)
                dve.wait_ge(s_list, c.up())
                dve.tensor_scalar(found[:, q, 0:NT], cand[:, :, 0], 0.0, None, ALU.is_gt).then_inc(s_list, 1)
                dve.wait_ge(s_list, c.up())
                dve.tensor_scalar(found[:, q, NT:NT + LIST], listed[:, q, :], 0.0, None, ALU.is_gt).then_inc(s_list, 1)
                dve.wait_ge(s_list, c.up())
                dve.tensor_reduce(found_n[:, q:q + 1], found[:, q, :], axis=AX, op=ALU.add).then_inc(s_list, 1)
                dve.wait_ge(s_list, c.up())

            def lists_out(g):
                c = Count((g * G + G) * LSTEPS + g * 2)
                dve.tensor_scalar(grp(IDX, g), listed[:, :, :], -1.0, float(N), ALU.mult, ALU.add).then_inc(s_list, 1)
                dve.wait_ge(s_list, c.up())
                dve.tensor_copy(grp(FOUND, g), found_n[:, :]).then_inc(s_list, 1)
                dve.wait_ge(s_list, c.up())

            def layer0_out(g):
                dve.wait_ge(s_agg, (g + 1) * G + 2)
                dve.tensor_copy(grp(DEG, g), agg[:, :, F]).then_inc(s_y, 1)
                gsc_free(1, g)
                if isinstance(g, int) and g == 0:
                    pass
                else:
                    dve.wait_ge(s_feat, 16 * g)
                dve.tensor_tensor(tmp[:, :, :], agg[:, :, 0:F], bias3("b0"), ALU.add).then_inc(s_post, 1)
                dve.wait_ge(s_post, 2 * g + 1)
                dve.wait_ge(s_y, g + 1)
                dve.tensor_scalar(gsc[:, :, 0:F], tmp[:, :, :], 0.0, None, ALU.max).then_inc(s_post, 1)
                dve.wait_ge(s_post, 2 * g + 2)
                dve.sem_inc(s_gsc, 1)

            def turn(g, peeled):
                for q in range(G):
                    take_product(g * G + q, q)
                    lists(g, q)
                lists_out(g)
                layer0_out(g)
            turns(dve, turn)

            dve.wait_ge(s_y, NG)
            dve.tensor_tensor(missing[:, :], DEG[:, :], FOUND[:, :], ALU.subtract).then_inc(s_deg, 1)
            dve.tensor_scalar(NOROW[:, :], DEG[:, :], 0.0, -FLT_MAX, ALU.is_equal, ALU.mult).then_inc(s_deg, 1)
            dve.wait_ge(s_deg, 2)
            dve.tensor_reduce(missing_n[:, :], missing[:, :], axis=AX, op=ALU.add).then_inc(s_deg, 1)
            dve.wait_ge(s_sstd, 1)
            dve.reciprocal(DINV[:, :], DSTD[:, :]).then_inc(s_deg, 1)
            dve.wait_ge(s_missing, 1)
            dve.tensor_copy(flag[0:1, 0:1], psT[0:1, 0:1]).then_inc(s_flag, 1)
            dve.wait_ge(s_flag, 1)
            short = dve.value_load(flag[0:1, 0:1], min_val=0, max_val=1 << 24)
            with dve.If(short > 0):
                CH = N // 64
                feats = rows[:, :, :].rearrange("p a (j f) -> p (a j) f", f=F)
                with dve.Fori(0, NT) as t:
                    dve.memset(general_acc[:, :], 0.0).then_inc(s_gen, 1)
                    with dve.Fori(0, CH) as c:
                        m = t * CH + c
                        k = t * (4 * CH + 2) + c * 4 + 1
                        dve.wait_ge(s_gen, k)
                        dve.wait_ge(s_gen_m, 16 * (m + 1))
                        dve.tensor_scalar(general_cap[:, :], general_mask[:, :], 0.0, FLT_MAX, ALU.not_equal,
                                          ALU.mult).then_inc(s_gen, 1)
                        dve.wait_ge(s_gen, k + 1)
                        dve.wait_ge(s_gen_f, 16 * (m + 1))
                        dve.tensor_tensor(feats, feats, general_cap[:, :].unsqueeze(2).to_broadcast([P, 64, F]),
                                          ALU.min).then_inc(s_gen, 1)
                        dve.wait_ge(s_gen, k + 2)
                        dve.tensor_reduce(general_new[:, :], feats.rearrange("p j f -> p f j"), axis=AX,
                                          op=ALU.max).then_inc(s_gen, 1)
                        dve.wait_ge(s_gen, k + 3)
                        dve.tensor_tensor(general_acc[:, :], general_acc[:, :], general_new[:, :], ALU.max
                                          ).then_inc(s_gen, 1)
                        dve.wait_ge(s_gen, k + 4)
                        dve.sem_inc(s_gen_used, 1)
                    dve.tensor_copy(wide[:, ds(t, 1), :].rearrange("p a f -> p (a f)"), general_acc[:, :]
                                    ).then_inc(s_gen, 1)
                    dve.wait_ge(s_gen, (t + 1) * (4 * CH + 2))

            dve.wait_ge(s_deg, 4)
            dve.wait_ge(s_feat, 16 * NG)

            def pooled(g, q):
                t = g * G + q
                for c in range(8):
                    dve.wait_ge(s_fp, 8 * t + c + 1)
                    dve.tensor_reduce(gath[:, q % 2, LIST + c, :],
                                      bank[c % 2][:, :].rearrange("p (b f) -> p f b", b=BPB),
                                      axis=AX, op=ALU.max).then_inc(s_fp_used, 1)
                dve.wait_ge(s_fp_used, 8 * (t + 1) + 2)
                dve.wait_ge(s_gath[q % 2], 16 * LIST * (g * 2 + q // 2 + 1))
                dve.tensor_reduce(tmp[:, q, :], gath[:, q % 2, :, :].rearrange("p k f -> p f k"), axis=AX,
                                  op=ALU.max).then_inc(s_gath_used, 1)

            def turn(g, peeled):
                for q in range(G):
                    pooled(g, q)
                if not peeled:
                    operand(1, g - 1)
                c = Count(2 * NG + g * 3)
                dve.wait_ge(s_gath_used, (g + 1) * G + 2)
                dve.tensor_tensor(tmp[:, :, :], tmp[:, :, :], grp(wide, g), ALU.max).then_inc(s_post, 1)
                dve.wait_ge(s_post, c.up())
                dve.tensor_tensor(tmp[:, :, :], tmp[:, :, :], per_row(grp(NOROW, g)), ALU.add).then_inc(s_post, 1)
                dve.wait_ge(s_post, c.up())
                dve.tensor_tensor(xg[:, :, :], grp(X, g), tmp[:, :, :], ALU.add).then_inc(s_x, 1)
                dve.tensor_tensor(grp(X, g), grp(X, g), tmp[:, :, :], ALU.add).then_inc(s_post, 1)
                dve.wait_ge(s_post, c.up())
                normalise(1, g)
            turns(dve, turn)
            operand(1, NG - 1)

            def half_square(g):
                for q in range(G):
                    i = dve.scalar_tensor_tensor(relu_junk[:, q, :], hn[:, q, :], 0.0, hn[:, q, :], ALU.max, ALU.mult,
                                                 accum_out=ss[:, 0, q:q + 1])
                i.then_inc(s_ssh, 1)

            ASTEPS = 17

            def artanh(c, x_, s_base):
                t_, t2 = V[0], V[1]
                dve.tensor_scalar(t_, x_, BALL_CLIP, None, ALU.min).then_inc(s_hyp, 1)
                dve.wait_ge(s_hyp, c.up())
                dve.tensor_scalar(V[7], t_, -1.0, 1.0, ALU.mult, ALU.add).then_inc(s_hyp, 1)
                dve.wait_ge(s_hyp, c.up())
                dve.reciprocal(V[8], V[7]).then_inc(s_hyp, 1)
                dve.wait_ge(s_hyp, c.up())
                dve.scalar_tensor_tensor(V[2], t_, 1.0, V[8], ALU.add, ALU.mult).then_inc(s_ratio, 1)
                dve.tensor_tensor(t2, t_, t_, ALU.mult).then_inc(s_hyp, 1)
                dve.wait_ge(s_hyp, c.up())
                dve.tensor_scalar(V[9], t2, 1.0 / 11, None, ALU.mult).then_inc(s_hyp, 1)
                dve.wait_ge(s_hyp, c.up())
                for k in (9, 7, 5, 3):
                    dve.scalar_tensor_tensor(V[9], V[9], 1.0 / k, t2, ALU.add, ALU.mult).then_inc(s_hyp, 1)
                    dve.wait_ge(s_hyp, c.up())
                dve.scalar_tensor_tensor(V[9], V[9], 1.0, t_, ALU.add, ALU.mult).then_inc(s_hyp, 1)
                dve.wait_ge(s_hyp, c.up())
                dve.tensor_scalar(V[10], t_, 0.25, None, ALU.is_lt).then_inc(s_hyp, 1)
                dve.wait_ge(s_hyp, c.up())
                dve.wait_ge(s_ln, s_base + 1)
                dve.tensor_scalar(V[11], V[3], 0.5, None, ALU.mult).then_inc(s_hyp, 1)
                dve.wait_ge(s_hyp, c.up())
                dve.tensor_tensor(V[12], V[9], V[11], ALU.subtract).then_inc(s_hyp, 1)
                dve.wait_ge(s_hyp, c.up())
                dve.tensor_tensor(V[12], V[12], V[10], ALU.mult).then_inc(s_hyp, 1)
                dve.wait_ge(s_hyp, c.up())
                dve.tensor_tensor(V[6], V[12], V[11], ALU.add).then_inc(s_hyp, 1)
                dve.wait_ge(s_hyp, c.up())

            ISTEPS = 26

            def operand_ball(g):
                c = Count(g * ISTEPS)
                gsc_free(3, g)
                dve.wait_ge(s_nn, g + 1)
                dve.tensor_scalar(nn[:, :, :], nn[:, :, :], MIN_NORM, None, ALU.max).then_inc(s_hyp, 1)
                dve.wait_ge(s_hyp, c.up())
                artanh(c, nn[:, 0, :], g)
                dve.reciprocal(V[13], nn[:, 0, :]).then_inc(s_hyp, 1)
                dve.wait_ge(s_hyp, c.up())
                dve.reciprocal(V[14], nn[:, 1, :]).then_inc(s_hyp, 1)
                dve.wait_ge(s_hyp, c.up())
                dve.tensor_tensor(V[13], V[13], nn[:, 1, :], ALU.mult).then_inc(s_hyp, 1)
                dve.wait_ge(s_hyp, c.up())
                dve.tensor_tensor(V[4], V[13], V[6], ALU.mult).then_inc(s_targ, 1)
                dve.wait_ge(s_tanh, g + 1)
                dve.tensor_tensor(V[7], V[5], V[5], ALU.mult).then_inc(s_hyp, 1)
                dve.wait_ge(s_hyp, c.up())
                dve.tensor_scalar(V[7], V[7], -1.0, 1.0, ALU.mult, ALU.add).then_inc(s_hyp, 1)
                dve.wait_ge(s_hyp, c.up())
                dve.tensor_scalar(V[7], V[7], BALL_EPS, 0.5, ALU.max, ALU.mult).then_inc(s_hyp, 1)
                dve.wait_ge(s_hyp, c.up())
                dve.reciprocal(V[8], V[7]).then_inc(s_hyp, 1)
                dve.wait_ge(s_hyp, c.up())
                dve.tensor_scalar(gsc[:, :, F], V[8], 1.0, None, ALU.subtract).then_inc(s_hyp, 1)
                dve.wait_ge(s_hyp, c.up())
                dve.tensor_tensor(V[9], V[8], V[5], ALU.mult).then_inc(s_hyp, 1)
                dve.wait_ge(s_hyp, c.up())
                dve.tensor_tensor(V[9], V[9], V[14], ALU.mult).then_inc(s_hyp, 1)
                dve.wait_ge(s_hyp, c.up())
                assert c.k <= ISTEPS, c.k
                for _i in range(ISTEPS - c.k):
                    dve.sem_inc(s_hyp, 1)
                dve.tensor_tensor(gsc[:, :, 0:F], psW[:, :].rearrange("p (q f) -> p q f", q=G), per_row(V[9]),
                                  ALU.mult).then_inc(s_gsc, 1)
                dve.wait_ge(s_gsc, g + 3 * NG + 2)

            def turn(g, peeled):
                for q in range(G):
                    take_product((g + NG) * G + q, q)
                if not peeled:
                    operand_ball(g - 1)
                c = Count(5 * NG + g * 2)
                dve.wait_ge(s_agg, (g + NG + 1) * G + 2)
                dve.wait_ge(s_side, g + 2)
                dve.tensor_tensor(tmp[:, :, :], agg[:, :, 0:F], grp(side, g), ALU.add).then_inc(s_post, 1)
                dve.wait_ge(s_post, c.up())
                dve.tensor_tensor(xg[:, :, :], grp(X, g), tmp[:, :, :], ALU.add).then_inc(s_x, 1)
                dve.tensor_tensor(grp(X, g), grp(X, g), tmp[:, :, :], ALU.add).then_inc(s_post, 1)
                dve.wait_ge(s_post, c.up())
                normalise(2, g)
                dve.wait_ge(s_norm, g + 2 * NG + 1)
                half_square(g)
            turns(dve, turn)
            operand_ball(NG - 1)

            OSTEPS = 40

            def ball_out(g):
                c = Count(NG * ISTEPS + g * OSTEPS)
                dve.tensor_scalar(V[15], agg[:, :, F], MIN_DENOMINATOR, None, ALU.max).then_inc(s_hyp, 1)
                dve.wait_ge(s_hyp, c.up())
                dve.reciprocal(V[15], V[15]).then_inc(s_hyp, 1)
                dve.wait_ge(s_hyp, c.up())
                dve.tensor_tensor(tmp[:, :, :], agg[:, :, 0:F], per_row(V[15]), ALU.mult).then_inc(s_hyp, 1)
                dve.wait_ge(s_hyp, c.up())
                for q in range(G):
                    dve.scalar_tensor_tensor(relu_junk[:, q, :], tmp[:, q, :], 1.0, tmp[:, q, :], ALU.mult, ALU.mult,
                                             accum_out=ss[:, 0, q:q + 1]).then_inc(s_hyp, 1)
                    dve.wait_ge(s_hyp, c.up())
                    dve.scalar_tensor_tensor(relu_junk[:, q, :], tmp[:, q, :], 0.0, tmp[:, q, :], ALU.max, ALU.mult,
                                             accum_out=ss[:, 1, q:q + 1]).then_inc(s_hyp, 1)
                    dve.wait_ge(s_hyp, c.up())
                dve.sem_inc(s_ssm, 1)
                dve.wait_ge(s_nn, NG + g + 1)
                dve.tensor_scalar(V[13], nn[:, 0, :], MIN_NORM, None, ALU.max).then_inc(s_hyp, 1)
                dve.wait_ge(s_hyp, c.up())
                artanh(c, V[13], NG + g)
                dve.reciprocal(V[13], V[13]).then_inc(s_hyp, 1)
                dve.wait_ge(s_hyp, c.up())
                dve.tensor_tensor(V[6], V[6], grp(DEG, g), ALU.mult).then_inc(s_hyp, 1)
                dve.wait_ge(s_hyp, c.up())
                dve.tensor_scalar(V[6], V[6], 0.5, ARTANH_CLIP, ALU.mult, ALU.min).then_inc(s_hyp, 1)
                dve.wait_ge(s_hyp, c.up())
                dve.tensor_tensor(V[14], V[6], V[13], ALU.mult).then_inc(s_hyp, 1)
                dve.wait_ge(s_hyp, c.up())
                dve.tensor_tensor(V[4], V[14], nn[:, 1, :], ALU.mult).then_inc(s_targ, 1)
                dve.wait_ge(s_targ, NG + g + 1)
                dve.tensor_scalar(V[7], V[4], MIN_NORM, None, ALU.max).then_inc(s_hyp, 1)
                dve.wait_ge(s_hyp, c.up())
                dve.reciprocal(V[8], V[7]).then_inc(s_hyp, 1)
                dve.wait_ge(s_hyp, c.up())
                dve.tensor_tensor(V[8], V[8], V[14], ALU.mult).then_inc(s_hyp, 1)
                dve.wait_ge(s_hyp, c.up())
                dve.wait_ge(s_tanh, NG + g + 1)
                dve.tensor_tensor(V[8], V[8], V[5], ALU.mult).then_inc(s_hyp, 1)
                dve.wait_ge(s_hyp, c.up())
                dve.tensor_scalar(tmp[:, :, :], tmp[:, :, :], 0.0, None, ALU.max).then_inc(s_hyp, 1)
                dve.wait_ge(s_hyp, c.up())
                dve.tensor_tensor(tmp[:, :, :], tmp[:, :, :], per_row(V[8]), ALU.mult).then_inc(s_hyp, 1)
                dve.wait_ge(s_hyp, c.up())
                assert c.k <= OSTEPS, c.k
                for _i in range(OSTEPS - c.k):
                    dve.sem_inc(s_hyp, 1)

            def turn(g, peeled):
                for q in range(G):
                    take_product((g + 2 * NG) * G + q, q)
                if not peeled:
                    operand(3, g - 1)
                dve.wait_ge(s_agg, (g + 2 * NG + 1) * G + 2)
                ball_out(g)
                c = Count(7 * NG + g)
                dve.tensor_tensor(xg[:, :, :], grp(X, g), tmp[:, :, :], ALU.add).then_inc(s_x, 1)
                dve.tensor_tensor(grp(X, g), grp(X, g), tmp[:, :, :], ALU.add).then_inc(s_post, 1)
                dve.wait_ge(s_post, c.up())
                normalise(3, g)
            turns(dve, turn)
            operand(3, NG - 1)

            def turn(g, peeled):
                for q in range(G):
                    take_product((g + 3 * NG) * G + q, q)
                dve.wait_ge(s_agg, (g + 3 * NG + 1) * G + 2)
                z = agg[:, :, 0:F]
                c = Count(8 * NG + g * 12)
                dve.tensor_tensor(tmp[:, :, :], z, per_row(grp(DINV, g)), ALU.mult).then_inc(s_post, 1)
                dve.wait_ge(s_post, c.up())
                dve.tensor_tensor(tmp[:, :, :], tmp[:, :, :], bias3("b31"), ALU.add).then_inc(s_post, 1)
                dve.wait_ge(s_post, c.up())
                dve.scalar_tensor_tensor(z, tmp[:, :, :], SLOPE, tmp[:, :, :], ALU.mult, ALU.max).then_inc(s_z, 1)
                dve.wait_ge(s_z, g + 1)
                for q in range(G):
                    dve.scalar_tensor_tensor(relu_junk[:, q, :], agg[:, q, 0:F], 1.0, agg[:, q, 0:F], ALU.mult,
                                             ALU.mult, accum_out=sqg[:, q:q + 1]).then_inc(s_post, 1)
                    dve.wait_ge(s_post, c.up())
                dve.tensor_copy(grp(SQ, g), sqg[:, :]).then_inc(s_post, 1)
                dve.wait_ge(s_post, c.up())
                dve.tensor_scalar(sqh[:, :], sqg[:, :], -0.5, None, ALU.mult).then_inc(s_post, 1)
                dve.wait_ge(s_post, c.up())
                dve.tensor_copy(sqp[:, :, 0], sqh[:, :]).then_inc(s_post, 1)
                dve.wait_ge(s_post, c.up())
                dve.tensor_tensor(sqr[:, :], sqh[:, :], sqp[:, :, 0], ALU.subtract).then_inc(s_post, 1)
                dve.wait_ge(s_post, c.up())
                dve.tensor_copy(sqp[:, :, 1], sqr[:, :]).then_inc(s_post, 1)
                dve.wait_ge(s_post, c.up())
                dve.tensor_tensor(sqp[:, :, 2], sqr[:, :], sqp[:, :, 1], ALU.subtract).then_inc(s_post, 1)
                dve.wait_ge(s_post, c.up())
                assert c.k == 12
                dve.sem_inc(s_sqp, 1)
                dve.wait_ge(s_zTp, g + 1)
                dve.wait_ge(s_sqTp, g + 1)
            turns(dve, turn)

            def turn(g, peeled):
                for q in range(G):
                    t = g * G + q
                    dve.wait_ge(s_keyrow, 8 * (t + 1) + 4)
                    dve.sem_inc(waited["dve"], 1)
                    dve.max(top_v[:, q, :], rows[:, q % 2, :]).then_inc(s_top, 1)
                    dve.wait_ge(s_top, t + 1)
                    dve.sem_inc(waited["dve"], 1)
                    dve.max_index(top_i[:, q, :], top_v[:, q, :], rows[:, q % 2, :]).then_inc(s_keyused, 1)
                dve.wait_ge(s_keyused, (g + 1) * G + 2)
                dve.tensor_copy(grp(TK, g), top_v[:, :, 0:TOP]).then_inc(s_topi, 1)
                dve.tensor_copy(grp(TI, g), top_i[:, :, 0:TOP]).then_inc(s_topi, 1)
                dve.wait_ge(s_topi, 2 * (g + 1))
            turns(dve, turn)

            sq_all = SQ[:, :].unsqueeze(2).to_broadcast([P, NT, TOP])
            dve.scalar_tensor_tensor(D2[:, :, :], TK[:, :, :], -2.0, sq_all, ALU.mult, ALU.add).then_inc(s_w, 1)
            dve.wait_ge(s_w, 1)
            dve.tensor_scalar(D2c[:, :, :], D2[:, :, :], 0.0, None, ALU.max).then_inc(s_w, 1)
            dve.wait_ge(s_exp, 1)
            dve.tensor_reduce(SSUM[:, :], S[:, :, :], axis=AX, op=ALU.add).then_inc(s_w, 1)
            dve.wait_ge(s_w, 3)
            dve.tensor_tensor(SDEG[:, :], SSUM[:, :], DEG[:, :], ALU.add).then_inc(s_w, 1)
            dve.wait_ge(s_sstd, 2)
            dve.reciprocal(D2INV[:, :], SSTD[:, :]).then_inc(s_w, 1)
            dve.wait_ge(s_w, 5)

            def turn(g, peeled):
                gsc_free(5, g)
                if not peeled:
                    dve.wait_ge(s_g2, 16 * g)
                dve.tensor_tensor(gsc[:, :, 0:F], grp(side, g), per_row(grp(D2INV, g)), ALU.mult).then_inc(s_gsc, 1)
            turns(dve, turn)

            def last(g, r, peeled):
                LS = 4 + 1 + G * (TOP - 1) + 1
                c = Count(g * 16)
                dve.tensor_copy(sg[:, :, :], grp(S, g)).then_inc(s_last, 1)
                dve.wait_ge(s_last, c.up())
                for q in range(G):
                    t = g * G + q
                    take_product((g + 4 * NG) * G + q, q)
                    dve.wait_ge(s_agg, (g + 4 * NG) * G + q + 3)
                    dve.wait_ge(s_gath[q % 2], 16 * LIST * NG * 2 + 16 * TOP * (g * 2 + q // 2 + 1))
                    for k in range(TOP - 1):
                        dve.scalar_tensor_tensor(agg[:, q, 0:F], gath[:, q % 2, k, :], sg[:, q, k:k + 1],
                                                 agg[:, q, 0:F], ALU.mult, ALU.add).then_inc(s_last, 1)
                        dve.wait_ge(s_last, c.up())
                    dve.scalar_tensor_tensor(agg[:, q, 0:F], gath[:, q % 2, TOP - 1, :], sg[:, q, TOP - 1:TOP],
                                             agg[:, q, 0:F], ALU.mult, ALU.add).then_inc(s_gath_used, 1)
                dve.wait_ge(s_gath_used, NT + (g + 1) * G + 2)
                dve.tensor_tensor(tmp[:, :, :], agg[:, :, 0:F], per_row(grp(D2INV, g)), ALU.mult).then_inc(s_last, 1)
                dve.wait_ge(s_last, c.up())
                dve.tensor_tensor(tmp[:, :, :], tmp[:, :, :], bias3("b32"), ALU.add).then_inc(s_last, 1)
                dve.wait_ge(s_last, c.up())
                if not peeled:
                    dve.wait_ge(s_out[r], 8 * (g - r))
                dve.tensor_tensor(fin[:, r, :, :], grp(X, g), tmp[:, :, :], ALU.add).then_inc(s_last, 1)
                dve.wait_ge(s_last, c.up())
                assert c.k == 16, c.k
                dve.sem_inc(s_fin, 1)
            last(0, 0, True)
            last(1, 1, True)
            with dve.Fori(1, NG // 2) as h:
                last(h * 2, 0, False)
                last(h * 2 + 1, 1, False)


_INS = ['x', 'adj', 'L0_gnn_weight', 'L0_gnn_bias', 'L1_gnn_weight', 'L2_gnn_W', 'L3_gnn_W1', 'L3_gnn_b1',
        'L3_gnn_W2', 'L3_gnn_b2']


def kernel(**inputs):
    import concourse.bacc as bacc
    from concourse.bass_utils import run_bass_kernel_spmd as run

    nc = bacc.Bacc("TRN2", target_bir_lowering=False, num_devices=1)
    arrays, args = {}, []
    for name in _INS:
        a = np.ascontiguousarray(inputs[name])
        arrays[f"in_{name}"] = a
        args.append(nc.dram_tensor(f"in_{name}", a.shape, mybir.dt.from_np(a.dtype), kind="ExternalInput").ap())
    out = nc.dram_tensor("out_x", inputs['x'].shape, F32, kind="ExternalOutput").ap()
    program(nc, *args, out)
    return run(nc, [arrays], core_ids=[0]).results[0]["out_x"]
```

```python
import numpy as np
import concourse.bass as bass
from concourse import mybir
from contextlib import ExitStack

F32, BF16, F8, I32, U32 = (mybir.dt.float32, mybir.dt.bfloat16, mybir.dt.float8e4, mybir.dt.int32,
                           mybir.dt.uint32)
ALU = mybir.AluOpType
ACT = mybir.ActivationFunctionType
AX = mybir.AxisListType.X
ts, ds = bass.ts, bass.ds

P = 128
G = 4
LN_EPS = 1e-5
BALL_EPS = 1e-5
MIN_NORM = 1e-15
MIN_DENOMINATOR = 1e-10
DISTANCE_EPS = 1e-10
SLOPE = 0.1
TOP = 4
LIST = 16
BASE = 8
MORE = (9, 10, 11, 12, 14, 16)
FLT_MAX = float(np.finfo(np.float32).max)
BALL_CLIP = float(np.float32(1.0) - np.float32(BALL_EPS))
ARTANH_CLIP = float(0.5 * np.log((1.0 + BALL_CLIP) / (1.0 - BALL_CLIP)))


def program(nc, x, adj, w0, b0, w1, w2, w31, b31, w32, b32, out):
    N, F = x.shape
    NT = N // P
    NG = NT // G
    FE = F + 1
    FW = 3 * FE
    BPB = 512 // P

    ctx = ExitStack()
    with ctx:
        def sb(name, shape, dt):
            return ctx.enter_context(nc.sbuf_tensor(name, shape, dt))

        def sem(name):
            return ctx.enter_context(nc.semaphore(name))

        adjT_dram = nc.dram_tensor("adjT_panels", (NT, P, NT * P // 2), BF16).ap()
        feat_dram = nc.dram_tensor("pool_features", (N + 1, F), F32).ap()
        g2_dram = nc.dram_tensor("last_features", (N, F), F32).ap()

        X = sb("X", [P, NT, F], F32)
        spare = sb("partsA", [P, NT * FW], BF16)
        partsA = spare[:, :].rearrange("p (t w) -> p t w", t=NT)
        partsB = sb("partsB", [P, NT, FW], BF16)
        side = sb("side", [P, NT, F], F32)
        rows = sb("rows", [P, 2, N], F32)
        panel = sb("panel", [P, G, NT, P], F8)
        first = sb("first", [P, 2, NT, P], F8)
        wide = sb("wide", [P, NT, F], F32)
        zT = wide[:, :, :].rearrange("p t f -> p (t f)")
        gath = sb("gath", [P, 2, LIST + 8, F], F32)
        gsc = sb("gsc", [P, G, FE], F32)
        rem = sb("rem", [P, G, FE], F32)
        agg = sb("agg", [P, G, FE], F32)
        xg = sb("xg", [P, G, F], F32)
        hn = sb("hn", [P, G, F], F32)
        hT = sb("hT", [P, G * P], F32)
        tmp = sb("tmp", [P, G, F], F32)
        st = sb("st", [P, G, nc.vector.BN_STATS_DIM], F32)
        mv = sb("mv", [P, G, nc.vector.BN_AGGR_DIM], F32)
        std = sb("std", [P, G], F32)
        rstd = sb("rstd", [P, G], F32)
        W = {k: sb(k, [P, F], F32) for k in ("W0", "W1a", "W1b", "W2", "W31", "W32")}
        B = {k: sb(k, [P, F], F32) for k in ("b0", "b31", "b32")}
        ident = sb("ident", [P, P], F32)
        identb = sb("identb", [P, P], BF16)
        tri = sb("tri", [P, P], BF16)
        diag_code = sb("diag_code", [P, P], BF16)
        code_row = sb("code_row", [P, P], F32)
        block_code = sb("block_code", [P, NT, 7], BF16)
        eps_ln = sb("eps_ln", [P, 1], F32)
        eps_dist = sb("eps_dist", [P, 1], F32)
        ones_col = sb("ones_col", [P, 1], F32)
        ones3 = sb("ones3", [3, P], BF16)
        zero_row = sb("zero_row", [1, F], F32)
        cand = sb("cand", [P, NT, 8], F32)
        relu_junk = cand[:, :, :].rearrange("p b k -> p (b k)").bitcast(BF16).rearrange("p (q f) -> p q f", q=G)
        rest = sb("rest", [P, NT * 7], F32)
        rest2 = sb("rest2", [P, NT * 7], F32)
        listed = sb("listed", [P, G, LIST], F32)
        found = sb("found", [P, G, NT + LIST], F32)
        IDX = sb("IDX", [P, NT, LIST], I32)
        idx_now = sb("idx_now", [P, 2, LIST], I32)
        DEG = sb("DEG", [P, NT], F32)
        FOUND = sb("FOUND", [P, NT], F32)
        missing = sb("missing", [P, NT], F32)
        missing_n = sb("missing_n", [P, 1], F32)
        LISTN = sb("LISTN", [P, NT], F32)
        list_idx = sb("list_idx", [P, G, LIST], I32)
        level = sb("level", [NT, 3, len(MORE)], F32)
        longest = sb("longest", [NT, 2], F32)
        upto = sb("upto", [NT, NT], F32)
        parity = sb("parity", [NT, NT], I32)
        control = sb("control", [1, 1 + 2 * NT], I32)
        NOROW = sb("NOROW", [P, NT], F32)
        DSTD = sb("DSTD", [P, NT], F32)
        DINV = sb("DINV", [P, NT], F32)
        general_mask, general_cap = hT[:, 0:64], hT[:, 64:128]
        general_new, general_acc = hn[:, 0, :], hn[:, 1, :]
        ss = sb("ss", [P, 2, G], F32)
        nn = sb("nn", [P, 2, G], F32)
        v = [sb(f"v{i}", [P, G], F32) for i in range(16)]
        SQ = sb("SQ", [P, NT], F32)
        sqg = sb("sqg", [P, G], F32)
        sqh = sb("sqh", [P, G], F32)
        sqr = sb("sqr", [P, G], F32)
        sqp = sb("sqp", [P, G, 3], BF16)
        SQT = first[0:3, :, :, :].bitcast(BF16).rearrange("p a b i -> p (a b i)")
        D2 = rest[:, 0:NT * TOP].rearrange("p (t k) -> p t k", k=TOP)
        D2c = rest2[:, 0:NT * TOP].rearrange("p (t k) -> p t k", k=TOP)
        DR = cand[:, :, 0:TOP]
        at = 4 * P + 4 * G * F
        TK, TI, S = (spare[:, at + k * 2 * NT * TOP:at + (k + 1) * 2 * NT * TOP].bitcast(dt)
                     .rearrange("p (t k) -> p t k", k=TOP) for k, dt in ((0, F32), (1, I32), (2, F32)))
        at += 6 * NT * TOP
        top_v, top_i = (spare[:, at + k * 16 * G:at + (k + 1) * 16 * G].bitcast(dt)
                        .rearrange("p (q k) -> p q k", k=8) for k, dt in ((0, F32), (1, U32)))
        zs = spare[:, 0:4 * P].bitcast(F32).rearrange("p (r c) -> p r c", r=2)
        fin = spare[:, 4 * P:4 * P + 4 * G * F].bitcast(F32).rearrange("p (r q f) -> p r q f", r=2, q=G)
        SSUM = sb("SSUM", [P, NT], F32)
        SDEG = sb("SDEG", [P, NT], F32)
        SSTD = sb("SSTD", [P, NT], F32)
        D2INV = sb("D2INV", [P, NT], F32)
        sg = sb("sg", [P, G, TOP], F32)

        bank = [ctx.enter_context(nc.psum_tensor(f"bank{i}", [P, 512], F32)) for i in range(8)]
        psT, psW, psV = bank[6], bank[7], bank[5]
        sq_junk = bank[4][:, :].rearrange("p (q f) -> p q f", q=G)

        s_loaded = sem("inputs_loaded")
        s_const = sem("constants_ready")
        s_x = sem("x_group_ready")
        s_stats = sem("stats_ready")
        s_mv = sem("mean_var_ready")
        s_std = sem("std_ready")
        s_rstd = sem("rstd_ready")
        s_norm = sem("norm_ready")
        s_hTp = sem("hT_in_psum")
        s_hT = sem("hT_ready")
        s_hw = sem("hw_in_psum")
        s_side = sem("side_ready")
        s_gsc = sem("operand_ready")
        s_p0 = sem("part0_ready")
        s_rem = sem("remainder_ready")
        s_p1 = sem("part1_ready")
        s_parts = sem("parts_ready")
        s_rows = [sem(f"adj_rows_loaded{i}") for i in range(2)]
        s_tr = sem("blocks_transposed")
        s_panel = sem("panel_chunk_ready")
        s_stored = [sem(f"panel_stored{i}") for i in range(G)]
        s_code = sem("codes_in_psum")
        s_code_used = sem("codes_used")
        s_list = sem("list_chain")
        s_prod = sem("product_in_psum")
        s_agg = sem("product_taken")
        s_lprod = sem("layer_product_in_psum")
        s_sum = sem("layer_product_taken")
        s_post = sem("post_chain")
        s_feat = sem("features_stored")
        s_deg = sem("degree_chain")
        s_found = sem("lists_counted")
        s_upto = sem("slot_sums_ready")
        s_counted = sem("list_counts_ready")
        s_list_idx = sem("list_indices_chain")
        s_listT = sem("list_counts_transposed")
        s_long = sem("longest_chain")
        s_missing = sem("control_in_psum")
        s_flag = sem("flag_ready")
        s_gen_m = sem("general_mask_loaded")
        s_gen_f = sem("general_features_loaded")
        s_gen_used = sem("general_chunk_used")
        s_gen = sem("general_chain")
        s_load = [sem(f"panel_loaded{i}") for i in range(G)]
        s_tri = sem("first_codes_in_psum")
        s_first = sem("first_chunk_ready")
        s_fp = sem("first_features_in_psum")
        s_fp_used = sem("first_features_taken")
        s_idx = sem("indices_staged")
        s_gath = [sem(f"rows_gathered{i}") for i in range(2)]
        s_gath2 = [sem(f"nearest_gathered{i}") for i in range(2)]
        s_gath_used = sem("gathered_used")
        s_max = sem("maxima_taken")
        s_y = sem("pooled_ready")
        s_hyp = sem("ball_chain")
        s_ssm = sem("mx_squares_ready")
        s_ssh = sem("h_squares_ready")
        s_nn = sem("norms_ready")
        s_ratio = sem("ln_argument_ready")
        s_ln = sem("ln_ready")
        s_targ = sem("tanh_argument_ready")
        s_tanh = sem("tanh_ready")
        s_z = sem("z_ready")
        s_zTp = sem("zT_in_psum")
        s_zT = sem("zT_ready")
        s_sqp = sem("square_parts_ready")
        s_sqTp = sem("squares_in_psum")
        s_sqT = sem("squares_row_ready")
        s_zs = sem("z_tile_staged")
        s_key = sem("keys_in_psum")
        s_keyrow = sem("key_chunk_ready")
        s_keyused = sem("key_row_used")
        s_top = sem("top_chain")
        s_topi = sem("top_lists_ready")
        s_w = sem("weights_chain")
        s_sqrt = sem("distances_ready")
        s_exp = sem("similarities_ready")
        s_sstd = sem("second_std_ready")
        s_g2 = sem("last_features_stored")
        s_fin = sem("output_ready")
        s_out = [sem(f"output_stored{i}") for i in range(2)]
        s_last = sem("last_chain")
        waited = {k: sem(f"{k}_has_waited") for k in ("pe", "act", "dve", "pool")}

        block = ctx.enter_context(nc.Block())

        class Count:
            def __init__(self, base):
                self.base, self.k = base, 0

            def up(self):
                self.k += 1
                return self.base + self.k

        parts_of = {0: partsA, 1: partsB, 2: partsA, 3: partsB, 4: partsA, 5: partsB}
        SPLIT_OF_PREP = {0: 0, 1: 2, 2: 3, 3: 4}

        def part(u, g, k):
            return parts_of[u][:, ds(g * G, G), k * FE:(k + 1) * FE]

        def grp(t, g):
            return t[:, ds(g * G, G)]

        def turns(eng, body, first=0):
            body(first, True)
            with eng.Fori(first + 1, NG) as g:
                body(g, False)

        @block.sync
        def _(sp):
            n = 0
            loads = [(W["W0"], w0), (W["W1a"], w1[0:F, :]), (W["W1b"], w1[F:2 * F, :]), (W["W2"], w2),
                     (W["W31"], w31), (W["W32"], w32)]
            sp.dma_start(X[:, :, :], x.rearrange("(t p) f -> p t f", p=P)).then_inc(s_loaded, 16)
            for t, a in loads:
                sp.dma_start(t[:, :], a).then_inc(s_loaded, 16)
            for k, a in (("b0", b0), ("b31", b31), ("b32", b32)):
                sp.dma_start(B[k][:, :], a.partition_broadcast(P)).then_inc(s_loaded, 16)
            sp.wait_ge(s_const, 1)
            sp.dma_start(feat_dram[N:N + 1, :], zero_row[:, :]).then_inc(s_loaded, 16)

            def load_rows(g, q, peeled):
                t = g * G + q
                if not (peeled and q < 2):
                    sp.wait_ge(s_tr, 4 * (t - 1))
                sp.dma_start(rows[:, q % 2, :], adj[ts(t, P), :]).then_inc(s_rows[q % 2], 16)

            def store_panel(g, q):
                t = g * G + q
                sp.wait_ge(s_panel, 4 * (t + 1) + 2)
                sp.dma_start(adjT_dram[ds(t, 1), :, :].rearrange("a p n -> p (a n)"),
                             panel[:, q, :, :].rearrange("p b i -> p (b i)").bitcast(BF16)).then_inc(s_stored[q], 16)

            def turn(g, peeled):
                for q in range(G):
                    load_rows(g, q, peeled)
                    if not (peeled and q == 0):
                        if q:
                            store_panel(g, q - 1)
                        else:
                            store_panel(g - 1, G - 1)
            turns(sp, turn)
            store_panel(NG - 1, G - 1)
            for q in range(G):
                sp.wait_ge(s_stored[q], 16 * NG)

            sp.wait_ge(s_feat, 16 * NG)
            sp.wait_ge(s_flag, 1)
            short = sp.value_load(control[0:1, 0:1], min_val=0, max_val=1 << 24)
            with sp.If(short > 0):
                with sp.Fori(0, NT) as t:
                    with sp.Fori(0, N // 64) as c:
                        m = t * (N // 64) + c
                        sp.wait_ge(s_gen_used, m + 1)
                        sp.dma_start(general_mask[:, :], adj[ts(t, P), ts(c, 64)]).then_inc(s_gen_m, 16)
                        sp.dma_start(rows[:, :, :].rearrange("p a n -> p (a n)"),
                                     feat_dram[ts(c, 64), :].rearrange("j f -> (j f)").partition_broadcast(P)
                                     ).then_inc(s_gen_f, 16)

            def load_panel(g, q):
                sp.dma_start(panel[:, q, :, :].rearrange("p b i -> p (b i)").bitcast(BF16),
                             adjT_dram[ds(g * G + q, 1), :, :].rearrange("a p n -> p (a n)")
                             ).then_inc(s_load[q], 16)

            def turn(g, peeled):
                for q in range(G):
                    if not peeled:
                        sp.wait_ge(s_tri, 8 * (g * G + q - G + 1))
                    load_panel(g, q)
            turns(sp, turn)
            for ps in range(1, 5):
                def turn(g, peeled):
                    for q in range(G):
                        if peeled and ps == 1:
                            sp.wait_ge(s_tri, 8 * (NT - G + q + 1))
                        else:
                            sp.wait_ge(s_lprod, (g + (ps - 1) * NG) * G + q - G + 1)
                        load_panel(g, q)
                turns(sp, turn)
            sp.wait_ge(s_g2, 16 * NG)

        @block.tensor
        def _(pe):
            pe.wait_ge(s_const, 8)
            pe.wait_ge(s_loaded, 16 * 11)

            def aux(s, g):
                n, m = g + s * NG, g + SPLIT_OF_PREP[s] * NG
                pe.wait_ge(s_norm, n + 1)
                for q in range(G):
                    i = pe.transpose(psT[:, q * P:(q + 1) * P], hn[:, q, :], ident[:, :])
                i.then_inc(s_hTp, 1)
                pe.wait_ge(s_hT, n + 1)
                pe.wait_ge(s_gsc, m + 1)
                ws = {0: ["W0"], 1: ["W1b", "W1a"], 2: ["W2"], 3: ["W31", "W32"]}[s]
                for w, o in zip(ws, (psW, psV)):
                    if o is psV:
                        pe.wait_ge(s_side, (g + (0 if s == 1 else NG)) + 1)
                    for q in range(G):
                        i = pe.matmul(o[:, q * P:(q + 1) * P], hT[:, q * P:(q + 1) * P], W[w][:, :],
                                      start=True, stop=True)
                i.then_inc(s_hw, 1)

            turns(pe, lambda g, peeled: aux(0, g))

            def transposes(g, q, c):
                if c == 0:
                    pe.wait_ge(s_rows[q % 2], 16 * (g * 2 + q // 2 + 1))
                rb = rows[:, q % 2, :].bitcast(BF16).rearrange("p (n two) -> p n two", two=2)
                pe.wait_ge(s_panel, 4 * (g * G + q) + c + 1)
                o = bank[2 + c % 2][:, :].bitcast(BF16)
                for b in range(8):
                    j = c * 8 + b
                    i = pe.transpose(o[:, b * P:(b + 1) * P], rb[:, j * P:(j + 1) * P, 1], identb[:, :])
                i.then_inc(s_tr, 1)

            def product_chunk(g, q, c, wait_parts):
                t = g * G + q
                if wait_parts:
                    pe.wait_ge(s_parts, c + 1)
                if c == 0:
                    pe.wait_ge(s_agg, t + 1)
                pe.wait_ge(s_panel, 4 * t + c // 2 + 3)
                pe.wait_ge(s_code_used, 8 * t + c + 1)
                pe.sem_inc(waited["pe"], 1)
                for b in range(BPB):
                    j = c * BPB + b
                    i = pe.matmul(bank[q % 2][:, 0:FW], panel[:, q, j, :], parts_of[0][:, j, :],
                                  start=(j == 0), stop=(j == NT - 1))
                if c == NT // BPB - 1:
                    i.then_inc(s_prod, 1)
                for b in range(BPB):
                    i = pe.matmul(bank[4 + c % 4][:, b * P:(b + 1) * P], panel[:, q, c * BPB + b, :],
                                  diag_code[:, :], start=True, stop=True)
                i.then_inc(s_code, 1)

            def turn(g, peeled):
                for q in range(G):
                    before = (g, q - 1) if q else (g - 1, G - 1)
                    for c in range(NT // BPB):
                        if c % 2 == 0:
                            transposes(g, q, c // 2)
                        if not (peeled and q == 0):
                            product_chunk(*before, c, peeled and q == 1)
            turns(pe, turn)
            for c in range(NT // BPB):
                product_chunk(NG - 1, G - 1, c, False)
            pe.wait_ge(s_code_used, 8 * NT + 4)

            pe.wait_ge(s_counted, 2 * NG)
            pe.transpose(psW[0:NT, 0:P], LISTN[:, :], ident[:, :]).then_inc(s_listT, 1)
            pe.wait_ge(s_deg, 3)
            pe.wait_ge(s_long, 5)
            pe.wait_ge(s_upto, 3)
            pe.matmul(psT[0:1, 0:1], missing_n[:, 0:1], ones_col[:, 0:1], start=True, stop=True)
            pe.matmul(psT[0:1, 1:1 + NT], longest[:, 0:1], ident[0:NT, 0:NT], start=True, stop=True)
            pe.matmul(psT[0:1, 1 + NT:1 + 2 * NT], longest[:, 1:2], upto[:, :], start=True, stop=True
                      ).then_inc(s_missing, 1)

            pparts = parts_of[1]

            def firsts(g, q, peeled):
                t = g * G + q
                pe.wait_ge(s_load[q], 16 * (g + 1))

                def tri_chunk(c):
                    pe.wait_ge(s_first, 8 * t + c + 1)
                    pe.sem_inc(waited["pe"], 1)
                    i = pe.matmul(bank[2 + c % 2][:, :], tri[:, :],
                                  panel[:, q, c * BPB:(c + 1) * BPB, :].rearrange("p b i -> p (b i)"),
                                  start=True, stop=True)
                    i.then_inc(s_tri, 1)

                tri_chunk(0)
                tri_chunk(1)
                for c in range(NT // BPB):
                    pe.wait_ge(s_first, 8 * t + c + 3)
                    pe.wait_ge(s_fp_used, 8 * t + c + 1)
                    pe.sem_inc(waited["pe"], 1)
                    for b in range(BPB):
                        j = c * BPB + b
                        for k in range(3):
                            i = pe.matmul(bank[c % 2][:, b * P:(b + 1) * P], first[:, q % 2, j, :],
                                          pparts[:, j, k * FE:k * FE + F], start=(k == 0), stop=(k == 2))
                    i.then_inc(s_fp, 1)
                    if c + 2 < NT // BPB:
                        tri_chunk(c + 2)

            def pool_turn(g, peeled):
                for q in range(G):
                    firsts(g, q, peeled)
                if not peeled:
                    aux(1, g - 1)
            pe.wait_ge(s_parts, 2 * NG)
            turns(pe, pool_turn)
            aux(1, NG - 1)

            def product(u, g, q, ps, first_group):
                T = (g + (ps - 1) * NG) * G + q
                pe.wait_ge(s_load[q], 16 * (g + ps * NG + 1))
                pe.wait_ge(s_sum, T + 1)
                pe.sem_inc(waited["pe"], 1)
                for j in range(NT):
                    if first_group and q == 0 and j % G == 0:
                        pe.wait_ge(s_parts, u * NG + j // G + 1)
                    i = pe.matmul(bank[q][:, 0:FW], panel[:, q, j, :], parts_of[u][:, j, :],
                                  start=(j == 0), stop=(j == NT - 1))
                i.then_inc(s_lprod, 1)

            def layer(u, ps, s):
                def turn(g, peeled):
                    for q in range(G):
                        product(u, g, q, ps, peeled)
                    if not peeled and s is not None:
                        aux(s, g - 1)
                turns(pe, turn)
                if s is not None:
                    aux(s, NG - 1)

            pe.wait_ge(s_fp_used, 8 * NT + 2)
            pe.wait_ge(s_first, 8 * NT + 2)
            layer(2, 1, 2)
            layer(3, 2, 3)

            def z_aux(g, peeled):
                if not peeled:
                    pe.wait_ge(s_zT, g)
                    pe.wait_ge(s_sqT, g)
                pe.wait_ge(s_z, g + 1)
                for q in range(G):
                    i = pe.transpose(psT[:, q * P:(q + 1) * P], xg[:, q, :], ident[:, :])
                i.then_inc(s_zTp, 1)
                pe.wait_ge(s_sqp, g + 1)
                for q in range(G):
                    i = pe.transpose(psW[0:3, :].bitcast(BF16)[:, q * P:(q + 1) * P], sqp[:, q, :], identb[:, :])
                i.then_inc(s_sqTp, 1)

            for q in range(G):
                product(4, 0, q, 3, True)
            for q in range(G):
                product(4, 1, q, 3, False)
            z_aux(0, True)
            with pe.Fori(2, NG) as g:
                for q in range(G):
                    product(4, g, q, 3, False)
                z_aux(g - 1, False)
            z_aux(NG - 1, False)

            pe.wait_ge(s_zT, NG)
            pe.wait_ge(s_sqT, NG)
            pe.wait_ge(s_sum, 3 * NT + 4)

            def keys(g, peeled):
                for q in range(G):
                    t = g * G + q
                    pe.wait_ge(s_zs, t + 1)
                    for c in range(8):
                        pe.wait_ge(s_keyrow, 8 * t + c + 1)
                        o = bank[c]
                        pe.matmul(o[:, :], zs[:, q % 2, :], zT[:, c * 512:(c + 1) * 512], start=True, stop=False)
                        pe.matmul(o[:, :], ones3[:, :], SQT[:, c * 512:(c + 1) * 512], start=False, stop=True
                                  ).then_inc(s_key, 1)
            with pe.Fori(0, NG) as g:
                keys(g, False)
            pe.wait_ge(s_keyrow, 8 * NT + 8)
            layer(5, 4, None)

        @block.scalar
        def _(act):
            act.wait_ge(s_const, 8)
            for s, k in ((s_panel, 2), (s_first, 2), (s_side, 1), (s_keyrow, 8)):
                act.sem_inc(s, k)

            def std_of(s, g):
                n = g + s * NG
                act.wait_ge(s_mv, n + 1)
                act.activation(std[:, :], mv[:, :, 1], ACT.Sqrt, bias=eps_ln[:, 0:1]).then_inc(s_std, 1)

            def hT_of(s, g):
                act.wait_ge(s_hTp, g + s * NG + 1)
                act.activation(hT[:, :], psT[:, :], ACT.Relu).then_inc(s_hT, 1)

            def side_of(s, g):
                act.wait_ge(s_hw, g + s * NG + 1)
                act.copy(grp(side, g), psV[:, :].rearrange("p (q f) -> p q f", q=G)).then_inc(s_side, 1)

            def split(u, g):
                m = g + u * NG
                act.wait_ge(s_gsc, m + 2)
                act.copy(part(u, g, 0), gsc[:, :, :]).then_inc(s_p0, 1)
                act.wait_ge(s_rem, m + 2)
                act.copy(part(u, g, 1), rem[:, :, :]).then_inc(s_p1, 1)

            def turn(g, peeled):
                std_of(0, g)
                hT_of(0, g)
                if not peeled:
                    split(0, g - 1)
            turns(act, turn)
            split(0, NG - 1)

            def evac_panel(g, q, first_group):
                t = g * G + q
                if not first_group:
                    act.wait_ge(s_stored[q], 16 * g)
                    act.wait_ge(s_code, 8 * (t - G + 1))
                for c in range(4):
                    act.wait_ge(s_tr, 4 * t + c + 1)
                    act.sem_inc(waited["act"], 1)
                    act.activation(panel[:, q, c * 8:(c + 1) * 8, :].rearrange("p b i -> p (b i)"),
                                   bank[2 + c % 2][:, :].bitcast(BF16), ACT.Copy, saturate=False
                                   ).then_inc(s_panel, 1)

            def feat_store(g):
                act.wait_ge(s_post, 2 * (g + 1))
                act.dma_start(feat_dram[ds(g * G * P, G * P), :].rearrange("(t p) f -> p t f", p=P),
                              gsc[:, :, 0:F]).then_inc(s_feat, 16)

            def turn(g, peeled):
                for q in range(G):
                    evac_panel(g, q, peeled)
                    if q == 2 and not peeled:
                        feat_store(g - 1)
                        split(1, g - 1)
            turns(act, turn)
            feat_store(NG - 1)
            split(1, NG - 1)

            act.wait_ge(s_deg, 3)
            act.activation(DSTD[:, :], DEG[:, :], ACT.Sqrt).then_inc(s_sstd, 1)

            def firsts(g, q):
                t = g * G + q
                for c in range(8):
                    act.wait_ge(s_tri, 8 * t + c + 1)
                    act.sem_inc(waited["act"], 1)
                    act.activation(first[:, q % 2, c * BPB:(c + 1) * BPB, :].rearrange("p b i -> p (b i)"),
                                   bank[2 + c % 2][:, :], ACT.Relu, saturate=False).then_inc(s_first, 1)

            def after(u, s, g, more=None):
                hT_of(s, g)
                if s in (1, 3):
                    side_of(s, g)
                if more:
                    more(g)
                split(u, g)

            def turn(g, peeled):
                for q in range(G):
                    firsts(g, q)
                if not peeled:
                    after(2, 1, g - 1)
                std_of(1, g)
            turns(act, turn)
            after(2, 1, NG - 1)

            def ball_in(g):
                act.wait_ge(s_hw, g + 2 * NG + 1)
                for q in range(G):
                    i = act.activation(sq_junk[:, q, :], psW[:, q * P:(q + 1) * P], ACT.Square,
                                       accum_out=ss[:, 1, q:q + 1])
                i.then_inc(s_ssm, 1)
                act.wait_ge(s_ssm, g + 1)
                act.wait_ge(s_ssh, g + 1)
                act.activation(nn[:, :, :], ss[:, :, :], ACT.Sqrt).then_inc(s_nn, 1)
                act.wait_ge(s_ratio, g + 1)
                act.activation(v[3][:, :], v[2][:, :], ACT.Ln).then_inc(s_ln, 1)
                act.wait_ge(s_targ, g + 1)
                act.activation(v[5][:, :], v[4][:, :], ACT.Tanh).then_inc(s_tanh, 1)

            def turn(g, peeled):
                if not peeled:
                    after(3, 2, g - 1, ball_in)
                std_of(2, g)
            turns(act, turn)
            after(3, 2, NG - 1, ball_in)

            def ball_out(g):
                act.wait_ge(s_ssm, NG + g + 1)
                act.activation(nn[:, :, :], ss[:, :, :], ACT.Sqrt).then_inc(s_nn, 1)
                act.wait_ge(s_ratio, NG + g + 1)
                act.activation(v[3][:, :], v[2][:, :], ACT.Ln).then_inc(s_ln, 1)
                act.wait_ge(s_targ, NG + g + 1)
                act.activation(v[5][:, :], v[4][:, :], ACT.Tanh).then_inc(s_tanh, 1)

            def turn(g, peeled):
                if not peeled:
                    after(4, 3, g - 1)
                ball_out(g)
                std_of(3, g)
            turns(act, turn)
            after(4, 3, NG - 1)

            with act.Fori(0, NG) as g:
                act.wait_ge(s_zTp, g + 1)
                act.copy(zT[:, ds(g * G * P, G * P)], psT[:, :]).then_inc(s_zT, 1)
                act.wait_ge(s_sqTp, g + 1)
                act.copy(SQT[:, ds(g * G * P, G * P)], psW[0:3, :].bitcast(BF16)[:, 0:G * P]).then_inc(s_sqT, 1)

            act.wait_ge(s_zT, NG)
            def turn(g, peeled):
                for q in range(G):
                    t = g * G + q
                    if not (peeled and q < 2):
                        act.wait_ge(s_key, 8 * (t - 1))
                    act.copy(zs[:, q % 2, :], zT[:, ts(t, P)]).then_inc(s_zs, 1)
                    act.wait_ge(s_keyused, t + 1)
                    for c in range(8):
                        act.wait_ge(s_key, 8 * t + c + 1)
                        act.copy(rows[:, q % 2, c * 512:(c + 1) * 512], bank[c][:, :]).then_inc(s_keyrow, 1)
            turns(act, turn)

            act.wait_ge(s_w, 2)
            act.activation(DR[:, :, :], D2c[:, :, :], ACT.Sqrt, bias=eps_dist[:, 0:1]).then_inc(s_sqrt, 1)
            act.wait_ge(s_sqrt, 1)
            act.activation(S[:, :, :], DR[:, :, :], ACT.Exp, scale=-0.5).then_inc(s_exp, 1)
            act.wait_ge(s_w, 4)
            act.activation(SSTD[:, :], SDEG[:, :], ACT.Sqrt).then_inc(s_sstd, 1)

            with act.Fori(0, NG) as g:
                act.wait_ge(s_gsc, g + 5 * NG + 2)
                act.dma_start(g2_dram[ds(g * G * P, G * P), :].rearrange("(t p) f -> p t f", p=P),
                              gsc[:, :, 0:F]).then_inc(s_g2, 16)
                split(5, g)
                act.wait_ge(s_g2, 16 * (g + 1))

            with act.Fori(0, NG // 2) as h:
                for r in range(2):
                    g = h * 2 + r
                    act.wait_ge(s_fin, g + 1)
                    act.dma_start(out[ds(g * G * P, G * P), :].rearrange("(t p) f -> p t f", p=P),
                                 fin[:, r, :, :]).then_inc(s_out[r], 16)
            for r in range(2):
                act.wait_ge(s_out[r], 16 * (NG // 2))

        @block.gpsimd
        def _(pool):
            pool.memset(zero_row[:, :], 0.0).then_inc(s_const, 1)
            pool.memset(ident[:, :], 0.0).then_inc(s_const, 1)
            pool.wait_ge(s_const, 2)
            pool.affine_select(out=ident[:, :], in_=ident[:, :], compare_op=ALU.not_equal, fill=1.0, base=0,
                               pattern=[[-1, P]], channel_multiplier=1).then_inc(s_const, 1)
            pool.iota(code_row[:, :], pattern=[[-1, P]], base=P, channel_multiplier=0,
                      allow_small_or_imprecise_dtypes=True)
            pool.iota(block_code[:, :, :], pattern=[[-P, NT], [0, 7]], base=N - P, channel_multiplier=0,
                      allow_small_or_imprecise_dtypes=True)
            pool.iota(parity[:, :], pattern=[[1, NT]], base=0, channel_multiplier=1)
            pool.memset(eps_ln[:, :], LN_EPS)
            pool.memset(eps_dist[:, :], DISTANCE_EPS)
            pool.memset(ones_col[:, :], 1.0)
            pool.memset(ones3[:, :], 1.0)
            pool.memset(gsc[:, :, F:FE], 1.0)
            pool.memset(wide[:, :, :], 0.0).then_inc(s_const, 1)
            pool.wait_ge(s_const, 4)
            pool.tensor_copy(identb[:, :], ident[:, :]).then_inc(s_const, 1)
            pool.tensor_tensor(diag_code[:, :], ident[:, :], code_row[:, :], ALU.mult).then_inc(s_const, 1)
            pool.affine_select(out=tri[:, :], in_=ident[:, :], compare_op=ALU.is_ge, fill=-1.0, base=0,
                               pattern=[[-1, P]], channel_multiplier=1).then_inc(s_const, 1)
            pool.sem_inc(s_rem, 1)
            pool.sem_inc(s_found, 1)
            for k, (k0, k1) in enumerate(zip((BASE,) + MORE, MORE)):
                pool.memset(level[:, 0, k:k + 1], float(k0))
                pool.memset(level[:, 1, k:k + 1], float(k1 - k0))
            pool.memset(gath[:, :, BASE:LIST, :], 0.0).then_inc(s_const, 1)

            def split(u, g):
                m = g + u * NG
                pool.wait_ge(s_p0, m + 1)
                pool.tensor_tensor(rem[:, :, :], gsc[:, :, :], part(u, g, 0), ALU.subtract).then_inc(s_rem, 1)
                pool.wait_ge(s_p1, m + 1)
                pool.tensor_tensor(part(u, g, 2), rem[:, :, :], part(u, g, 1), ALU.subtract).then_inc(s_parts, 1)
                pool.wait_ge(s_parts, m + 1)

            pool.wait_ge(s_upto, 2)
            pool.affine_select(out=upto[:, :], in_=upto[:, :], compare_op=ALU.is_ge, fill=0.0, base=0,
                               pattern=[[1, NT]], channel_multiplier=-1).then_inc(s_upto, 1)
            with pool.Fori(0, NG) as g:
                split(0, g)
            def count_lists(g, q):
                t = g * G + q
                pool.wait_ge(s_list, 5 * (t + 1))
                pool.sem_inc(waited["pool"], 1)
                pool.tensor_scalar(found[:, q, 0:NT], cand[:, :, 0], 0.0, None, ALU.is_gt)
                pool.tensor_scalar(found[:, q, NT:NT + LIST], listed[:, q, :], 0.0, None, ALU.is_gt).then_inc(s_found, 1)

            def turn(g, peeled):
                if not peeled:
                    pool.wait_ge(s_counted, 2 * g)
                for q in range(G):
                    count_lists(g, q)
                    if q == 1 and not peeled:
                        split(1, g - 1)
                pool.tensor_scalar(list_idx[:, :, :], listed[:, :, :], -1.0, float(N), ALU.mult, ALU.add
                                   ).then_inc(s_list_idx, 1)
                pool.wait_ge(s_list_idx, 2 * g + 1)
                pool.tensor_copy(grp(IDX, g), list_idx[:, :, :]).then_inc(s_list_idx, 1)
                pool.wait_ge(s_list_idx, 2 * g + 2)
            turns(pool, turn)
            split(1, NG - 1)

            pool.wait_ge(s_feat, 16 * NG)
            pool.wait_ge(s_loaded, 16 * 11)
            pool.wait_ge(s_flag, 1)

            def gathers(g, q):
                t = g * G + q
                pool.wait_ge(s_gath_used, t + 1)
                pool.tensor_copy(idx_now[:, q % 2, :], IDX[:, ds(t, 1), :].rearrange("p a k -> p (a k)")
                                 ).then_inc(s_idx, 1)
                pool.wait_ge(s_idx, t + 1)
                pool.sem_inc(waited["pool"], 1)
                for k in range(BASE):
                    pool.indirect_dma_start(gath[:, q % 2, k, :], None, feat_dram,
                                            bass.IndirectOffsetOnAxis(idx_now[:, q % 2, k:k + 1], axis=0)
                                            ).then_inc(s_gath[q % 2], 16)
                longest_list = pool.value_load(control[0:1, ds(t + 1, 1)], min_val=0, max_val=LIST)
                for k0, k1 in zip((BASE,) + MORE, MORE):
                    with pool.If(longest_list > k0):
                        for k in range(k0, k1):
                            pool.indirect_dma_start(gath[:, q % 2, k, :], None, feat_dram,
                                                    bass.IndirectOffsetOnAxis(idx_now[:, q % 2, k:k + 1], axis=0)
                                                    ).then_inc(s_gath[q % 2], 16)

            def turn(g, peeled):
                for q in range(G):
                    gathers(g, q)
                if not peeled:
                    split(2, g - 1)
            turns(pool, turn)
            split(2, NG - 1)
            for u in (3, 4):
                with pool.Fori(0, NG) as g:
                    split(u, g)
            with pool.Fori(0, NG) as g:
                split(5, g)

            pool.wait_ge(s_g2, 16 * NG)

            def last_gathers(g, q):
                t = NT + g * G + q
                pool.wait_ge(s_gath_used, t + 1)
                pool.tensor_copy(idx_now[:, q % 2, 0:TOP], TI[:, ds(g * G + q, 1), :].rearrange("p a k -> p (a k)")
                                 ).then_inc(s_idx, 1)
                pool.wait_ge(s_idx, t + 1)
                pool.sem_inc(waited["pool"], 1)
                for k in range(TOP):
                    pool.indirect_dma_start(gath[:, q % 2, k, :], None, g2_dram,
                                            bass.IndirectOffsetOnAxis(idx_now[:, q % 2, k:k + 1], axis=0)
                                            ).then_inc(s_gath2[q % 2], 16)
            with pool.Fori(0, NG) as g:
                for q in range(G):
                    last_gathers(g, q)

        @block.vector
        def _(dve):
            V = [t[:, :] for t in v]
            dve.wait_ge(s_const, 8)
            dve.wait_ge(s_loaded, 16 * 11)
            for s, k in ((s_gsc, 1), (s_agg, 2), (s_sum, 4), (s_code_used, 4), (s_fp_used, 2), (s_gath_used, 2),
                         (s_keyused, 2), (s_gen_used, 1)):
                dve.sem_inc(s, k)

            dve.tensor_scalar(parity[:, :], parity[:, :], 1, None, ALU.bitwise_and).then_inc(s_upto, 1)
            dve.wait_ge(s_upto, 1)
            dve.tensor_scalar(upto[:, :], parity[:, :], -16.0, 16.0, ALU.mult, ALU.add).then_inc(s_upto, 1)

            def per_row(t2, width=F):
                return t2.unsqueeze(2).to_broadcast([P, G, width])

            def bias3(k):
                return B[k][:, :].unsqueeze(1).to_broadcast([P, G, F])

            def normalise(s, g):
                n = g + s * NG
                dve.wait_ge(s_x, n + 1)
                for q in range(G):
                    i = dve.bn_stats(st[:, q, :], xg[:, q, :])
                i.then_inc(s_stats, 1)
                dve.wait_ge(s_stats, n + 1)
                dve.sem_inc(waited["dve"], 1)
                for q in range(G):
                    i = dve.bn_aggr(mv[:, q, :], st[:, q, :])
                i.then_inc(s_mv, 1)
                dve.wait_ge(s_std, n + 1)
                dve.reciprocal(rstd[:, :], std[:, :]).then_inc(s_rstd, 1)
                dve.wait_ge(s_rstd, n + 1)
                for q in range(G):
                    i = dve.tensor_scalar(hn[:, q, :], xg[:, q, :], mv[:, q, 0:1], rstd[:, q:q + 1],
                                          ALU.subtract, ALU.mult)
                i.then_inc(s_norm, 1)

            def gsc_free(u, g):
                dve.wait_ge(s_rem, g + u * NG + 1)

            def operand(s, g):
                u = SPLIT_OF_PREP[s]
                dve.wait_ge(s_hw, g + s * NG + 1)
                gsc_free(u, g)
                ps = psW[:, :].rearrange("p (q f) -> p q f", q=G)
                if s == 3:
                    dve.tensor_tensor(gsc[:, :, 0:F], ps, per_row(grp(DINV, g)), ALU.mult).then_inc(s_gsc, 1)
                else:
                    dve.tensor_copy(gsc[:, :, 0:F], ps).then_inc(s_gsc, 1)

            def turn(g, peeled):
                if not peeled:
                    dve.wait_ge(s_norm, g)
                    dve.wait_ge(s_hTp, g)
                dve.tensor_copy(xg[:, :, :], grp(X, g)).then_inc(s_x, 1)
                normalise(0, g)
                if not peeled:
                    operand(0, g - 1)
            turns(dve, turn)
            operand(0, NG - 1)

            def take_product(T, q):
                dve.wait_ge(s_lprod, T + 1)
                dve.tensor_reduce(agg[:, q, :], bank[q][:, 0:FW].rearrange("p (k f) -> p f k", k=3),
                                  axis=AX, op=ALU.add).then_inc(s_sum, 1)

            LSTEPS = 5

            def lists(g, q):
                t = g * G + q
                c = Count(t * LSTEPS)
                dve.wait_ge(s_found, t + 1)
                for ch in range(NT // BPB):
                    dve.wait_ge(s_code, 8 * t + ch + 1)
                    dve.sem_inc(waited["dve"], 1)
                    for b in range(BPB):
                        i = dve.max(cand[:, ch * BPB + b, :], bank[4 + ch % 4][:, b * P:(b + 1) * P])
                    i.then_inc(s_code_used, 1)
                dve.wait_ge(s_prod, t + 1)
                dve.tensor_reduce(agg[:, q, :], bank[q % 2][:, 0:FW].rearrange("p (k f) -> p f k", k=3),
                                  axis=AX, op=ALU.add).then_inc(s_agg, 1)
                dve.wait_ge(s_code_used, 8 * (t + 1) + 4)
                r3 = rest[:, :].rearrange("p (b k) -> p b k", k=7)
                dve.scalar_tensor_tensor(r3, cand[:, :, 1:8], 0.0, block_code[:, :, :], ALU.is_gt, ALU.mult
                                         ).then_inc(s_list, 1)
                dve.wait_ge(s_list, c.up())
                dve.tensor_tensor(r3, r3, cand[:, :, 1:8], ALU.add).then_inc(s_list, 1)
                dve.wait_ge(s_list, c.up())
                dve.sem_inc(waited["dve"], 1)
                dve.max(listed[:, q, 0:8], rest[:, :]).then_inc(s_list, 1)
                dve.wait_ge(s_list, c.up())
                dve.scalar_tensor_tensor(rest2[:, :], rest[:, :], listed[:, q, 7:8], rest[:, :],
                                         ALU.is_lt, ALU.mult).then_inc(s_list, 1)
                dve.wait_ge(s_list, c.up())
                dve.sem_inc(waited["dve"], 1)
                dve.max(listed[:, q, 8:16], rest2[:, :]).then_inc(s_list, 1)

            def layer0_out(g):
                dve.wait_ge(s_agg, (g + 1) * G + 2)
                dve.tensor_copy(grp(DEG, g), agg[:, :, F]).then_inc(s_y, 1)
                gsc_free(1, g)
                if isinstance(g, int) and g == 0:
                    pass
                else:
                    dve.wait_ge(s_feat, 16 * g)
                dve.tensor_tensor(tmp[:, :, :], agg[:, :, 0:F], bias3("b0"), ALU.add).then_inc(s_post, 1)
                dve.wait_ge(s_post, 2 * g + 1)
                dve.wait_ge(s_y, g + 1)
                dve.tensor_scalar(gsc[:, :, 0:F], tmp[:, :, :], 0.0, None, ALU.max).then_inc(s_post, 1)
                dve.wait_ge(s_post, 2 * g + 2)
                dve.sem_inc(s_gsc, 1)

            def turn(g, peeled):
                if not peeled:
                    dve.wait_ge(s_list_idx, 2 * g)
                for q in range(G):
                    lists(g, q)
                layer0_out(g)
                dve.wait_ge(s_found, (g + 1) * G + 1)
                dve.sem_inc(waited["dve"], 1)
                dve.tensor_reduce(grp(FOUND, g), found[:, :, :], axis=AX, op=ALU.add).then_inc(s_counted, 1)
                dve.tensor_reduce(grp(LISTN, g), found[:, :, NT:NT + LIST], axis=AX, op=ALU.add
                                  ).then_inc(s_counted, 1)
            turns(dve, turn)

            dve.wait_ge(s_y, NG)
            dve.wait_ge(s_counted, 2 * NG)
            dve.wait_ge(s_listT, 1)
            dve.tensor_reduce(longest[:, 0:1], psW[0:NT, 0:P], axis=AX, op=ALU.max).then_inc(s_long, 1)
            dve.wait_ge(s_long, 1)
            dve.tensor_tensor(level[:, 2, :], longest[:, 0:1].to_broadcast([NT, len(MORE)]), level[:, 0, :],
                              ALU.is_gt).then_inc(s_long, 1)
            dve.wait_ge(s_long, 2)
            dve.tensor_tensor(level[:, 2, :], level[:, 2, :], level[:, 1, :], ALU.mult).then_inc(s_long, 1)
            dve.wait_ge(s_long, 3)
            dve.tensor_reduce(longest[:, 1:2], level[:, 2, :], axis=AX, op=ALU.add).then_inc(s_long, 1)
            dve.wait_ge(s_long, 4)
            dve.tensor_scalar(longest[:, 1:2], longest[:, 1:2], float(BASE), None, ALU.add).then_inc(s_long, 1)
            dve.tensor_tensor(missing[:, :], DEG[:, :], FOUND[:, :], ALU.subtract).then_inc(s_deg, 1)
            dve.tensor_scalar(NOROW[:, :], DEG[:, :], 0.0, -FLT_MAX, ALU.is_equal, ALU.mult).then_inc(s_deg, 1)
            dve.wait_ge(s_deg, 2)
            dve.tensor_reduce(missing_n[:, :], missing[:, :], axis=AX, op=ALU.add).then_inc(s_deg, 1)
            dve.wait_ge(s_sstd, 1)
            dve.reciprocal(DINV[:, :], DSTD[:, :]).then_inc(s_deg, 1)
            dve.wait_ge(s_missing, 1)
            dve.tensor_copy(control[:, :], psT[0:1, 0:1 + 2 * NT]).then_inc(s_flag, 1)
            dve.wait_ge(s_flag, 1)
            short = dve.value_load(control[0:1, 0:1], min_val=0, max_val=1 << 24)
            with dve.If(short > 0):
                CH = N // 64
                feats = rows[:, :, :].rearrange("p a (j f) -> p (a j) f", f=F)
                with dve.Fori(0, NT) as t:
                    dve.memset(general_acc[:, :], 0.0).then_inc(s_gen, 1)
                    with dve.Fori(0, CH) as c:
                        m = t * CH + c
                        k = t * (4 * CH + 2) + c * 4 + 1
                        dve.wait_ge(s_gen, k)
                        dve.wait_ge(s_gen_m, 16 * (m + 1))
                        dve.tensor_scalar(general_cap[:, :], general_mask[:, :], 0.0, FLT_MAX, ALU.not_equal,
                                          ALU.mult).then_inc(s_gen, 1)
                        dve.wait_ge(s_gen, k + 1)
                        dve.wait_ge(s_gen_f, 16 * (m + 1))
                        dve.tensor_tensor(feats, feats, general_cap[:, :].unsqueeze(2).to_broadcast([P, 64, F]),
                                          ALU.min).then_inc(s_gen, 1)
                        dve.wait_ge(s_gen, k + 2)
                        dve.tensor_reduce(general_new[:, :], feats.rearrange("p j f -> p f j"), axis=AX,
                                          op=ALU.max).then_inc(s_gen, 1)
                        dve.wait_ge(s_gen, k + 3)
                        dve.tensor_tensor(general_acc[:, :], general_acc[:, :], general_new[:, :], ALU.max
                                          ).then_inc(s_gen, 1)
                        dve.wait_ge(s_gen, k + 4)
                        dve.sem_inc(s_gen_used, 1)
                    dve.tensor_copy(wide[:, ds(t, 1), :].rearrange("p a f -> p (a f)"), general_acc[:, :]
                                    ).then_inc(s_gen, 1)
                    dve.wait_ge(s_gen, (t + 1) * (4 * CH + 2))

            dve.wait_ge(s_deg, 4)
            dve.wait_ge(s_feat, 16 * NG)

            def pooled(g, q):
                t = g * G + q
                for c in range(8):
                    dve.wait_ge(s_fp, 8 * t + c + 1)
                    dve.tensor_reduce(gath[:, q % 2, LIST + c, :],
                                      bank[c % 2][:, :].rearrange("p (b f) -> p f b", b=BPB),
                                      axis=AX, op=ALU.max).then_inc(s_fp_used, 1)
                dve.wait_ge(s_fp_used, 8 * (t + 1) + 2)
                gathered = dve.value_load(control[0:1, ds(t + 1 + NT, 1)], min_val=16 * BASE, max_val=16 * LIST * NT)
                dve.wait_ge(s_gath[q % 2], gathered)
                dve.tensor_reduce(tmp[:, q, :], gath[:, q % 2, :, :].rearrange("p k f -> p f k"), axis=AX,
                                  op=ALU.max).then_inc(s_max, 1)
                dve.wait_ge(s_max, t + 1)
                dve.memset(gath[:, q % 2, BASE:LIST, :], 0.0).then_inc(s_gath_used, 1)

            def turn(g, peeled):
                for q in range(G):
                    pooled(g, q)
                if not peeled:
                    operand(1, g - 1)
                c = Count(2 * NG + g * 3)
                dve.wait_ge(s_gath_used, (g + 1) * G + 2)
                dve.tensor_tensor(tmp[:, :, :], tmp[:, :, :], grp(wide, g), ALU.max).then_inc(s_post, 1)
                dve.wait_ge(s_post, c.up())
                dve.tensor_tensor(tmp[:, :, :], tmp[:, :, :], per_row(grp(NOROW, g)), ALU.add).then_inc(s_post, 1)
                dve.wait_ge(s_post, c.up())
                dve.tensor_tensor(xg[:, :, :], grp(X, g), tmp[:, :, :], ALU.add).then_inc(s_x, 1)
                dve.tensor_tensor(grp(X, g), grp(X, g), tmp[:, :, :], ALU.add).then_inc(s_post, 1)
                dve.wait_ge(s_post, c.up())
                normalise(1, g)
            turns(dve, turn)
            operand(1, NG - 1)

            def half_square(g):
                for q in range(G):
                    i = dve.scalar_tensor_tensor(relu_junk[:, q, :], hn[:, q, :], 0.0, hn[:, q, :], ALU.max, ALU.mult,
                                                 accum_out=ss[:, 0, q:q + 1])
                i.then_inc(s_ssh, 1)

            ASTEPS = 17

            def artanh(c, x_, s_base):
                t_, t2 = V[0], V[1]
                dve.tensor_scalar(t_, x_, BALL_CLIP, None, ALU.min).then_inc(s_hyp, 1)
                dve.wait_ge(s_hyp, c.up())
                dve.tensor_scalar(V[7], t_, -1.0, 1.0, ALU.mult, ALU.add).then_inc(s_hyp, 1)
                dve.wait_ge(s_hyp, c.up())
                dve.reciprocal(V[8], V[7]).then_inc(s_hyp, 1)
                dve.wait_ge(s_hyp, c.up())
                dve.scalar_tensor_tensor(V[2], t_, 1.0, V[8], ALU.add, ALU.mult).then_inc(s_ratio, 1)
                dve.tensor_tensor(t2, t_, t_, ALU.mult).then_inc(s_hyp, 1)
                dve.wait_ge(s_hyp, c.up())
                dve.tensor_scalar(V[9], t2, 1.0 / 11, None, ALU.mult).then_inc(s_hyp, 1)
                dve.wait_ge(s_hyp, c.up())
                for k in (9, 7, 5, 3):
                    dve.scalar_tensor_tensor(V[9], V[9], 1.0 / k, t2, ALU.add, ALU.mult).then_inc(s_hyp, 1)
                    dve.wait_ge(s_hyp, c.up())
                dve.scalar_tensor_tensor(V[9], V[9], 1.0, t_, ALU.add, ALU.mult).then_inc(s_hyp, 1)
                dve.wait_ge(s_hyp, c.up())
                dve.tensor_scalar(V[10], t_, 0.25, None, ALU.is_lt).then_inc(s_hyp, 1)
                dve.wait_ge(s_hyp, c.up())
                dve.wait_ge(s_ln, s_base + 1)
                dve.tensor_scalar(V[11], V[3], 0.5, None, ALU.mult).then_inc(s_hyp, 1)
                dve.wait_ge(s_hyp, c.up())
                dve.tensor_tensor(V[12], V[9], V[11], ALU.subtract).then_inc(s_hyp, 1)
                dve.wait_ge(s_hyp, c.up())
                dve.tensor_tensor(V[12], V[12], V[10], ALU.mult).then_inc(s_hyp, 1)
                dve.wait_ge(s_hyp, c.up())
                dve.tensor_tensor(V[6], V[12], V[11], ALU.add).then_inc(s_hyp, 1)
                dve.wait_ge(s_hyp, c.up())

            ISTEPS = 26

            def operand_ball(g):
                c = Count(g * ISTEPS)
                gsc_free(3, g)
                dve.wait_ge(s_nn, g + 1)
                dve.tensor_scalar(nn[:, :, :], nn[:, :, :], MIN_NORM, None, ALU.max).then_inc(s_hyp, 1)
                dve.wait_ge(s_hyp, c.up())
                artanh(c, nn[:, 0, :], g)
                dve.reciprocal(V[13], nn[:, 0, :]).then_inc(s_hyp, 1)
                dve.wait_ge(s_hyp, c.up())
                dve.reciprocal(V[14], nn[:, 1, :]).then_inc(s_hyp, 1)
                dve.wait_ge(s_hyp, c.up())
                dve.tensor_tensor(V[13], V[13], nn[:, 1, :], ALU.mult).then_inc(s_hyp, 1)
                dve.wait_ge(s_hyp, c.up())
                dve.tensor_tensor(V[4], V[13], V[6], ALU.mult).then_inc(s_targ, 1)
                dve.wait_ge(s_tanh, g + 1)
                dve.tensor_tensor(V[7], V[5], V[5], ALU.mult).then_inc(s_hyp, 1)
                dve.wait_ge(s_hyp, c.up())
                dve.tensor_scalar(V[7], V[7], -1.0, 1.0, ALU.mult, ALU.add).then_inc(s_hyp, 1)
                dve.wait_ge(s_hyp, c.up())
                dve.tensor_scalar(V[7], V[7], BALL_EPS, 0.5, ALU.max, ALU.mult).then_inc(s_hyp, 1)
                dve.wait_ge(s_hyp, c.up())
                dve.reciprocal(V[8], V[7]).then_inc(s_hyp, 1)
                dve.wait_ge(s_hyp, c.up())
                dve.tensor_scalar(gsc[:, :, F], V[8], 1.0, None, ALU.subtract).then_inc(s_hyp, 1)
                dve.wait_ge(s_hyp, c.up())
                dve.tensor_tensor(V[9], V[8], V[5], ALU.mult).then_inc(s_hyp, 1)
                dve.wait_ge(s_hyp, c.up())
                dve.tensor_tensor(V[9], V[9], V[14], ALU.mult).then_inc(s_hyp, 1)
                dve.wait_ge(s_hyp, c.up())
                assert c.k <= ISTEPS, c.k
                for _i in range(ISTEPS - c.k):
                    dve.sem_inc(s_hyp, 1)
                dve.tensor_tensor(gsc[:, :, 0:F], psW[:, :].rearrange("p (q f) -> p q f", q=G), per_row(V[9]),
                                  ALU.mult).then_inc(s_gsc, 1)
                dve.wait_ge(s_gsc, g + 3 * NG + 2)

            def turn(g, peeled):
                for q in range(G):
                    take_product(g * G + q, q)
                if not peeled:
                    operand_ball(g - 1)
                c = Count(5 * NG + g * 2)
                dve.wait_ge(s_sum, (g + 1) * G + 4)
                dve.wait_ge(s_side, g + 2)
                dve.tensor_tensor(tmp[:, :, :], agg[:, :, 0:F], grp(side, g), ALU.add).then_inc(s_post, 1)
                dve.wait_ge(s_post, c.up())
                dve.tensor_tensor(xg[:, :, :], grp(X, g), tmp[:, :, :], ALU.add).then_inc(s_x, 1)
                dve.tensor_tensor(grp(X, g), grp(X, g), tmp[:, :, :], ALU.add).then_inc(s_post, 1)
                dve.wait_ge(s_post, c.up())
                normalise(2, g)
                dve.wait_ge(s_norm, g + 2 * NG + 1)
                half_square(g)
            turns(dve, turn)
            operand_ball(NG - 1)

            OSTEPS = 40

            def ball_out(g):
                c = Count(NG * ISTEPS + g * OSTEPS)
                dve.tensor_scalar(V[15], agg[:, :, F], MIN_DENOMINATOR, None, ALU.max).then_inc(s_hyp, 1)
                dve.wait_ge(s_hyp, c.up())
                dve.reciprocal(V[15], V[15]).then_inc(s_hyp, 1)
                dve.wait_ge(s_hyp, c.up())
                dve.tensor_tensor(tmp[:, :, :], agg[:, :, 0:F], per_row(V[15]), ALU.mult).then_inc(s_hyp, 1)
                dve.wait_ge(s_hyp, c.up())
                for q in range(G):
                    dve.scalar_tensor_tensor(relu_junk[:, q, :], tmp[:, q, :], 1.0, tmp[:, q, :], ALU.mult, ALU.mult,
                                             accum_out=ss[:, 0, q:q + 1]).then_inc(s_hyp, 1)
                    dve.wait_ge(s_hyp, c.up())
                    dve.scalar_tensor_tensor(relu_junk[:, q, :], tmp[:, q, :], 0.0, tmp[:, q, :], ALU.max, ALU.mult,
                                             accum_out=ss[:, 1, q:q + 1]).then_inc(s_hyp, 1)
                    dve.wait_ge(s_hyp, c.up())
                dve.sem_inc(s_ssm, 1)
                dve.wait_ge(s_nn, NG + g + 1)
                dve.tensor_scalar(V[13], nn[:, 0, :], MIN_NORM, None, ALU.max).then_inc(s_hyp, 1)
                dve.wait_ge(s_hyp, c.up())
                artanh(c, V[13], NG + g)
                dve.reciprocal(V[13], V[13]).then_inc(s_hyp, 1)
                dve.wait_ge(s_hyp, c.up())
                dve.tensor_tensor(V[6], V[6], grp(DEG, g), ALU.mult).then_inc(s_hyp, 1)
                dve.wait_ge(s_hyp, c.up())
                dve.tensor_scalar(V[6], V[6], 0.5, ARTANH_CLIP, ALU.mult, ALU.min).then_inc(s_hyp, 1)
                dve.wait_ge(s_hyp, c.up())
                dve.tensor_tensor(V[14], V[6], V[13], ALU.mult).then_inc(s_hyp, 1)
                dve.wait_ge(s_hyp, c.up())
                dve.tensor_tensor(V[4], V[14], nn[:, 1, :], ALU.mult).then_inc(s_targ, 1)
                dve.wait_ge(s_targ, NG + g + 1)
                dve.tensor_scalar(V[7], V[4], MIN_NORM, None, ALU.max).then_inc(s_hyp, 1)
                dve.wait_ge(s_hyp, c.up())
                dve.reciprocal(V[8], V[7]).then_inc(s_hyp, 1)
                dve.wait_ge(s_hyp, c.up())
                dve.tensor_tensor(V[8], V[8], V[14], ALU.mult).then_inc(s_hyp, 1)
                dve.wait_ge(s_hyp, c.up())
                dve.wait_ge(s_tanh, NG + g + 1)
                dve.tensor_tensor(V[8], V[8], V[5], ALU.mult).then_inc(s_hyp, 1)
                dve.wait_ge(s_hyp, c.up())
                dve.tensor_scalar(tmp[:, :, :], tmp[:, :, :], 0.0, None, ALU.max).then_inc(s_hyp, 1)
                dve.wait_ge(s_hyp, c.up())
                dve.tensor_tensor(tmp[:, :, :], tmp[:, :, :], per_row(V[8]), ALU.mult).then_inc(s_hyp, 1)
                dve.wait_ge(s_hyp, c.up())
                assert c.k <= OSTEPS, c.k
                for _i in range(OSTEPS - c.k):
                    dve.sem_inc(s_hyp, 1)

            def turn(g, peeled):
                for q in range(G):
                    take_product((g + NG) * G + q, q)
                if not peeled:
                    operand(3, g - 1)
                dve.wait_ge(s_sum, (g + NG + 1) * G + 4)
                ball_out(g)
                c = Count(7 * NG + g)
                dve.tensor_tensor(xg[:, :, :], grp(X, g), tmp[:, :, :], ALU.add).then_inc(s_x, 1)
                dve.tensor_tensor(grp(X, g), grp(X, g), tmp[:, :, :], ALU.add).then_inc(s_post, 1)
                dve.wait_ge(s_post, c.up())
                normalise(3, g)
            turns(dve, turn)
            operand(3, NG - 1)

            def turn(g, peeled):
                for q in range(G):
                    take_product((g + 2 * NG) * G + q, q)
                dve.wait_ge(s_sum, (g + 2 * NG + 1) * G + 4)
                if not peeled:
                    dve.wait_ge(s_zTp, g)
                    dve.wait_ge(s_sqTp, g)
                c = Count(8 * NG + g * 12)
                dve.tensor_tensor(tmp[:, :, :], agg[:, :, 0:F], per_row(grp(DINV, g)), ALU.mult).then_inc(s_post, 1)
                dve.wait_ge(s_post, c.up())
                dve.tensor_tensor(tmp[:, :, :], tmp[:, :, :], bias3("b31"), ALU.add).then_inc(s_post, 1)
                dve.wait_ge(s_post, c.up())
                dve.scalar_tensor_tensor(xg[:, :, :], tmp[:, :, :], SLOPE, tmp[:, :, :], ALU.mult, ALU.max).then_inc(s_z, 1)
                dve.wait_ge(s_z, g + 1)
                for q in range(G):
                    dve.scalar_tensor_tensor(relu_junk[:, q, :], xg[:, q, :], 1.0, xg[:, q, :], ALU.mult,
                                             ALU.mult, accum_out=sqg[:, q:q + 1]).then_inc(s_post, 1)
                    dve.wait_ge(s_post, c.up())
                dve.tensor_copy(grp(SQ, g), sqg[:, :]).then_inc(s_post, 1)
                dve.wait_ge(s_post, c.up())
                dve.tensor_scalar(sqh[:, :], sqg[:, :], -0.5, None, ALU.mult).then_inc(s_post, 1)
                dve.wait_ge(s_post, c.up())
                dve.tensor_copy(sqp[:, :, 0], sqh[:, :]).then_inc(s_post, 1)
                dve.wait_ge(s_post, c.up())
                dve.tensor_tensor(sqr[:, :], sqh[:, :], sqp[:, :, 0], ALU.subtract).then_inc(s_post, 1)
                dve.wait_ge(s_post, c.up())
                dve.tensor_copy(sqp[:, :, 1], sqr[:, :]).then_inc(s_post, 1)
                dve.wait_ge(s_post, c.up())
                dve.tensor_tensor(sqp[:, :, 2], sqr[:, :], sqp[:, :, 1], ALU.subtract).then_inc(s_post, 1)
                dve.wait_ge(s_post, c.up())
                assert c.k == 12
                dve.sem_inc(s_sqp, 1)
            turns(dve, turn)

            def turn(g, peeled):
                for q in range(G):
                    t = g * G + q
                    dve.wait_ge(s_keyrow, 8 * (t + 1) + 8)
                    dve.sem_inc(waited["dve"], 1)
                    dve.max(top_v[:, q, :], rows[:, q % 2, :]).then_inc(s_top, 1)
                    dve.wait_ge(s_top, t + 1)
                    dve.sem_inc(waited["dve"], 1)
                    dve.max_index(top_i[:, q, :], top_v[:, q, :], rows[:, q % 2, :]).then_inc(s_keyused, 1)
                dve.wait_ge(s_keyused, (g + 1) * G + 2)
                dve.tensor_copy(grp(TK, g), top_v[:, :, 0:TOP]).then_inc(s_topi, 1)
                dve.tensor_copy(grp(TI, g), top_i[:, :, 0:TOP]).then_inc(s_topi, 1)
                dve.wait_ge(s_topi, 2 * (g + 1))
            turns(dve, turn)

            sq_all = SQ[:, :].unsqueeze(2).to_broadcast([P, NT, TOP])
            dve.scalar_tensor_tensor(D2[:, :, :], TK[:, :, :], -2.0, sq_all, ALU.mult, ALU.add).then_inc(s_w, 1)
            dve.wait_ge(s_w, 1)
            dve.tensor_scalar(D2c[:, :, :], D2[:, :, :], 0.0, None, ALU.max).then_inc(s_w, 1)
            dve.wait_ge(s_exp, 1)
            dve.tensor_reduce(SSUM[:, :], S[:, :, :], axis=AX, op=ALU.add).then_inc(s_w, 1)
            dve.wait_ge(s_w, 3)
            dve.tensor_tensor(SDEG[:, :], SSUM[:, :], DEG[:, :], ALU.add).then_inc(s_w, 1)
            dve.wait_ge(s_sstd, 2)
            dve.reciprocal(D2INV[:, :], SSTD[:, :]).then_inc(s_w, 1)
            dve.wait_ge(s_w, 5)

            def turn(g, peeled):
                gsc_free(5, g)
                if not peeled:
                    dve.wait_ge(s_g2, 16 * g)
                dve.tensor_tensor(gsc[:, :, 0:F], grp(side, g), per_row(grp(D2INV, g)), ALU.mult).then_inc(s_gsc, 1)
            turns(dve, turn)

            def last(g, r, peeled):
                LS = 4 + 1 + G * (TOP - 1) + 1
                c = Count(g * 16)
                dve.tensor_copy(sg[:, :, :], grp(S, g)).then_inc(s_last, 1)
                dve.wait_ge(s_last, c.up())
                for q in range(G):
                    t = g * G + q
                    take_product((g + 3 * NG) * G + q, q)
                    dve.wait_ge(s_sum, (g + 3 * NG) * G + q + 5)
                    dve.wait_ge(s_gath2[q % 2], 16 * TOP * (g * 2 + q // 2 + 1))
                    for k in range(TOP - 1):
                        dve.scalar_tensor_tensor(agg[:, q, 0:F], gath[:, q % 2, k, :], sg[:, q, k:k + 1],
                                                 agg[:, q, 0:F], ALU.mult, ALU.add).then_inc(s_last, 1)
                        dve.wait_ge(s_last, c.up())
                    dve.scalar_tensor_tensor(agg[:, q, 0:F], gath[:, q % 2, TOP - 1, :], sg[:, q, TOP - 1:TOP],
                                             agg[:, q, 0:F], ALU.mult, ALU.add).then_inc(s_gath_used, 1)
                dve.wait_ge(s_gath_used, NT + (g + 1) * G + 2)
                dve.tensor_tensor(tmp[:, :, :], agg[:, :, 0:F], per_row(grp(D2INV, g)), ALU.mult).then_inc(s_last, 1)
                dve.wait_ge(s_last, c.up())
                dve.tensor_tensor(tmp[:, :, :], tmp[:, :, :], bias3("b32"), ALU.add).then_inc(s_last, 1)
                dve.wait_ge(s_last, c.up())
                if not peeled:
                    dve.wait_ge(s_out[r], 8 * (g - r))
                dve.tensor_tensor(fin[:, r, :, :], grp(X, g), tmp[:, :, :], ALU.add).then_inc(s_last, 1)
                dve.wait_ge(s_last, c.up())
                assert c.k == 16, c.k
                dve.sem_inc(s_fin, 1)
            last(0, 0, True)
            last(1, 1, True)
            with dve.Fori(1, NG // 2) as h:
                last(h * 2, 0, False)
                last(h * 2 + 1, 1, False)


_INS = ['x', 'adj', 'L0_gnn_weight', 'L0_gnn_bias', 'L1_gnn_weight', 'L2_gnn_W', 'L3_gnn_W1', 'L3_gnn_b1',
        'L3_gnn_W2', 'L3_gnn_b2']


def kernel(**inputs):
    import concourse.bacc as bacc
    from concourse.bass_utils import run_bass_kernel_spmd as run

    nc = bacc.Bacc("TRN2", target_bir_lowering=False, num_devices=1)
    arrays, args = {}, []
    for name in _INS:
        a = np.ascontiguousarray(inputs[name])
        arrays[f"in_{name}"] = a
        args.append(nc.dram_tensor(f"in_{name}", a.shape, mybir.dt.from_np(a.dtype), kind="ExternalInput").ap())
    out = nc.dram_tensor("out_x", inputs['x'].shape, F32, kind="ExternalOutput").ap()
    program(nc, *args, out)
    return run(nc, [arrays], core_ids=[0]).results[0]["out_x"]
```

```python
import numpy as np
import concourse.bass as bass
from concourse import mybir
from contextlib import ExitStack

F32, BF16, F8, I32, U32 = (mybir.dt.float32, mybir.dt.bfloat16, mybir.dt.float8e4, mybir.dt.int32,
                           mybir.dt.uint32)
ALU = mybir.AluOpType
ACT = mybir.ActivationFunctionType
AX = mybir.AxisListType.X
ts, ds = bass.ts, bass.ds

P = 128
G = 4
LN_EPS = 1e-5
BALL_EPS = 1e-5
MIN_NORM = 1e-15
MIN_DENOMINATOR = 1e-10
DISTANCE_EPS = 1e-10
SLOPE = 0.1
TOP = 4
LIST = 16
BASE = 8
MORE = (9, 10, 11, 12, 13, 14, 16)
FLT_MAX = float(np.finfo(np.float32).max)
BALL_CLIP = float(np.float32(1.0) - np.float32(BALL_EPS))
ARTANH_CLIP = float(0.5 * np.log((1.0 + BALL_CLIP) / (1.0 - BALL_CLIP)))


def program(nc, x, adj, w0, b0, w1, w2, w31, b31, w32, b32, out):
    N, F = x.shape
    NT = N // P
    NG = NT // G
    FE = F + 1
    FW = 3 * FE
    BPB = 512 // P

    ctx = ExitStack()
    with ctx:
        def sb(name, shape, dt):
            return ctx.enter_context(nc.sbuf_tensor(name, shape, dt))

        def sem(name):
            return ctx.enter_context(nc.semaphore(name))

        adjT_dram = nc.dram_tensor("adjT_panels", (NT, P, NT * P // 2), BF16).ap()
        feat_dram = nc.dram_tensor("pool_features", (N + 1, F), F32).ap()
        g2_dram = nc.dram_tensor("last_features", (N, F), F32).ap()

        X = sb("X", [P, NT, F], F32)
        spare = sb("partsA", [P, NT * FW], BF16)
        partsA = spare[:, :].rearrange("p (t w) -> p t w", t=NT)
        partsB = sb("partsB", [P, NT, FW], BF16)
        side = sb("side", [P, NT, F], F32)
        rows = sb("rows", [P, 2, N], F32)
        panel = sb("panel", [P, G, NT, P], F8)
        first = sb("first", [P, 2, NT, P], F8)
        wide = sb("wide", [P, NT, F], F32)
        zT = wide[:, :, :].rearrange("p t f -> p (t f)")
        gath = sb("gath", [P, 2, LIST + 8, F], F32)
        gsc = sb("gsc", [P, G, FE], F32)
        rem = sb("rem", [P, G, FE], F32)
        agg = sb("agg", [P, G, FE], F32)
        xg = sb("xg", [P, G, F], F32)
        hn = sb("hn", [P, G, F], F32)
        hT = sb("hT", [P, G * P], F32)
        tmp = sb("tmp", [P, G, F], F32)
        st = sb("st", [P, G, nc.vector.BN_STATS_DIM], F32)
        mv = sb("mv", [P, G, nc.vector.BN_AGGR_DIM], F32)
        std = sb("std", [P, G], F32)
        rstd = sb("rstd", [P, G], F32)
        W = {k: sb(k, [P, F], F32) for k in ("W0", "W1a", "W1b", "W2", "W31", "W32")}
        B = {k: sb(k, [P, F], F32) for k in ("b0", "b31", "b32")}
        ident = sb("ident", [P, P], F32)
        identb = sb("identb", [P, P], BF16)
        tri = sb("tri", [P, P], BF16)
        diag_code = sb("diag_code", [P, P], BF16)
        code_row = sb("code_row", [P, P], F32)
        block_code = sb("block_code", [P, NT, 7], BF16)
        eps_ln = sb("eps_ln", [P, 1], F32)
        eps_dist = sb("eps_dist", [P, 1], F32)
        ones_col = sb("ones_col", [P, 1], F32)
        ones3 = sb("ones3", [3, P], BF16)
        zero_row = sb("zero_row", [1, F], F32)
        cand = sb("cand", [P, NT, 8], F32)
        relu_junk = cand[:, :, :].rearrange("p b k -> p (b k)").bitcast(BF16).rearrange("p (q f) -> p q f", q=G)
        rest = sb("rest", [P, NT * 7], F32)
        rest2 = sb("rest2", [P, NT * 7], F32)
        listed = sb("listed", [P, G, LIST], F32)
        found = sb("found", [P, G, NT + LIST], F32)
        IDX = sb("IDX", [P, NT, LIST], I32)
        idx_now = sb("idx_now", [P, 2, LIST], I32)
        DEG = sb("DEG", [P, NT], F32)
        FOUND = sb("FOUND", [P, NT], F32)
        missing = sb("missing", [P, NT], F32)
        missing_n = sb("missing_n", [P, 1], F32)
        LISTN = sb("LISTN", [P, NT], F32)
        list_idx = sb("list_idx", [P, G, LIST], I32)
        level = sb("level", [NT, 3, len(MORE)], F32)
        longest = sb("longest", [NT, 2], F32)
        upto = sb("upto", [NT, NT], F32)
        parity = sb("parity", [NT, NT], I32)
        control = sb("control", [1, 1 + 2 * NT], I32)
        NOROW = sb("NOROW", [P, NT], F32)
        DSTD = sb("DSTD", [P, NT], F32)
        DINV = sb("DINV", [P, NT], F32)
        general_mask, general_cap = hT[:, 0:64], hT[:, 64:128]
        general_new, general_acc = hn[:, 0, :], hn[:, 1, :]
        ss = sb("ss", [P, 2, G], F32)
        nn = sb("nn", [P, 2, G], F32)
        v = [sb(f"v{i}", [P, G], F32) for i in range(16)]
        SQ = sb("SQ", [P, NT], F32)
        sqg = sb("sqg", [P, G], F32)
        sqh = sb("sqh", [P, G], F32)
        sqr = sb("sqr", [P, G], F32)
        sqp = sb("sqp", [P, G, 3], BF16)
        SQT = first[0:3, :, :, :].bitcast(BF16).rearrange("p a b i -> p (a b i)")
        d2, d2c, dist, simil = (sb(k, [P, G, TOP], F32) for k in ("d2", "d2_floored", "dist", "simil"))
        ssum, sdeg, sstd, sinv = (sb(k, [P, G], F32) for k in ("sim_sum", "second_degree", "second_std", "second_inv"))
        at = 4 * P + 4 * G * F
        TI, S = (spare[:, at + k * 2 * NT * TOP:at + (k + 1) * 2 * NT * TOP].bitcast(dt)
                     .rearrange("p (t k) -> p t k", k=TOP) for k, dt in ((0, I32), (1, F32)))
        at += 6 * NT * TOP
        top_v, top_i = (spare[:, at + k * 16 * G:at + (k + 1) * 16 * G].bitcast(dt)
                        .rearrange("p (q k) -> p q k", k=8) for k, dt in ((0, F32), (1, U32)))
        zs = spare[:, 0:4 * P].bitcast(F32).rearrange("p (r c) -> p r c", r=2)
        fin = spare[:, 4 * P:4 * P + 4 * G * F].bitcast(F32).rearrange("p (r q f) -> p r q f", r=2, q=G)
        D2INV = sb("D2INV", [P, NT], F32)
        sg = sb("sg", [P, G, TOP], F32)

        bank = [ctx.enter_context(nc.psum_tensor(f"bank{i}", [P, 512], F32)) for i in range(8)]
        psT, psW = bank[6], bank[7]
        pool_bank = [bank[0], bank[1], bank[4], bank[5]]
        psV = psT
        sq_junk = bank[4][:, :].rearrange("p (q f) -> p q f", q=G)

        s_loaded = sem("inputs_loaded")
        s_first_rows = sem("first_rows_loaded")
        s_w0 = sem("first_weights_loaded")
        s_cleared = sem("floor_and_slots_cleared")
        s_const = sem("constants_ready")
        s_x = sem("x_group_ready")
        s_stats = sem("stats_ready")
        s_mv = sem("mean_var_ready")
        s_std = sem("std_ready")
        s_rstd = sem("rstd_ready")
        s_norm = sem("norm_ready")
        s_hTp = sem("hT_in_psum")
        s_hT = sem("hT_ready")
        s_hw = sem("hw_in_psum")
        s_side = sem("side_ready")
        s_gsc = sem("operand_ready")
        s_p0 = sem("part0_ready")
        s_rem = sem("remainder_ready")
        s_p1 = sem("part1_ready")
        s_parts = sem("parts_ready")
        s_rows = [[sem(f"adj_rows_loaded{i}{h}") for h in "ab"] for i in range(2)]
        s_tr = sem("blocks_transposed")
        s_panel = sem("panel_chunk_ready")
        s_stored = [sem(f"panel_stored{i}") for i in range(G)]
        s_code = sem("codes_in_psum")
        s_code_used = sem("codes_used")
        s_list = sem("list_chain")
        s_prod = sem("product_in_psum")
        s_agg = sem("product_taken")
        s_lprod = sem("layer_product_in_psum")
        s_sum = sem("layer_product_taken")
        s_post = sem("post_chain")
        s_feat = sem("features_stored")
        s_deg = sem("degree_chain")
        s_found1 = sem("firsts_counted")
        s_found = sem("lists_counted")
        s_upto = sem("slot_sums_ready")
        s_counted = sem("list_counts_ready")
        s_list_idx = sem("list_indices_chain")
        s_listT = sem("list_counts_transposed")
        s_long = sem("longest_chain")
        s_missing = sem("control_in_psum")
        s_flag = sem("flag_ready")
        s_gen_m = sem("general_mask_loaded")
        s_gen_f = sem("general_features_loaded")
        s_gen_used = sem("general_chunk_used")
        s_gen = sem("general_chain")
        s_load = [sem(f"panel_loaded{i}") for i in range(G)]
        s_tri = sem("first_codes_in_psum")
        s_first = sem("first_chunk_ready")
        s_fp = sem("first_features_in_psum")
        s_fp_used = sem("first_features_taken")
        s_idx = sem("indices_staged")
        s_gath = [sem(f"rows_gathered{i}") for i in range(2)]
        s_gath2 = [sem(f"nearest_gathered{i}") for i in range(2)]
        s_gath_used = sem("gathered_used")
        s_max = sem("maxima_taken")
        s_deg_taken = sem("degrees_taken")
        s_hyp = sem("ball_chain")
        s_ssm = sem("mx_squares_ready")
        s_ssh = sem("h_squares_ready")
        s_nn = sem("norms_ready")
        s_ratio = sem("ln_argument_ready")
        s_ln = sem("ln_ready")
        s_targ = sem("tanh_argument_ready")
        s_tanh = sem("tanh_ready")
        s_z = sem("z_ready")
        s_zTp = sem("zT_in_psum")
        s_zT = sem("zT_ready")
        s_sqp = sem("square_parts_ready")
        s_sqTp = sem("squares_in_psum")
        s_sqT = sem("squares_row_ready")
        s_zs = sem("z_tile_staged")
        s_key = sem("keys_in_psum")
        s_keyrow = sem("key_chunk_ready")
        s_keyused = sem("key_row_used")
        s_top = sem("top_chain")
        s_topi = sem("top_lists_ready")
        s_w = sem("weights_chain")
        s_d2 = sem("square_distances_ready")
        s_sdeg = sem("second_degree_ready")
        s_sstd2 = sem("second_std_ready")
        s_sinv = sem("second_inverse_chain")
        s_sqrt = sem("distances_ready")
        s_exp = sem("similarities_ready")
        s_sstd = sem("degree_std_ready")
        s_g2 = sem("last_features_stored")
        s_fin = sem("output_ready")
        s_out = [sem(f"output_stored{i}") for i in range(2)]
        s_last = sem("last_chain")
        waited = {k: sem(f"{k}_has_waited") for k in ("pe", "act", "dve", "pool")}

        block = ctx.enter_context(nc.Block())

        class Count:
            def __init__(self, base):
                self.base, self.k = base, 0

            def up(self):
                self.k += 1
                return self.base + self.k

        parts_of = {0: partsA, 1: partsB, 2: partsA, 3: partsB, 4: partsA, 5: partsB}
        WIDTH = {0: FE, 2: F, 3: FE, 4: F, 5: F}
        SPLIT_OF_PREP = {0: 0, 1: 2, 2: 3, 3: 4}

        def part(u, g, k):
            return parts_of[u][:, ds(g * G, G), k * FE:(k + 1) * FE]

        def grp(t, g):
            return t[:, ds(g * G, G)]

        def turns(eng, body, first=0):
            body(first, True)
            with eng.Fori(first + 1, NG) as g:
                body(g, False)

        @block.sync
        def _(sp):
            loads = [(W["W1a"], w1[0:F, :]), (W["W1b"], w1[F:2 * F, :]), (W["W2"], w2),
                     (W["W31"], w31), (W["W32"], w32)]
            xr = x.rearrange("(t p) f -> p t f", p=P)
            sp.dma_start(X[:, 0:G, :], xr[:, 0:G, :]).then_inc(s_first_rows, 16)
            sp.dma_start(W["W0"][:, :], w0).then_inc(s_w0, 16)
            sp.dma_start(X[:, G:NT, :], xr[:, G:NT, :]).then_inc(s_loaded, 16)
            for t, a in loads:
                sp.dma_start(t[:, :], a).then_inc(s_loaded, 16)
            for k, a in (("b0", b0), ("b31", b31), ("b32", b32)):
                sp.dma_start(B[k][:, :], a.partition_broadcast(P)).then_inc(s_loaded, 16)
            sp.wait_ge(s_const, 1)
            sp.dma_start(feat_dram[N:N + 1, :], zero_row[:, :]).then_inc(s_loaded, 16)

            def load_rows(g, q, peeled):
                t = g * G + q
                for h in range(2):
                    if not (peeled and q < 2):
                        sp.wait_ge(s_tr, 4 * (t - 2) + 2 * (h + 1))
                    sp.dma_start(rows[:, q % 2, h * (N // 2):(h + 1) * (N // 2)],
                                 adj[ts(t, P), h * (N // 2):(h + 1) * (N // 2)]).then_inc(s_rows[q % 2][h], 16)

            def store_panel(g, q):
                t = g * G + q
                sp.wait_ge(s_panel, 4 * (t + 1) + 2)
                sp.dma_start(adjT_dram[ds(t, 1), :, :].rearrange("a p n -> p (a n)"),
                             panel[:, q, :, :].rearrange("p b i -> p (b i)").bitcast(BF16)).then_inc(s_stored[q], 16)

            def turn(g, peeled):
                for q in range(G):
                    load_rows(g, q, peeled)
                    if not (peeled and q == 0):
                        if q:
                            store_panel(g, q - 1)
                        else:
                            store_panel(g - 1, G - 1)
            turns(sp, turn)
            store_panel(NG - 1, G - 1)
            for q in range(G):
                sp.wait_ge(s_stored[q], 16 * NG)

            def load_panel(g, q):
                sp.dma_start(panel[:, q, :, :].rearrange("p b i -> p (b i)").bitcast(BF16),
                             adjT_dram[ds(g * G + q, 1), :, :].rearrange("a p n -> p (a n)")
                             ).then_inc(s_load[q], 16)

            for q in range(G):
                sp.wait_ge(s_code, 8 * (NT - G + q + 1))
                load_panel(0, q)

            sp.wait_ge(s_feat, 16 * NG)
            sp.wait_ge(s_flag, 1)
            short = sp.value_load(control[0:1, 0:1], min_val=0, max_val=1 << 24)
            with sp.If(short > 0):
                with sp.Fori(0, NT) as t:
                    with sp.Fori(0, N // 64) as c:
                        m = t * (N // 64) + c
                        sp.wait_ge(s_gen_used, m + 1)
                        sp.dma_start(general_mask[:, :], adj[ts(t, P), ts(c, 64)]).then_inc(s_gen_m, 16)
                        sp.dma_start(rows[:, :, :].rearrange("p a n -> p (a n)"),
                                     feat_dram[ts(c, 64), :].rearrange("j f -> (j f)").partition_broadcast(P)
                                     ).then_inc(s_gen_f, 16)

            with sp.Fori(1, NG) as g:
                for q in range(G):
                    sp.wait_ge(s_tri, 8 * (g * G + q - G + 1))
                    load_panel(g, q)
            for ps in range(1, 5):
                def turn(g, peeled):
                    for q in range(G):
                        if peeled and ps == 1:
                            sp.wait_ge(s_tri, 8 * (NT - G + q + 1))
                        else:
                            sp.wait_ge(s_lprod, (g + (ps - 1) * NG) * G + q - G + 1)
                        load_panel(g, q)
                turns(sp, turn)
            sp.wait_ge(s_g2, 16 * NG)

        @block.tensor
        def _(pe):
            pe.wait_ge(s_const, 7)
            pe.wait_ge(s_w0, 16)

            def aux_transposes(s, g):
                pe.wait_ge(s_norm, g + s * NG + 1)
                if s:
                    pe.wait_ge(s_side, 1 + (g if s == 1 else NG if s == 2 else g + NG))
                for q in range(G):
                    i = pe.transpose(psT[:, q * P:(q + 1) * P], hn[:, q, :], ident[:, :])
                i.then_inc(s_hTp, 1)

            def aux_products(s, g):
                pe.wait_ge(s_hT, g + s * NG + 1)
                pe.wait_ge(s_gsc, g + SPLIT_OF_PREP[s] * NG + 1)
                ws = {0: ["W0"], 1: ["W1b", "W1a"], 2: ["W2"], 3: ["W31", "W32"]}[s]
                for w, o in zip(ws, (psW, psV)):
                    for q in range(G):
                        i = pe.matmul(o[:, q * P:(q + 1) * P], hT[:, q * P:(q + 1) * P], W[w][:, :],
                                      start=True, stop=True)
                i.then_inc(s_hw, 1)

            def aux0(g, peeled):
                aux_transposes(0, g)
                aux_products(0, g)
            turns(pe, aux0)
            pe.wait_ge(s_loaded, 16 * 10)

            def transposes(g, q, c):
                if c % 2 == 0:
                    pe.wait_ge(s_rows[q % 2][c // 2], 16 * (g * 2 + q // 2 + 1))
                rb = rows[:, q % 2, :].bitcast(BF16).rearrange("p (n two) -> p n two", two=2)
                pe.wait_ge(s_panel, 4 * (g * G + q) + c + 1)
                o = bank[2 + c % 2][:, :].bitcast(BF16)
                for b in range(8):
                    j = c * 8 + b
                    i = pe.transpose(o[:, b * P:(b + 1) * P], rb[:, j * P:(j + 1) * P, 1], identb[:, :])
                i.then_inc(s_tr, 1)

            def product_chunk(g, q, c, wait_parts):
                t = g * G + q
                if wait_parts:
                    pe.wait_ge(s_parts, c + 1)
                if c == 0:
                    pe.wait_ge(s_agg, t + 1)
                pe.wait_ge(s_panel, 4 * t + c // 2 + 3)
                pe.wait_ge(s_code_used, 8 * t + c + 1)
                pe.sem_inc(waited["pe"], 1)
                for b in range(BPB):
                    j = c * BPB + b
                    i = pe.matmul(bank[q % 2][:, 0:FW], panel[:, q, j, :], parts_of[0][:, j, :],
                                  start=(j == 0), stop=(j == NT - 1))
                if c == NT // BPB - 1:
                    i.then_inc(s_prod, 1)
                for b in range(BPB):
                    i = pe.matmul(bank[4 + c % 4][:, b * P:(b + 1) * P], panel[:, q, c * BPB + b, :],
                                  diag_code[:, :], start=True, stop=True)
                i.then_inc(s_code, 1)

            def turn(g, peeled):
                for q in range(G):
                    before = (g, q - 1) if q else (g - 1, G - 1)
                    for c in range(NT // BPB):
                        if c % 2 == 0:
                            transposes(g, q, c // 2)
                        if not (peeled and q == 0):
                            product_chunk(*before, c, peeled and q == 1)
            turns(pe, turn)
            for c in range(NT // BPB):
                product_chunk(NG - 1, G - 1, c, False)
            pe.wait_ge(s_code_used, 8 * NT + 4)

            def tri_chunk(g, q, c):
                if c == 0:
                    pe.wait_ge(s_load[q], 16 * (g + 1))
                pe.wait_ge(s_first, 8 * (g * G + q) + c + 1)
                pe.sem_inc(waited["pe"], 1)
                pe.matmul(bank[2 + c % 2][:, :], tri[:, :],
                          panel[:, q, c * BPB:(c + 1) * BPB, :].rearrange("p b i -> p (b i)"),
                          start=True, stop=True).then_inc(s_tri, 1)

            pe.wait_ge(s_counted, 2 * NG)
            pe.transpose(psW[0:NT, 0:P], LISTN[:, :], ident[:, :]).then_inc(s_listT, 1)
            tri_chunk(0, 0, 0)
            tri_chunk(0, 0, 1)
            pe.wait_ge(s_deg, 3)
            pe.wait_ge(s_long, 5)
            pe.wait_ge(s_upto, 3)
            pe.matmul(psT[0:1, 0:1], missing_n[:, 0:1], ones_col[:, 0:1], start=True, stop=True)
            pe.matmul(psT[0:1, 1:1 + NT], longest[:, 0:1], ident[0:NT, 0:NT], start=True, stop=True)
            pe.matmul(psT[0:1, 1 + NT:1 + 2 * NT], longest[:, 1:2], upto[:, :], start=True, stop=True
                      ).then_inc(s_missing, 1)

            pparts = parts_of[1]

            def firsts(g, q, last, c0=0, c1=NT // BPB):
                t = g * G + q
                for c in range(c0, c1):
                    pe.wait_ge(s_first, 8 * t + c + 3)
                    pe.wait_ge(s_fp_used, 8 * t + c + 1)
                    pe.sem_inc(waited["pe"], 1)
                    for b in range(BPB):
                        j = c * BPB + b
                        for k in range(3):
                            i = pe.matmul(pool_bank[c % 4][:, b * P:(b + 1) * P], first[:, q % 2, j, :],
                                          pparts[:, j, k * FE:k * FE + F], start=(k == 0), stop=(k == 2))
                    i.then_inc(s_fp, 1)
                    if c + 2 < NT // BPB:
                        tri_chunk(g, q, c + 2)
                    elif q + 1 < G:
                        tri_chunk(g, q + 1, c + 2 - NT // BPB)
                    elif not last:
                        tri_chunk(g + 1, 0, c + 2 - NT // BPB)

            def pool_turn(g, first_group, last):
                for q in range(3):
                    firsts(g, q, last)
                if not first_group:
                    aux_transposes(1, g - 1)
                firsts(g, 3, last, 0, 2)
                if not first_group:
                    aux_products(1, g - 1)
                firsts(g, 3, last, 2)
            pe.wait_ge(s_parts, 2 * NG)
            pool_turn(0, True, False)
            with pe.Fori(1, NG - 1) as g:
                pool_turn(g, False, False)
            pool_turn(NG - 1, False, True)

            def blocks(u, q, j0, j1):
                w = WIDTH[u]
                for j in range(j0, j1):
                    of_block = parts_of[u][:, j, :].rearrange("p (k f) -> p k f", k=3)[:, :, 0:w]
                    i = pe.matmul(bank[q][:, 0:3 * w], panel[:, q, j, :], of_block if w < FE else parts_of[u][:, j, :],
                                  start=(j == 0), stop=(j == NT - 1))
                return i

            def product(u, g, q, ps, j0=0, j1=NT):
                if j0 == 0:
                    pe.wait_ge(s_load[q], 16 * (g + ps * NG + 1))
                    pe.wait_ge(s_sum, (g + (ps - 1) * NG) * G + q + 1)
                    pe.sem_inc(waited["pe"], 1)
                i = blocks(u, q, j0, j1)
                if j1 == NT:
                    i.then_inc(s_lprod, 1)

            def first_products(u, ps, s):
                for q in range(G):
                    pe.wait_ge(s_load[q], 16 * (ps * NG + 1))
                    pe.wait_ge(s_sum, (ps - 1) * NG * G + q + 1)
                    pe.wait_ge(s_parts, (u + 1) * NG - 2)
                    if q == 3 and s is not None:
                        aux_transposes(s, NG - 1)
                        blocks(u, q, 0, 6)
                        aux_products(s, NG - 1)
                        blocks(u, q, 6, NT - 2 * G)
                    else:
                        blocks(u, q, 0, NT - 2 * G)
                pe.wait_ge(s_parts, (u + 1) * NG - 1)
                for q in range(G):
                    blocks(u, q, NT - 2 * G, NT - G)
                pe.wait_ge(s_parts, (u + 1) * NG)
                for q in range(G):
                    blocks(u, q, NT - G, NT).then_inc(s_lprod, 1)

            def layer(u, ps, s):
                first_products(u, ps, s - 1)
                with pe.Fori(1, NG) as g:
                    for q in range(3):
                        product(u, g, q, ps)
                    product(u, g, 3, ps, 0, NT - 8)
                    aux_transposes(s, g - 1)
                    product(u, g, 3, ps, NT - 8, NT)
                    aux_products(s, g - 1)

            pe.wait_ge(s_fp_used, 8 * NT + 4)
            pe.wait_ge(s_first, 8 * NT + 2)
            layer(2, 1, 2)
            layer(3, 2, 3)

            def z_aux(g, peeled):
                if not peeled:
                    pe.wait_ge(s_zT, g)
                    pe.wait_ge(s_sqT, g)
                pe.wait_ge(s_z, g + 1)
                for q in range(G):
                    i = pe.transpose(psT[:, q * P:(q + 1) * P], xg[:, q, :], ident[:, :])
                i.then_inc(s_zTp, 1)
                pe.wait_ge(s_sqp, g + 1)
                for q in range(G):
                    i = pe.transpose(psW[0:3, :].bitcast(BF16)[:, q * P:(q + 1) * P], sqp[:, q, :], identb[:, :])
                i.then_inc(s_sqTp, 1)

            first_products(4, 3, 3)
            for q in range(G):
                product(4, 1, q, 3)
            z_aux(0, True)
            with pe.Fori(2, NG) as g:
                for q in range(G):
                    product(4, g, q, 3)
                z_aux(g - 1, False)

            pe.wait_ge(s_sum, 3 * NT + 4)

            def keys(g, first_tile=False):
                for q in range(G):
                    t = g * G + q
                    pe.wait_ge(s_zs, t + 1)
                    for c in range(8):
                        if first_tile and q == 0:
                            if c == 6:
                                z_aux(NG - 1, False)
                            pe.wait_ge(s_zT, c + 1 if c < 6 else NG)
                            pe.wait_ge(s_sqT, c + 1 if c < 6 else NG)
                        pe.wait_ge(s_keyrow, 8 * t + c + 1)
                        o = bank[c]
                        pe.matmul(o[:, :], zs[:, q % 2, :], zT[:, c * 512:(c + 1) * 512], start=True, stop=False)
                        pe.matmul(o[:, :], ones3[:, :], SQT[:, c * 512:(c + 1) * 512], start=False, stop=True
                                  ).then_inc(s_key, 1)
            keys(0, True)
            with pe.Fori(1, NG) as g:
                keys(g)
            pe.wait_ge(s_keyrow, 8 * NT + 8)
            first_products(5, 4, None)
            with pe.Fori(1, NG) as g:
                for q in range(G):
                    product(5, g, q, 4)

        @block.scalar
        def _(act):
            act.wait_ge(s_const, 7)
            for s, k in ((s_panel, 2), (s_first, 2), (s_side, 1), (s_keyrow, 8)):
                act.sem_inc(s, k)

            def std_of(s, g):
                n = g + s * NG
                act.wait_ge(s_mv, n + 1)
                act.activation(std[:, :], mv[:, :, 1], ACT.Sqrt, bias=eps_ln[:, 0:1]).then_inc(s_std, 1)

            def hT_of(s, g):
                act.wait_ge(s_hTp, g + s * NG + 1)
                act.activation(hT[:, :], psT[:, :], ACT.Relu).then_inc(s_hT, 1)

            def side_of(s, g):
                act.wait_ge(s_hw, g + s * NG + 1)
                act.copy(grp(side, g), psV[:, :].rearrange("p (q f) -> p q f", q=G)).then_inc(s_side, 1)

            def part0(u, g):
                act.wait_ge(s_gsc, g + u * NG + 2)
                act.copy(part(u, g, 0), gsc[:, :, :]).then_inc(s_p0, 1)

            def part1(u, g):
                act.wait_ge(s_rem, g + u * NG + 2)
                act.copy(part(u, g, 1), rem[:, :, :]).then_inc(s_p1, 1)

            def split(u, g):
                part0(u, g)
                part1(u, g)

            def turn(g, peeled, second=False):
                std_of(0, g)
                hT_of(0, g)
                if not (peeled or second):
                    part1(0, g - 2)
                if not peeled:
                    part0(0, g - 1)
            turn(0, True)
            turn(1, False, True)
            with act.Fori(2, NG) as g:
                turn(g, False)
            part1(0, NG - 2)
            split(0, NG - 1)

            def evac_panel(g, q, first_group):
                t = g * G + q
                if not first_group:
                    act.wait_ge(s_stored[q], 16 * g)
                    act.wait_ge(s_code, 8 * (t - G + 1))
                for c in range(4):
                    act.wait_ge(s_tr, 4 * t + c + 1)
                    act.sem_inc(waited["act"], 1)
                    act.activation(panel[:, q, c * 8:(c + 1) * 8, :].rearrange("p b i -> p (b i)"),
                                   bank[2 + c % 2][:, :].bitcast(BF16), ACT.Copy, saturate=False
                                   ).then_inc(s_panel, 1)

            def feat_store(g):
                act.wait_ge(s_post, 2 * (g + 1))
                act.dma_start(feat_dram[ds(g * G * P, G * P), :].rearrange("(t p) f -> p t f", p=P),
                              gsc[:, :, 0:F]).then_inc(s_feat, 16)

            def turn(g, peeled):
                for q in range(G):
                    evac_panel(g, q, peeled)
                    if q == 1 and not peeled:
                        feat_store(g - 1)
                        part0(1, g - 1)
                    if q == 3 and not peeled:
                        part1(1, g - 1)
            turns(act, turn)
            feat_store(NG - 1)
            split(1, NG - 1)

            act.wait_ge(s_deg, 3)
            act.activation(DSTD[:, :], DEG[:, :], ACT.Sqrt).then_inc(s_sstd, 1)

            def firsts(g, q, c0=0, c1=8):
                t = g * G + q
                for c in range(c0, c1):
                    act.wait_ge(s_tri, 8 * t + c + 1)
                    act.sem_inc(waited["act"], 1)
                    act.activation(first[:, q % 2, c * BPB:(c + 1) * BPB, :].rearrange("p b i -> p (b i)"),
                                   bank[2 + c % 2][:, :], ACT.Relu, saturate=False).then_inc(s_first, 1)

            def after(u, s, g, more=None):
                hT_of(s, g)
                if s in (1, 3):
                    side_of(s, g)
                if more:
                    more(g)
                split(u, g)

            def clear(g, q):
                t = g * G + q
                act.wait_ge(s_max, t + 1)
                act.activation(gath[:, q % 2, BASE:LIST, :].rearrange("p k f -> p (k f)"),
                               ones_col[:, 0:1].to_broadcast([P, (LIST - BASE) * F]), ACT.Copy, scale=0.0
                               ).then_inc(s_gath_used, 1)

            def turn(g, peeled, second=False):
                for q in range(G):
                    firsts(g, q, 0, 2)
                    if q >= 2:
                        clear(g, q - 2)
                    elif not peeled:
                        clear(0 if second else g - 1, q + 2)
                    firsts(g, q, 2, 4)
                    if not peeled:
                        if q == 2:
                            std_of(1, g - 1)
                        if q == 3:
                            side_of(1, g - 1)
                    firsts(g, q, 4, 8)
                    if q == 0 and not (peeled or second):
                        part1(2, g - 2)
                    if not peeled:
                        if q == 2:
                            hT_of(1, g - 1)
                        if q == 3:
                            part0(2, g - 1)
            turn(0, True)
            turn(1, False, True)
            with act.Fori(2, NG) as g:
                turn(g, False)
            part1(2, NG - 2)
            clear(NG - 1, 2)
            clear(NG - 1, 3)
            std_of(1, NG - 1)
            after(2, 1, NG - 1)

            def ball_in(g):
                act.wait_ge(s_hw, g + 2 * NG + 1)
                for q in range(G):
                    i = act.activation(sq_junk[:, q, :], psW[:, q * P:(q + 1) * P], ACT.Square,
                                       accum_out=ss[:, 1, q:q + 1])
                i.then_inc(s_ssm, 1)
                act.wait_ge(s_ssm, g + 1)
                act.wait_ge(s_ssh, g + 1)
                act.activation(nn[:, :, :], ss[:, :, :], ACT.Sqrt).then_inc(s_nn, 1)
                act.wait_ge(s_ratio, g + 1)
                act.activation(v[3][:, :], v[2][:, :], ACT.Ln).then_inc(s_ln, 1)
                act.wait_ge(s_targ, g + 1)
                act.activation(v[5][:, :], v[4][:, :], ACT.Tanh).then_inc(s_tanh, 1)

            def turn(g, peeled):
                if not peeled:
                    after(3, 2, g - 1, ball_in)
                std_of(2, g)
            turns(act, turn)
            after(3, 2, NG - 1, ball_in)

            def ball_out(g):
                act.wait_ge(s_ssm, NG + g + 1)
                act.activation(nn[:, :, :], ss[:, :, :], ACT.Sqrt).then_inc(s_nn, 1)
                act.wait_ge(s_ratio, NG + g + 1)
                act.activation(v[3][:, :], v[2][:, :], ACT.Ln).then_inc(s_ln, 1)
                act.wait_ge(s_targ, NG + g + 1)
                act.activation(v[5][:, :], v[4][:, :], ACT.Tanh).then_inc(s_tanh, 1)

            def turn(g, peeled):
                if not peeled:
                    after(4, 3, g - 1)
                ball_out(g)
                std_of(3, g)
            turns(act, turn)
            after(4, 3, NG - 1)

            def z_out(g):
                act.wait_ge(s_zTp, g + 1)
                act.copy(zT[:, ds(g * G * P, G * P)], psT[:, :]).then_inc(s_zT, 1)
                act.wait_ge(s_sqTp, g + 1)
                act.copy(SQT[:, ds(g * G * P, G * P)], psW[0:3, :].bitcast(BF16)[:, 0:G * P]).then_inc(s_sqT, 1)

            with act.Fori(0, NG - 1) as g:
                z_out(g)

            def similarities(g):
                act.wait_ge(s_d2, g + 1)
                act.activation(dist[:, :, :], d2c[:, :, :], ACT.Sqrt, bias=eps_dist[:, 0:1]).then_inc(s_sqrt, 1)
                act.wait_ge(s_sqrt, g + 1)
                act.activation(simil[:, :, :], dist[:, :, :], ACT.Exp, scale=-0.5).then_inc(s_exp, 1)

            def second_std(g):
                act.wait_ge(s_sdeg, g + 1)
                act.activation(sstd[:, :], sdeg[:, :], ACT.Sqrt).then_inc(s_sstd2, 1)

            def last_operand(g):
                act.wait_ge(s_gsc, g + 5 * NG + 2)
                act.dma_start(g2_dram[ds(g * G * P, G * P), :].rearrange("(t p) f -> p t f", p=P),
                              gsc[:, :, 0:F]).then_inc(s_g2, 16)
                part0(5, g)

            act.wait_ge(s_zT, NG - 1)

            act.copy(zs[:, 0, :], zT[:, 0:P]).then_inc(s_zs, 1)

            def turn(g, peeled, second_group=False, last=False):
                for q in range(G):
                    t = g * G + q
                    if not (last and q == G - 1):
                        if not (peeled and q == 0):
                            act.wait_ge(s_key, 8 * t)
                        act.copy(zs[:, (q + 1) % 2, :], zT[:, ts(t + 1, P)]).then_inc(s_zs, 1)
                    act.wait_ge(s_keyused, t + 1)
                    for c in range(8):
                        if peeled and q == 0 and c == 6:
                            z_out(NG - 1)
                        act.wait_ge(s_key, 8 * t + c + 1)
                        act.copy(rows[:, q % 2, c * 512:(c + 1) * 512], bank[c][:, :]).then_inc(s_keyrow, 1)
                    if not peeled:
                        if q == 1:
                            similarities(g - 1)
                            if not second_group:
                                last_operand(g - 2)
                        if q == 2 and not second_group:
                            part1(5, g - 2)
                        if q == 3:
                            second_std(g - 1)
            turn(0, True)
            turn(1, False, second_group=True)
            with act.Fori(2, NG - 1) as g:
                turn(g, False)
            turn(NG - 1, False, last=True)
            last_operand(NG - 2)
            part1(5, NG - 2)
            similarities(NG - 1)
            second_std(NG - 1)
            last_operand(NG - 1)
            part1(5, NG - 1)
            act.wait_ge(s_g2, 16 * NG)

            with act.Fori(0, NG // 2) as h:
                for r in range(2):
                    g = h * 2 + r
                    act.wait_ge(s_fin, g + 1)
                    act.dma_start(out[ds(g * G * P, G * P), :].rearrange("(t p) f -> p t f", p=P),
                                 fin[:, r, :, :]).then_inc(s_out[r], 16)
            for r in range(2):
                act.wait_ge(s_out[r], 16 * (NG // 2))

        @block.gpsimd
        def _(pool):
            pool.memset(zero_row[:, :], 0.0).then_inc(s_const, 1)
            pool.memset(ident[:, :], 0.0).then_inc(s_const, 1)
            pool.wait_ge(s_const, 2)
            pool.affine_select(out=ident[:, :], in_=ident[:, :], compare_op=ALU.not_equal, fill=1.0, base=0,
                               pattern=[[-1, P]], channel_multiplier=1).then_inc(s_const, 1)
            pool.iota(code_row[:, :], pattern=[[-1, P]], base=P, channel_multiplier=0,
                      allow_small_or_imprecise_dtypes=True)
            pool.iota(block_code[:, :, :], pattern=[[-P, NT], [0, 7]], base=N - P, channel_multiplier=0,
                      allow_small_or_imprecise_dtypes=True)
            pool.iota(parity[:, :], pattern=[[1, NT]], base=0, channel_multiplier=1)
            pool.memset(eps_ln[:, :], LN_EPS)
            pool.memset(eps_dist[:, :], DISTANCE_EPS)
            pool.memset(ones_col[:, :], 1.0)
            pool.memset(ones3[:, :], 1.0)
            pool.memset(gsc[:, :, F:FE], 1.0).then_inc(s_const, 1)
            pool.wait_ge(s_const, 4)
            pool.tensor_copy(identb[:, :], ident[:, :]).then_inc(s_const, 1)
            pool.tensor_tensor(diag_code[:, :], ident[:, :], code_row[:, :], ALU.mult).then_inc(s_const, 1)
            pool.affine_select(out=tri[:, :], in_=ident[:, :], compare_op=ALU.is_ge, fill=-1.0, base=0,
                               pattern=[[-1, P]], channel_multiplier=1).then_inc(s_const, 1)
            pool.sem_inc(s_rem, 1)
            pool.sem_inc(s_found1, 1)

            def remainder(u, g):
                pool.wait_ge(s_p0, g + u * NG + 1)
                pool.tensor_tensor(rem[:, :, :], gsc[:, :, :], part(u, g, 0), ALU.subtract).then_inc(s_rem, 1)

            def part2(u, g):
                m = g + u * NG
                pool.wait_ge(s_p1, m + 1)
                pool.tensor_tensor(part(u, g, 2), rem[:, :, :], part(u, g, 1), ALU.subtract).then_inc(s_parts, 1)
                pool.wait_ge(s_parts, m + 1)

            def split(u, g):
                remainder(u, g)
                part2(u, g)

            pool.wait_ge(s_upto, 2)
            pool.affine_select(out=upto[:, :], in_=upto[:, :], compare_op=ALU.is_ge, fill=0.0, base=0,
                               pattern=[[1, NT]], channel_multiplier=-1).then_inc(s_upto, 1)
            remainder(0, 0)
            with pool.Fori(1, NG) as g:
                part2(0, g - 1)
                remainder(0, g)
            part2(0, NG - 1)
            for k, (k0, k1) in enumerate(zip((BASE,) + MORE, MORE)):
                pool.memset(level[:, 0, k:k + 1], float(k0))
                pool.memset(level[:, 1, k:k + 1], float(k1 - k0))
            pool.memset(gath[:, :, BASE:LIST, :], 0.0).then_inc(s_cleared, 1)
            pool.memset(wide[:, :, :], 0.0).then_inc(s_cleared, 1)

            def count_lists(g, q):
                t = g * G + q
                pool.wait_ge(s_code_used, 8 * (t + 1) + 4)
                pool.sem_inc(waited["pool"], 1)
                pool.tensor_scalar(found[:, q, 0:NT], cand[:, :, 0], 0.0, None, ALU.is_gt).then_inc(s_found1, 1)
                pool.wait_ge(s_list, 5 * (t + 1))
                pool.sem_inc(waited["pool"], 1)
                pool.tensor_scalar(found[:, q, NT:NT + LIST], listed[:, q, :], 0.0, None, ALU.is_gt).then_inc(s_found, 1)

            def turn(g, peeled):
                if not peeled:
                    pool.wait_ge(s_counted, 2 * g)
                for q in range(G):
                    count_lists(g, q)
                    if q == 0 and not peeled:
                        remainder(1, g - 1)
                    if q == 2 and not peeled:
                        part2(1, g - 1)
                pool.tensor_scalar(list_idx[:, :, :], listed[:, :, :], -1.0, float(N), ALU.mult, ALU.add
                                   ).then_inc(s_list_idx, 1)
                pool.wait_ge(s_list_idx, 2 * g + 1)
                pool.tensor_copy(grp(IDX, g), list_idx[:, :, :]).then_inc(s_list_idx, 1)
                pool.wait_ge(s_list_idx, 2 * g + 2)
            turns(pool, turn)
            split(1, NG - 1)

            pool.wait_ge(s_cleared, 2)
            pool.wait_ge(s_feat, 16 * NG)
            pool.wait_ge(s_loaded, 16 * 10)
            pool.wait_ge(s_flag, 1)

            def gathers(g, q):
                t = g * G + q
                pool.wait_ge(s_idx, t + 1)
                pool.wait_ge(s_gath_used, t + 1)
                pool.sem_inc(waited["pool"], 1)
                for k in range(BASE):
                    pool.indirect_dma_start(gath[:, q % 2, k, :], None, feat_dram,
                                            bass.IndirectOffsetOnAxis(idx_now[:, q % 2, k:k + 1], axis=0)
                                            ).then_inc(s_gath[q % 2], 16)
                longest_list = pool.value_load(control[0:1, ds(t + 1, 1)], min_val=0, max_val=LIST)
                for k0, k1 in zip((BASE,) + MORE, MORE):
                    with pool.If(longest_list > k0):
                        for k in range(k0, k1):
                            pool.indirect_dma_start(gath[:, q % 2, k, :], None, feat_dram,
                                                    bass.IndirectOffsetOnAxis(idx_now[:, q % 2, k:k + 1], axis=0)
                                                    ).then_inc(s_gath[q % 2], 16)

            def turn(g, peeled):
                for q in range(G):
                    gathers(g, q)
            with pool.Fori(0, NG) as g:
                turn(g, False)
            pool.wait_ge(s_parts, 3 * NG)
            for u in (3, 4, 5):
                with pool.Fori(0, NG) as g:
                    split(u, g)

            pool.wait_ge(s_g2, 16 * NG)

            def last_gathers(g, q):
                t = NT + g * G + q
                pool.wait_ge(s_gath_used, t + 1)
                pool.tensor_copy(idx_now[:, q % 2, 0:TOP], TI[:, ds(g * G + q, 1), :].rearrange("p a k -> p (a k)")
                                 ).then_inc(s_idx, 1)
                pool.wait_ge(s_idx, t + 1)
                pool.sem_inc(waited["pool"], 1)
                for k in range(TOP):
                    pool.indirect_dma_start(gath[:, q % 2, k, :], None, g2_dram,
                                            bass.IndirectOffsetOnAxis(idx_now[:, q % 2, k:k + 1], axis=0)
                                            ).then_inc(s_gath2[q % 2], 16)
            with pool.Fori(0, NG) as g:
                for q in range(G):
                    last_gathers(g, q)

        @block.vector
        def _(dve):
            V = [t[:, :] for t in v]
            dve.wait_ge(s_const, 7)
            dve.wait_ge(s_first_rows, 16)
            for s, k in ((s_gsc, 1), (s_agg, 2), (s_sum, 4), (s_code_used, 4), (s_fp_used, 4), (s_gath_used, 2),
                         (s_keyused, 2), (s_gen_used, 1)):
                dve.sem_inc(s, k)

            dve.tensor_scalar(parity[:, :], parity[:, :], 1, None, ALU.bitwise_and).then_inc(s_upto, 1)
            dve.wait_ge(s_upto, 1)
            dve.tensor_scalar(upto[:, :], parity[:, :], -16.0, 16.0, ALU.mult, ALU.add).then_inc(s_upto, 1)

            def per_row(t2, width=F):
                return t2.unsqueeze(2).to_broadcast([P, G, width])

            def bias3(k):
                return B[k][:, :].unsqueeze(1).to_broadcast([P, G, F])

            def normalise(s, g):
                n = g + s * NG
                dve.wait_ge(s_x, n + 1)
                for q in range(G):
                    i = dve.bn_stats(st[:, q, :], xg[:, q, :])
                i.then_inc(s_stats, 1)
                dve.wait_ge(s_stats, n + 1)
                dve.sem_inc(waited["dve"], 1)
                for q in range(G):
                    i = dve.bn_aggr(mv[:, q, :], st[:, q, :])
                i.then_inc(s_mv, 1)
                dve.wait_ge(s_std, n + 1)
                dve.reciprocal(rstd[:, :], std[:, :]).then_inc(s_rstd, 1)
                dve.wait_ge(s_rstd, n + 1)
                for q in range(G):
                    i = dve.tensor_scalar(hn[:, q, :], xg[:, q, :], mv[:, q, 0:1], rstd[:, q:q + 1],
                                          ALU.subtract, ALU.mult)
                i.then_inc(s_norm, 1)

            def gsc_free(u, g):
                dve.wait_ge(s_rem, g + u * NG + 1)

            def operand(s, g):
                u = SPLIT_OF_PREP[s]
                dve.wait_ge(s_hw, g + s * NG + 1)
                gsc_free(u, g)
                ps = psW[:, :].rearrange("p (q f) -> p q f", q=G)
                if s == 3:
                    dve.tensor_tensor(gsc[:, :, 0:F], ps, per_row(grp(DINV, g)), ALU.mult).then_inc(s_gsc, 1)
                else:
                    dve.tensor_copy(gsc[:, :, 0:F], ps).then_inc(s_gsc, 1)

            def turn(g, peeled):
                if not peeled:
                    dve.wait_ge(s_loaded, 16 * 10)
                    dve.wait_ge(s_norm, g)
                    dve.wait_ge(s_hTp, g)
                dve.tensor_copy(xg[:, :, :], grp(X, g)).then_inc(s_x, 1)
                normalise(0, g)
                if not peeled:
                    operand(0, g - 1)
            turns(dve, turn)
            operand(0, NG - 1)

            def take_product(u, T, q):
                dve.wait_ge(s_lprod, T + 1)
                w = WIDTH[u]
                dve.tensor_reduce(agg[:, q, 0:w], bank[q][:, 0:3 * w].rearrange("p (k f) -> p f k", k=3),
                                  axis=AX, op=ALU.add).then_inc(s_sum, 1)

            LSTEPS = 5

            def list_max(g, q, k, first_group=False):
                t = g * G + q
                dve.wait_ge(s_list, LSTEPS * t + 2 + k)
                if k == 0:
                    if q == 0 and not first_group:
                        dve.wait_ge(s_list_idx, 2 * g)
                    dve.sem_inc(waited["dve"], 1)
                    dve.max(listed[:, q, 0:8], rest[:, :]).then_inc(s_list, 1)
                if k == 1:
                    dve.scalar_tensor_tensor(rest2[:, :], rest[:, :], listed[:, q, 7:8], rest[:, :],
                                             ALU.is_lt, ALU.mult).then_inc(s_list, 1)
                if k == 2:
                    dve.sem_inc(waited["dve"], 1)
                    dve.max(listed[:, q, 8:16], rest2[:, :]).then_inc(s_list, 1)

            def layer0_sum(g):
                dve.tensor_copy(grp(DEG, g), agg[:, :, F]).then_inc(s_deg_taken, 1)
                dve.tensor_tensor(tmp[:, :, :], agg[:, :, 0:F], bias3("b0"), ALU.add).then_inc(s_post, 1)

            def layer0_out(g, first_group):
                gsc_free(1, g)
                if not first_group:
                    dve.wait_ge(s_feat, 16 * g)
                dve.wait_ge(s_post, 2 * g + 1)
                dve.tensor_scalar(gsc[:, :, 0:F], tmp[:, :, :], 0.0, None, ALU.max).then_inc(s_post, 1)

            def count_found(g):
                dve.wait_ge(s_found, (g + 1) * G)
                dve.sem_inc(waited["dve"], 1)
                dve.tensor_reduce(grp(FOUND, g), found[:, :, :], axis=AX, op=ALU.add).then_inc(s_counted, 1)
                dve.tensor_reduce(grp(LISTN, g), found[:, :, NT:NT + LIST], axis=AX, op=ALU.add
                                  ).then_inc(s_counted, 1)

            def lists(g, q, peeled, second):
                t = g * G + q
                before = (g, q - 1) if q else (0 if second else g - 1, G - 1)
                first_tile = peeled and q == 0
                dve.wait_ge(s_found1, t + 1)
                for ch in range(NT // BPB):
                    if ch < 3 and not first_tile:
                        list_max(*before, ch, first_group=peeled)
                    if q == 0 and not first_tile:
                        if ch == 1:
                            dve.wait_ge(s_agg, t + 2)
                            layer0_sum(before[0])
                        if ch == 3:
                            layer0_out(before[0], second)
                        if ch == 4:
                            dve.wait_ge(s_post, 2 * (before[0] + 1))
                            dve.wait_ge(s_deg_taken, before[0] + 1)
                            dve.sem_inc(s_gsc, 1)
                        if ch == 6:
                            count_found(before[0])
                    dve.wait_ge(s_code, 8 * t + ch + 1)
                    dve.sem_inc(waited["dve"], 1)
                    for b in range(BPB):
                        i = dve.max(cand[:, ch * BPB + b, :], bank[4 + ch % 4][:, b * P:(b + 1) * P])
                    i.then_inc(s_code_used, 1)
                dve.wait_ge(s_prod, t + 1)
                dve.tensor_reduce(agg[:, q, :], bank[q % 2][:, 0:FW].rearrange("p (k f) -> p f k", k=3),
                                  axis=AX, op=ALU.add).then_inc(s_agg, 1)
                dve.wait_ge(s_code_used, 8 * (t + 1) + 4)
                if not first_tile:
                    dve.wait_ge(s_list, LSTEPS * t)
                r3 = rest[:, :].rearrange("p (b k) -> p b k", k=7)
                dve.scalar_tensor_tensor(r3, cand[:, :, 1:8], 0.0, block_code[:, :, :], ALU.is_gt, ALU.mult
                                         ).then_inc(s_list, 1)
                dve.wait_ge(s_list, LSTEPS * t + 1)
                dve.tensor_tensor(r3, r3, cand[:, :, 1:8], ALU.add).then_inc(s_list, 1)

            def turn(g, peeled, second=False):
                for q in range(G):
                    lists(g, q, peeled, second)
            turn(0, True)
            turn(1, False, True)
            with dve.Fori(2, NG) as g:
                turn(g, False)
            for k in range(3):
                list_max(NG - 1, G - 1, k)
            dve.wait_ge(s_agg, NT + 2)
            layer0_sum(NG - 1)
            layer0_out(NG - 1, False)
            dve.wait_ge(s_post, 2 * NG)
            dve.wait_ge(s_deg_taken, NG)
            dve.sem_inc(s_gsc, 1)
            count_found(NG - 1)
            dve.wait_ge(s_list_idx, 2 * NG)
            for q in range(2):
                dve.tensor_copy(idx_now[:, q, :], IDX[:, q, :]).then_inc(s_idx, 1)

            dve.wait_ge(s_cleared, 2)

            dve.wait_ge(s_deg_taken, NG)
            dve.wait_ge(s_counted, 2 * NG)
            dve.wait_ge(s_listT, 1)
            dve.tensor_reduce(longest[:, 0:1], psW[0:NT, 0:P], axis=AX, op=ALU.max).then_inc(s_long, 1)
            dve.wait_ge(s_long, 1)
            dve.tensor_tensor(level[:, 2, :], longest[:, 0:1].to_broadcast([NT, len(MORE)]), level[:, 0, :],
                              ALU.is_gt).then_inc(s_long, 1)
            dve.wait_ge(s_long, 2)
            dve.tensor_tensor(level[:, 2, :], level[:, 2, :], level[:, 1, :], ALU.mult).then_inc(s_long, 1)
            dve.wait_ge(s_long, 3)
            dve.tensor_reduce(longest[:, 1:2], level[:, 2, :], axis=AX, op=ALU.add).then_inc(s_long, 1)
            dve.wait_ge(s_long, 4)
            dve.tensor_scalar(longest[:, 1:2], longest[:, 1:2], float(BASE), None, ALU.add).then_inc(s_long, 1)
            dve.tensor_tensor(missing[:, :], DEG[:, :], FOUND[:, :], ALU.subtract).then_inc(s_deg, 1)
            dve.tensor_scalar(NOROW[:, :], DEG[:, :], 0.0, -FLT_MAX, ALU.is_equal, ALU.mult).then_inc(s_deg, 1)
            dve.wait_ge(s_deg, 2)
            dve.tensor_reduce(missing_n[:, :], missing[:, :], axis=AX, op=ALU.add).then_inc(s_deg, 1)
            dve.wait_ge(s_sstd, 1)
            dve.reciprocal(DINV[:, :], DSTD[:, :]).then_inc(s_deg, 1)
            dve.wait_ge(s_missing, 1)
            dve.tensor_copy(control[:, :], psT[0:1, 0:1 + 2 * NT]).then_inc(s_flag, 1)
            dve.wait_ge(s_flag, 1)
            short = dve.value_load(control[0:1, 0:1], min_val=0, max_val=1 << 24)
            with dve.If(short > 0):
                CH = N // 64
                feats = rows[:, :, :].rearrange("p a (j f) -> p (a j) f", f=F)
                with dve.Fori(0, NT) as t:
                    dve.memset(general_acc[:, :], 0.0).then_inc(s_gen, 1)
                    with dve.Fori(0, CH) as c:
                        m = t * CH + c
                        k = t * (4 * CH + 2) + c * 4 + 1
                        dve.wait_ge(s_gen, k)
                        dve.wait_ge(s_gen_m, 16 * (m + 1))
                        dve.tensor_scalar(general_cap[:, :], general_mask[:, :], 0.0, FLT_MAX, ALU.not_equal,
                                          ALU.mult).then_inc(s_gen, 1)
                        dve.wait_ge(s_gen, k + 1)
                        dve.wait_ge(s_gen_f, 16 * (m + 1))
                        dve.tensor_tensor(feats, feats, general_cap[:, :].unsqueeze(2).to_broadcast([P, 64, F]),
                                          ALU.min).then_inc(s_gen, 1)
                        dve.wait_ge(s_gen, k + 2)
                        dve.tensor_reduce(general_new[:, :], feats.rearrange("p j f -> p f j"), axis=AX,
                                          op=ALU.max).then_inc(s_gen, 1)
                        dve.wait_ge(s_gen, k + 3)
                        dve.tensor_tensor(general_acc[:, :], general_acc[:, :], general_new[:, :], ALU.max
                                          ).then_inc(s_gen, 1)
                        dve.wait_ge(s_gen, k + 4)
                        dve.sem_inc(s_gen_used, 1)
                    dve.tensor_copy(wide[:, ds(t, 1), :].rearrange("p a f -> p (a f)"), general_acc[:, :]
                                    ).then_inc(s_gen, 1)
                    dve.wait_ge(s_gen, (t + 1) * (4 * CH + 2))

            dve.wait_ge(s_deg, 4)
            dve.wait_ge(s_feat, 16 * NG)

            def firsts_max(g, q, half, first_two=False):
                t = g * G + q
                if half == 0 and not first_two:
                    dve.wait_ge(s_max, t - 1)
                for c in range(4 * half, 4 * half + 4):
                    dve.wait_ge(s_fp, 8 * t + c + 1)
                    dve.tensor_reduce(gath[:, q % 2, LIST + c, :],
                                      pool_bank[c % 4][:, :].rearrange("p (b f) -> p f b", b=BPB),
                                      axis=AX, op=ALU.max).then_inc(s_fp_used, 1)

            def stage(g, q):
                dve.tensor_copy(idx_now[:, q % 2, :], IDX[:, ds(g * G + q, 1), :].rearrange("p a k -> p (a k)")
                                ).then_inc(s_idx, 1)

            def pooled(g, q, following):
                t = g * G + q
                gathered = dve.value_load(control[0:1, ds(t + 1 + NT, 1)], min_val=16 * BASE, max_val=16 * LIST * NT)
                dve.wait_ge(s_fp_used, 8 * (t + 1) + 4)
                dve.wait_ge(s_gath[q % 2], gathered)
                dve.tensor_reduce(tmp[:, q, :], gath[:, q % 2, :, :].rearrange("p k f -> p f k"), axis=AX,
                                  op=ALU.max).then_inc(s_max, 1)
                if following is not None:
                    stage(*following)

            def pool_floor(g):
                dve.wait_ge(s_max, (g + 1) * G)
                dve.tensor_tensor(agg[:, :, 0:F], tmp[:, :, :], grp(wide, g), ALU.max).then_inc(s_post, 1)
                dve.wait_ge(s_post, 2 * NG + g * 3 + 1)

            def pool_post(g):
                c = Count(2 * NG + g * 3 + 1)
                dve.tensor_tensor(agg[:, :, 0:F], agg[:, :, 0:F], per_row(grp(NOROW, g)), ALU.add).then_inc(s_post, 1)
                dve.wait_ge(s_post, c.up())
                dve.tensor_tensor(xg[:, :, :], grp(X, g), agg[:, :, 0:F], ALU.add).then_inc(s_x, 1)
                dve.tensor_tensor(grp(X, g), grp(X, g), agg[:, :, 0:F], ALU.add).then_inc(s_post, 1)
                dve.wait_ge(s_post, c.up())
                normalise(1, g)

            def remainder(g):
                dve.wait_ge(s_p0, g + 2 * NG + 1)
                dve.tensor_tensor(rem[:, :, :], gsc[:, :, :], part(2, g, 0), ALU.subtract).then_inc(s_rem, 1)

            def part2(g):
                dve.wait_ge(s_p1, g + 2 * NG + 1)
                dve.tensor_tensor(part(2, g, 2), rem[:, :, :], part(2, g, 1), ALU.subtract).then_inc(s_parts, 1)

            def turn(g, peeled, second=False, last=False):
                firsts_max(g, 0, 0, peeled)
                if not (peeled or second):
                    remainder(g - 2)
                if not peeled:
                    pooled(0 if second else g - 1, G - 1, (g, 1))
                firsts_max(g, 0, 1)
                if not peeled:
                    pool_floor(g - 1)
                firsts_max(g, 1, 0, peeled)
                if not (peeled or second):
                    part2(g - 2)
                pooled(g, 0, (g, 2))
                firsts_max(g, 1, 1)
                if not peeled:
                    pool_post(g - 1)
                firsts_max(g, 2, 0)
                pooled(g, 1, (g, 3))
                firsts_max(g, 2, 1)
                firsts_max(g, 3, 0)
                pooled(g, 2, None if last else (g + 1, 0))
                if not peeled:
                    operand(1, g - 1)
                firsts_max(g, 3, 1)
            turn(0, True)
            turn(1, False, second=True)
            with dve.Fori(2, NG - 1) as g:
                turn(g, False)
            turn(NG - 1, False, last=True)
            remainder(NG - 2)
            pooled(NG - 1, G - 1, None)
            pool_floor(NG - 1)
            part2(NG - 2)
            pool_post(NG - 1)
            operand(1, NG - 1)
            remainder(NG - 1)
            part2(NG - 1)

            def half_square(g):
                for q in range(G):
                    i = dve.scalar_tensor_tensor(relu_junk[:, q, :], hn[:, q, :], 0.0, hn[:, q, :], ALU.max, ALU.mult,
                                                 accum_out=ss[:, 0, q:q + 1])
                i.then_inc(s_ssh, 1)

            def artanh(c, x_, s_base):
                t_, t2 = V[0], V[1]
                dve.tensor_scalar(t_, x_, BALL_CLIP, None, ALU.min).then_inc(s_hyp, 1)
                dve.wait_ge(s_hyp, c.up())
                dve.tensor_scalar(V[7], t_, -1.0, 1.0, ALU.mult, ALU.add).then_inc(s_hyp, 1)
                dve.wait_ge(s_hyp, c.up())
                dve.reciprocal(V[8], V[7]).then_inc(s_hyp, 1)
                dve.wait_ge(s_hyp, c.up())
                dve.scalar_tensor_tensor(V[2], t_, 1.0, V[8], ALU.add, ALU.mult).then_inc(s_ratio, 1)
                dve.tensor_tensor(t2, t_, t_, ALU.mult).then_inc(s_hyp, 1)
                dve.wait_ge(s_hyp, c.up())
                dve.tensor_scalar(V[9], t2, 1.0 / 11, None, ALU.mult).then_inc(s_hyp, 1)
                dve.wait_ge(s_hyp, c.up())
                for k in (9, 7, 5, 3):
                    dve.scalar_tensor_tensor(V[9], V[9], 1.0 / k, t2, ALU.add, ALU.mult).then_inc(s_hyp, 1)
                    dve.wait_ge(s_hyp, c.up())
                dve.scalar_tensor_tensor(V[9], V[9], 1.0, t_, ALU.add, ALU.mult).then_inc(s_hyp, 1)
                dve.wait_ge(s_hyp, c.up())
                dve.tensor_scalar(V[10], t_, 0.25, None, ALU.is_lt).then_inc(s_hyp, 1)
                dve.wait_ge(s_hyp, c.up())
                dve.wait_ge(s_ln, s_base + 1)
                dve.tensor_scalar(V[11], V[3], 0.5, None, ALU.mult).then_inc(s_hyp, 1)
                dve.wait_ge(s_hyp, c.up())
                dve.tensor_tensor(V[12], V[9], V[11], ALU.subtract).then_inc(s_hyp, 1)
                dve.wait_ge(s_hyp, c.up())
                dve.tensor_tensor(V[12], V[12], V[10], ALU.mult).then_inc(s_hyp, 1)
                dve.wait_ge(s_hyp, c.up())
                dve.tensor_tensor(V[6], V[12], V[11], ALU.add).then_inc(s_hyp, 1)
                dve.wait_ge(s_hyp, c.up())

            ISTEPS = 26

            def operand_ball(g):
                c = Count(g * ISTEPS)
                gsc_free(3, g)
                dve.wait_ge(s_nn, g + 1)
                dve.tensor_scalar(nn[:, :, :], nn[:, :, :], MIN_NORM, None, ALU.max).then_inc(s_hyp, 1)
                dve.wait_ge(s_hyp, c.up())
                artanh(c, nn[:, 0, :], g)
                dve.reciprocal(V[13], nn[:, 0, :]).then_inc(s_hyp, 1)
                dve.wait_ge(s_hyp, c.up())
                dve.reciprocal(V[14], nn[:, 1, :]).then_inc(s_hyp, 1)
                dve.wait_ge(s_hyp, c.up())
                dve.tensor_tensor(V[13], V[13], nn[:, 1, :], ALU.mult).then_inc(s_hyp, 1)
                dve.wait_ge(s_hyp, c.up())
                dve.tensor_tensor(V[4], V[13], V[6], ALU.mult).then_inc(s_targ, 1)
                dve.wait_ge(s_tanh, g + 1)
                dve.tensor_tensor(V[7], V[5], V[5], ALU.mult).then_inc(s_hyp, 1)
                dve.wait_ge(s_hyp, c.up())
                dve.tensor_scalar(V[7], V[7], -1.0, 1.0, ALU.mult, ALU.add).then_inc(s_hyp, 1)
                dve.wait_ge(s_hyp, c.up())
                dve.tensor_scalar(V[7], V[7], BALL_EPS, 0.5, ALU.max, ALU.mult).then_inc(s_hyp, 1)
                dve.wait_ge(s_hyp, c.up())
                dve.reciprocal(V[8], V[7]).then_inc(s_hyp, 1)
                dve.wait_ge(s_hyp, c.up())
                dve.tensor_scalar(gsc[:, :, F], V[8], 1.0, None, ALU.subtract).then_inc(s_hyp, 1)
                dve.wait_ge(s_hyp, c.up())
                dve.tensor_tensor(V[9], V[8], V[5], ALU.mult).then_inc(s_hyp, 1)
                dve.wait_ge(s_hyp, c.up())
                dve.tensor_tensor(V[9], V[9], V[14], ALU.mult).then_inc(s_hyp, 1)
                dve.wait_ge(s_hyp, c.up())
                assert c.k == ISTEPS, c.k
                dve.tensor_tensor(gsc[:, :, 0:F], psW[:, :].rearrange("p (q f) -> p q f", q=G), per_row(V[9]),
                                  ALU.mult).then_inc(s_gsc, 1)
                dve.wait_ge(s_gsc, g + 3 * NG + 2)

            def turn(g, peeled):
                for q in range(G):
                    take_product(2, g * G + q, q)
                if not peeled:
                    operand_ball(g - 1)
                c = Count(5 * NG + g * 2)
                dve.wait_ge(s_sum, (g + 1) * G + 4)
                dve.wait_ge(s_side, g + 2)
                dve.tensor_tensor(tmp[:, :, :], agg[:, :, 0:F], grp(side, g), ALU.add).then_inc(s_post, 1)
                dve.wait_ge(s_post, c.up())
                dve.tensor_tensor(xg[:, :, :], grp(X, g), tmp[:, :, :], ALU.add).then_inc(s_x, 1)
                dve.tensor_tensor(grp(X, g), grp(X, g), tmp[:, :, :], ALU.add).then_inc(s_post, 1)
                dve.wait_ge(s_post, c.up())
                normalise(2, g)
                dve.wait_ge(s_norm, g + 2 * NG + 1)
                half_square(g)
            turns(dve, turn)
            operand_ball(NG - 1)

            OSTEPS = 37

            def ball_out(g):
                c = Count(NG * ISTEPS + g * OSTEPS)
                dve.tensor_scalar(V[15], agg[:, :, F], MIN_DENOMINATOR, None, ALU.max).then_inc(s_hyp, 1)
                dve.wait_ge(s_hyp, c.up())
                dve.reciprocal(V[15], V[15]).then_inc(s_hyp, 1)
                dve.wait_ge(s_hyp, c.up())
                dve.tensor_tensor(tmp[:, :, :], agg[:, :, 0:F], per_row(V[15]), ALU.mult).then_inc(s_hyp, 1)
                dve.wait_ge(s_hyp, c.up())
                for q in range(G):
                    dve.scalar_tensor_tensor(relu_junk[:, q, :], tmp[:, q, :], 1.0, tmp[:, q, :], ALU.mult, ALU.mult,
                                             accum_out=ss[:, 0, q:q + 1]).then_inc(s_hyp, 1)
                    dve.wait_ge(s_hyp, c.up())
                    dve.scalar_tensor_tensor(relu_junk[:, q, :], tmp[:, q, :], 0.0, tmp[:, q, :], ALU.max, ALU.mult,
                                             accum_out=ss[:, 1, q:q + 1]).then_inc(s_hyp, 1)
                    dve.wait_ge(s_hyp, c.up())
                dve.sem_inc(s_ssm, 1)
                dve.wait_ge(s_nn, NG + g + 1)
                dve.tensor_scalar(V[13], nn[:, 0, :], MIN_NORM, None, ALU.max).then_inc(s_hyp, 1)
                dve.wait_ge(s_hyp, c.up())
                artanh(c, V[13], NG + g)
                dve.reciprocal(V[13], V[13]).then_inc(s_hyp, 1)
                dve.wait_ge(s_hyp, c.up())
                dve.tensor_tensor(V[6], V[6], grp(DEG, g), ALU.mult).then_inc(s_hyp, 1)
                dve.wait_ge(s_hyp, c.up())
                dve.tensor_scalar(V[6], V[6], 0.5, ARTANH_CLIP, ALU.mult, ALU.min).then_inc(s_hyp, 1)
                dve.wait_ge(s_hyp, c.up())
                dve.tensor_tensor(V[14], V[6], V[13], ALU.mult).then_inc(s_hyp, 1)
                dve.wait_ge(s_hyp, c.up())
                dve.tensor_tensor(V[4], V[14], nn[:, 1, :], ALU.mult).then_inc(s_targ, 1)
                dve.wait_ge(s_targ, NG + g + 1)
                dve.tensor_scalar(V[7], V[4], MIN_NORM, None, ALU.max).then_inc(s_hyp, 1)
                dve.wait_ge(s_hyp, c.up())
                dve.reciprocal(V[8], V[7]).then_inc(s_hyp, 1)
                dve.wait_ge(s_hyp, c.up())
                dve.tensor_tensor(V[8], V[8], V[14], ALU.mult).then_inc(s_hyp, 1)
                dve.wait_ge(s_hyp, c.up())
                dve.wait_ge(s_tanh, NG + g + 1)
                dve.tensor_tensor(V[8], V[8], V[5], ALU.mult).then_inc(s_hyp, 1)
                dve.wait_ge(s_hyp, c.up())
                dve.tensor_scalar(tmp[:, :, :], tmp[:, :, :], 0.0, None, ALU.max).then_inc(s_hyp, 1)
                dve.wait_ge(s_hyp, c.up())
                dve.tensor_tensor(tmp[:, :, :], tmp[:, :, :], per_row(V[8]), ALU.mult).then_inc(s_hyp, 1)
                dve.wait_ge(s_hyp, c.up())
                assert c.k == OSTEPS, c.k

            def turn(g, peeled):
                for q in range(G):
                    take_product(3, (g + NG) * G + q, q)
                if not peeled:
                    operand(3, g - 1)
                dve.wait_ge(s_sum, (g + NG + 1) * G + 4)
                ball_out(g)
                c = Count(7 * NG + g)
                dve.tensor_tensor(xg[:, :, :], grp(X, g), tmp[:, :, :], ALU.add).then_inc(s_x, 1)
                dve.tensor_tensor(grp(X, g), grp(X, g), tmp[:, :, :], ALU.add).then_inc(s_post, 1)
                dve.wait_ge(s_post, c.up())
                normalise(3, g)
            turns(dve, turn)
            operand(3, NG - 1)

            def turn(g, peeled):
                for q in range(G):
                    take_product(4, (g + 2 * NG) * G + q, q)
                dve.wait_ge(s_sum, (g + 2 * NG + 1) * G + 4)
                if not peeled:
                    dve.wait_ge(s_zTp, g)
                    dve.wait_ge(s_sqTp, g)
                c = Count(8 * NG + g * 12)
                dve.tensor_tensor(tmp[:, :, :], agg[:, :, 0:F], per_row(grp(DINV, g)), ALU.mult).then_inc(s_post, 1)
                dve.wait_ge(s_post, c.up())
                dve.tensor_tensor(tmp[:, :, :], tmp[:, :, :], bias3("b31"), ALU.add).then_inc(s_post, 1)
                dve.wait_ge(s_post, c.up())
                dve.scalar_tensor_tensor(xg[:, :, :], tmp[:, :, :], SLOPE, tmp[:, :, :], ALU.mult, ALU.max).then_inc(s_z, 1)
                dve.wait_ge(s_z, g + 1)
                for q in range(G):
                    dve.scalar_tensor_tensor(relu_junk[:, q, :], xg[:, q, :], 1.0, xg[:, q, :], ALU.mult,
                                             ALU.mult, accum_out=sqg[:, q:q + 1]).then_inc(s_post, 1)
                    dve.wait_ge(s_post, c.up())
                dve.tensor_copy(grp(SQ, g), sqg[:, :]).then_inc(s_post, 1)
                dve.wait_ge(s_post, c.up())
                dve.tensor_scalar(sqh[:, :], sqg[:, :], -0.5, None, ALU.mult).then_inc(s_post, 1)
                dve.wait_ge(s_post, c.up())
                dve.tensor_copy(sqp[:, :, 0], sqh[:, :]).then_inc(s_post, 1)
                dve.wait_ge(s_post, c.up())
                dve.tensor_tensor(sqr[:, :], sqh[:, :], sqp[:, :, 0], ALU.subtract).then_inc(s_post, 1)
                dve.wait_ge(s_post, c.up())
                dve.tensor_copy(sqp[:, :, 1], sqr[:, :]).then_inc(s_post, 1)
                dve.wait_ge(s_post, c.up())
                dve.tensor_tensor(sqp[:, :, 2], sqr[:, :], sqp[:, :, 1], ALU.subtract).then_inc(s_post, 1)
                dve.wait_ge(s_post, c.up())
                assert c.k == 12
                dve.sem_inc(s_sqp, 1)
            turns(dve, turn)

            def distances(g):
                dve.wait_ge(s_keyused, (g + 1) * G + 2)
                dve.tensor_copy(grp(TI, g), top_i[:, :, 0:TOP]).then_inc(s_topi, 1)
                dve.wait_ge(s_topi, 2 * (g + 1))
                dve.tensor_scalar(d2c[:, :, :], d2[:, :, :], 0.0, None, ALU.max).then_inc(s_d2, 1)

            def take_similarities(g):
                dve.wait_ge(s_exp, g + 1)
                dve.tensor_copy(grp(S, g), simil[:, :, :]).then_inc(s_w, 1)
                dve.tensor_reduce(ssum[:, :], simil[:, :, :], axis=AX, op=ALU.add).then_inc(s_w, 1)

            def second_degree(g):
                dve.wait_ge(s_w, 2 * (g + 1))
                dve.tensor_tensor(sdeg[:, :], ssum[:, :], grp(DEG, g), ALU.add).then_inc(s_sdeg, 1)

            def second_inverse(g):
                dve.wait_ge(s_sstd2, g + 1)
                dve.reciprocal(sinv[:, :], sstd[:, :]).then_inc(s_sinv, 1)

            def scaled_rows(g, first_group=False):
                dve.wait_ge(s_sinv, 2 * g + 1)
                dve.tensor_copy(grp(D2INV, g), sinv[:, :]).then_inc(s_sinv, 1)
                gsc_free(5, g)
                if not first_group:
                    dve.wait_ge(s_g2, 16 * g)
                dve.tensor_tensor(gsc[:, :, 0:F], grp(side, g), per_row(sinv[:, :]), ALU.mult).then_inc(s_gsc, 1)

            def turn(g, first_group, second_group=False, last_group=False):
                before = 0 if second_group else g - 1
                for q in range(G):
                    t = g * G + q
                    dve.wait_ge(s_keyrow, 8 * (t + 1) + 8)
                    if q == 0 and not first_group:
                        dve.wait_ge(s_topi, 2 * before + 1)
                    dve.sem_inc(waited["dve"], 1)
                    dve.max(top_v[:, q, :], rows[:, q % 2, :]).then_inc(s_top, 1)
                    if not first_group:
                        if q == 0:
                            distances(before)
                        if q == 1:
                            take_similarities(before)
                        if q == 3:
                            if last_group:
                                scaled_rows(before)
                            else:
                                second_inverse(before)
                    dve.wait_ge(s_top, t + 1)
                    if q == 3:
                        dve.scalar_tensor_tensor(d2[:, :, :], top_v[:, :, 0:TOP], -2.0, per_row(grp(SQ, g), TOP),
                                                 ALU.mult, ALU.add).then_inc(s_topi, 1)
                    dve.sem_inc(waited["dve"], 1)
                    dve.max_index(top_i[:, q, :], top_v[:, q, :], rows[:, q % 2, :]).then_inc(s_keyused, 1)
                    if not first_group:
                        if q == 1:
                            second_degree(before)
                        if q == 2 and last_group:
                            second_inverse(before)
                        if q == 3 and not last_group:
                            scaled_rows(before, second_group)
            turn(0, True)
            turn(1, False, True)
            with dve.Fori(2, NG - 1) as g:
                turn(g, False)
            turn(NG - 1, False, last_group=True)
            distances(NG - 1)
            take_similarities(NG - 1)
            second_degree(NG - 1)
            second_inverse(NG - 1)
            scaled_rows(NG - 1)
            dve.wait_ge(s_sinv, 2 * NG)

            def last(g, r, peeled):
                c = Count(g * 16)
                dve.tensor_copy(sg[:, :, :], grp(S, g)).then_inc(s_last, 1)
                dve.wait_ge(s_last, c.up())
                for q in range(G):
                    t = g * G + q
                    take_product(5, (g + 3 * NG) * G + q, q)
                    dve.wait_ge(s_sum, (g + 3 * NG) * G + q + 5)
                    dve.wait_ge(s_gath2[q % 2], 16 * TOP * (g * 2 + q // 2 + 1))
                    for k in range(TOP - 1):
                        dve.scalar_tensor_tensor(agg[:, q, 0:F], gath[:, q % 2, k, :], sg[:, q, k:k + 1],
                                                 agg[:, q, 0:F], ALU.mult, ALU.add).then_inc(s_last, 1)
                        dve.wait_ge(s_last, c.up())
                    dve.scalar_tensor_tensor(agg[:, q, 0:F], gath[:, q % 2, TOP - 1, :], sg[:, q, TOP - 1:TOP],
                                             agg[:, q, 0:F], ALU.mult, ALU.add).then_inc(s_gath_used, 1)
                dve.wait_ge(s_gath_used, NT + (g + 1) * G + 2)
                dve.tensor_tensor(tmp[:, :, :], agg[:, :, 0:F], per_row(grp(D2INV, g)), ALU.mult).then_inc(s_last, 1)
                dve.wait_ge(s_last, c.up())
                dve.tensor_tensor(tmp[:, :, :], tmp[:, :, :], bias3("b32"), ALU.add).then_inc(s_last, 1)
                dve.wait_ge(s_last, c.up())
                if not peeled:
                    dve.wait_ge(s_out[r], 8 * (g - r))
                dve.tensor_tensor(fin[:, r, :, :], grp(X, g), tmp[:, :, :], ALU.add).then_inc(s_last, 1)
                dve.wait_ge(s_last, c.up())
                assert c.k == 16, c.k
                dve.sem_inc(s_fin, 1)
            last(0, 0, True)
            last(1, 1, True)
            with dve.Fori(1, NG // 2) as h:
                last(h * 2, 0, False)
                last(h * 2 + 1, 1, False)


_INS = ['x', 'adj', 'L0_gnn_weight', 'L0_gnn_bias', 'L1_gnn_weight', 'L2_gnn_W', 'L3_gnn_W1', 'L3_gnn_b1',
        'L3_gnn_W2', 'L3_gnn_b2']


def kernel(**inputs):
    import concourse.bacc as bacc
    from concourse.bass_utils import run_bass_kernel_spmd as run

    nc = bacc.Bacc("TRN2", target_bir_lowering=False, num_devices=1)
    arrays, args = {}, []
    for name in _INS:
        a = np.ascontiguousarray(inputs[name])
        arrays[f"in_{name}"] = a
        args.append(nc.dram_tensor(f"in_{name}", a.shape, mybir.dt.from_np(a.dtype), kind="ExternalInput").ap())
    out = nc.dram_tensor("out_x", inputs['x'].shape, F32, kind="ExternalOutput").ap()
    program(nc, *args, out)
    return run(nc, [arrays], core_ids=[0]).results[0]["out_x"]
```
